# Optimizing a Trainium2 kernel written in Bass

```python
import numpy as np
import jax
import jax.numpy as jnp

def _softmax(x, axis=-1):
    return jax.nn.softmax(x, axis=axis)

def _gelu(x):
    return jax.nn.gelu(x, approximate=True)

def _silu(x):
    return jax.nn.silu(x)

def _sigmoid(x):
    return jax.nn.sigmoid(x)

def _layernorm(x, axis=-1, eps=1e-05):
    m = jnp.mean(x, axis=axis, keepdims=True)
    v = jnp.var(x, axis=axis, keepdims=True)
    return (x - m) / jnp.sqrt(v + eps)

def _scatter_add(tgt, idx, src, axis=0):
    return tgt.at[idx].add(src)

def _segment_sum(src, seg, n):
    return jax.ops.segment_sum(src, seg, n)
kernel_name = 'mk_xattn_ffn_d4_seqx_r8_616d1c'

def setup_inputs(seed: int=0):
    np.random.seed(seed)
    _w = jnp.asarray

    def _rec_inputs():
        import jax
        import jax.numpy as jnp
        _rk = jax.random.key(seed)
        x = -0.0002928 + 1 * jax.random.normal(jax.random.fold_in(_rk, 1), (16, 56, 256), jnp.float32)
        _lenS = 56 - jax.random.randint(jax.random.fold_in(_rk, 7), (16,), 0, max(1, 56 // 4) + 1, jnp.int32)
        _lenS2 = 1500 - jax.random.randint(jax.random.fold_in(_rk, 8), (16,), 0, max(1, 1500 // 4) + 1, jnp.int32)
        _ctx_512P = jax.random.normal(jax.random.fold_in(_rk, 11), (16, 16, 64), jnp.float32)
        _ctx_512c = jax.random.dirichlet(jax.random.fold_in(_rk, 511), 0.3 * jnp.ones((16,), jnp.float32), (16, 1500))
        _ctx_512t = jnp.einsum('bsk,bkd->bsd', _ctx_512c, _ctx_512P)
        _ctx_512t = _ctx_512t * jax.lax.rsqrt(jnp.mean(jnp.square(_ctx_512t)) + 1e-12) * 0.953939
        ctx_512 = 0.000227908 + 0.99994 * (_ctx_512t + 0.3 * jax.random.normal(jax.random.fold_in(_rk, 611), (16, 1500, 64), jnp.float32))
        return (x, ctx_512)
    x, ctx_512 = _rec_inputs()

    def _L0_xattn_setup():
        import jax, jax.numpy as jnp
        import numpy as np
        B, S, L = (2, 128, 128)
        DIM_Q, H, K, D_C, D_CQ, R = (256, 16, 128, 64, 192, 64)

        def _rope_tables(seq_len, dim, dtype):
            inv_freq = 1.0 / 10000.0 ** (jnp.arange(0, dim, 2, dtype=dtype) / dim)
            t = jnp.arange(seq_len, dtype=dtype)
            freqs = t[:, None] * inv_freq[None, :]
            sin = jnp.repeat(jnp.sin(freqs), 2, axis=-1)
            cos = jnp.repeat(jnp.cos(freqs), 2, axis=-1)
            return (sin, cos)

        def _rotate_half(x):
            h = x.shape[-1] // 2
            return jnp.concatenate([-x[..., h:], x[..., :h]], axis=-1)
        key = jax.random.key(seed)
        ks = jax.random.split(key, 8)
        s_in = 1.0 / np.sqrt(DIM_Q)
        s_k = 1.0 / np.sqrt(K)
        s_cq = 1.0 / np.sqrt(D_CQ)
        s_c = 1.0 / np.sqrt(D_C)
        return {'hidden_q': jax.random.normal(ks[0], (B, S, DIM_Q), jnp.float32), 'kv_c': jax.random.normal(ks[1], (B, L, D_C), jnp.float32), 'Wq': jax.random.normal(ks[2], (H * K, DIM_Q), jnp.float32) * s_in, 'w_kc_q': jax.random.normal(ks[3], (H, K, D_CQ), jnp.float32) * s_k, 'w_kc_kv': jax.random.normal(ks[4], (H, K, D_C), jnp.float32) * s_k, 'W_qr': jax.random.normal(ks[5], (H, D_CQ, R), jnp.float32) * s_cq / np.sqrt(R), 'W_kr': jax.random.normal(ks[6], (H, D_C, R), jnp.float32) * s_c, 'Wo': jax.random.normal(ks[7], (DIM_Q, H * K), jnp.float32) * s_k}
    _L0_xattn_all = _L0_xattn_setup()
    _L0_xattn_in = {k: v for k, v in _L0_xattn_all.items() if k in ('Wq', 'w_kc_q', 'w_kc_kv', 'W_qr', 'W_kr', 'Wo')}
    del _L0_xattn_all

    def _L0_ffn_setup():
        import jax, jax.numpy as jnp
        import numpy as np
        B, T, D = (2, 128, 256)
        E, F, K = (64, 64, 4)
        S, HS = (2, 64 * 4)
        key = jax.random.key(seed)
        ks = jax.random.split(key, 9)
        s = 0.02
        f32 = jnp.float32
        return {'x': jax.random.normal(ks[0], (B, T, D), f32), 'router_w': jax.random.normal(ks[1], (D, E), f32) * s, 'router_bias': jnp.zeros((E,), f32), 'wg': jax.random.normal(ks[2], (E, D, F), f32) * s, 'wu': jax.random.normal(ks[3], (E, D, F), f32) * s, 'wd': jax.random.normal(ks[4], (E, F, D), f32) * s, 'swg': jax.random.normal(ks[5], (S, D, HS), f32) * s, 'swu': jax.random.normal(ks[6], (S, D, HS), f32) * s, 'swd': jax.random.normal(ks[7], (S, HS, D), f32) * s}
    _L0_ffn_all = _L0_ffn_setup()
    _L0_ffn_in = {k: v for k, v in _L0_ffn_all.items() if k in ('router_w', 'router_bias', 'wg', 'wu', 'wd', 'swg', 'swu', 'swd')}
    del _L0_ffn_all

    def _L1_xattn_setup():
        import jax, jax.numpy as jnp
        import numpy as np
        B, S, L = (2, 128, 128)
        DIM_Q, H, K, D_C, D_CQ, R = (256, 16, 128, 64, 192, 64)

        def _rope_tables(length, dim):
            inv = 1.0 / 10000.0 ** (jnp.arange(0, dim, 2, dtype=jnp.float32) / dim)
            f = jnp.arange(length, dtype=jnp.float32)[:, None] * inv[None, :]
            sin = jnp.repeat(jnp.sin(f), 2, axis=-1)
            cos = jnp.repeat(jnp.cos(f), 2, axis=-1)
            return (sin, cos)

        def _rotate_half(x):
            half = x.shape[-1] // 2
            return jnp.concatenate([-x[..., half:], x[..., :half]], axis=-1)

        def _apply_rope(x, sin, cos):
            return x * cos + _rotate_half(x) * sin
        key = jax.random.key(seed)
        ks = jax.random.split(key, 8)
        return {'hidden_q': jax.random.normal(ks[0], (B, S, DIM_Q), jnp.float32), 'kv_c': jax.random.normal(ks[1], (B, L, D_C), jnp.float32), 'Wq': jax.random.normal(ks[2], (H * K, DIM_Q), jnp.float32) / np.sqrt(DIM_Q).astype(np.float32), 'w_kc_q': jax.random.normal(ks[3], (H, K, D_CQ), jnp.float32) / np.sqrt(K).astype(np.float32), 'w_kc_kv': jax.random.normal(ks[4], (H, K, D_C), jnp.float32) / np.sqrt(K).astype(np.float32), 'W_qr': jax.random.normal(ks[5], (H, D_CQ, R), jnp.float32) / np.float32(np.sqrt(D_CQ) * np.sqrt(R)), 'W_kr': jax.random.normal(ks[6], (H, D_C, R), jnp.float32) / np.sqrt(D_C).astype(np.float32), 'Wo': jax.random.normal(ks[7], (DIM_Q, H * K), jnp.float32) / np.sqrt(H * K).astype(np.float32)}
    _L1_xattn_all = _L1_xattn_setup()
    _L1_xattn_in = {k: v for k, v in _L1_xattn_all.items() if k in ('Wq', 'w_kc_q', 'w_kc_kv', 'W_qr', 'W_kr', 'Wo')}
    del _L1_xattn_all

    def _L1_ffn_setup():
        import jax, jax.numpy as jnp
        import numpy as np
        B, S, D_IN, D_OUT = (4, 256, 256, 256)
        EPS = 1e-10
        key = jax.random.key(seed)
        kx, kw, kb = jax.random.split(key, 3)
        x = jax.random.normal(kx, (B, S, D_IN), dtype=jnp.float32)
        weight = jax.random.normal(kw, (D_OUT, D_IN), dtype=jnp.float32) * 0.02
        bias = jax.random.normal(kb, (D_OUT,), dtype=jnp.float32) * 0.02
        return {'x': x, 'weight': weight, 'bias': bias}
    _L1_ffn_all = _L1_ffn_setup()
    _L1_ffn_in = {k: v for k, v in _L1_ffn_all.items() if k in ('weight', 'bias')}
    del _L1_ffn_all

    def _L2_xattn_setup():
        import jax, jax.numpy as jnp
        import numpy as np
        B, S, H, NH, L = (2, 256, 256, 16, 64)
        HD = H // NH
        key = jax.random.key(seed)
        k1, k2, k3, k4, k5 = jax.random.split(key, 5)
        scale = 0.02
        return {'q': jax.random.normal(k1, (B, S, H), dtype=jnp.float32), 'latent_kv': jax.random.normal(k2, (B, S, L), dtype=jnp.float32), 'Wq': jax.random.normal(k3, (H, H), dtype=jnp.float32) * scale, 'Wkv_expand': jax.random.normal(k4, (2 * H, L), dtype=jnp.float32) * scale, 'Wout': jax.random.normal(k5, (H, H), dtype=jnp.float32) * scale}
    _L2_xattn_all = _L2_xattn_setup()
    _L2_xattn_in = {k: v for k, v in _L2_xattn_all.items() if k in ('Wq', 'Wkv_expand', 'Wout')}
    del _L2_xattn_all

    def _L2_ffn_setup():
        import jax, jax.numpy as jnp
        import numpy as np
        N_BLOCKS = 16
        BLOCK_SIZE = 64
        TOP_K = N_BLOCKS // 4
        key = jax.random.key(seed)
        k1, k2, k3, k4, k5 = jax.random.split(key, 5)
        in_f, out_f = (256, 1024)
        x = jax.random.normal(k1, (2, 512, in_f), dtype=jnp.float32)
        Wr = jax.random.normal(k2, (N_BLOCKS, in_f), dtype=jnp.float32) * in_f ** (-0.5)
        br = jnp.zeros((N_BLOCKS,), dtype=jnp.float32)
        W1 = jax.random.normal(k3, (out_f, in_f), dtype=jnp.float32) * in_f ** (-0.5)
        W2 = jax.random.normal(k4, (in_f, out_f), dtype=jnp.float32) * out_f ** (-0.5)
        return {'x': x, 'Wr': Wr, 'br': br, 'W1': W1, 'W2': W2}
    _L2_ffn_all = _L2_ffn_setup()
    _L2_ffn_in = {k: v for k, v in _L2_ffn_all.items() if k in ('Wr', 'br', 'W1', 'W2')}
    del _L2_ffn_all

    def _L3_xattn_setup():
        import jax, jax.numpy as jnp
        import numpy as np
        B, S, L = (2, 128, 128)
        DIM_Q, H, K, D_C, D_CQ, R = (256, 16, 128, 64, 192, 64)

        def _rope_tables(length, dim):
            inv = 1.0 / 10000.0 ** (jnp.arange(0, dim, 2, dtype=jnp.float32) / dim)
            f = jnp.arange(length, dtype=jnp.float32)[:, None] * inv[None, :]
            sin = jnp.repeat(jnp.sin(f), 2, axis=-1)
            cos = jnp.repeat(jnp.cos(f), 2, axis=-1)
            return (sin, cos)

        def _rotate_half(x):
            half = x.shape[-1] // 2
            return jnp.concatenate([-x[..., half:], x[..., :half]], axis=-1)

        def _apply_rope(x, sin, cos):
            return x * cos + _rotate_half(x) * sin
        key = jax.random.key(seed)
        ks = jax.random.split(key, 8)
        return {'hidden_q': jax.random.normal(ks[0], (B, S, DIM_Q), jnp.float32), 'kv_c': jax.random.normal(ks[1], (B, L, D_C), jnp.float32), 'Wq': jax.random.normal(ks[2], (H * K, DIM_Q), jnp.float32) / np.sqrt(DIM_Q).astype(np.float32), 'w_kc_q': jax.random.normal(ks[3], (H, K, D_CQ), jnp.float32) / np.sqrt(K).astype(np.float32), 'w_kc_kv': jax.random.normal(ks[4], (H, K, D_C), jnp.float32) / np.sqrt(K).astype(np.float32), 'W_qr': jax.random.normal(ks[5], (H, D_CQ, R), jnp.float32) / np.float32(np.sqrt(D_CQ) * np.sqrt(R)), 'W_kr': jax.random.normal(ks[6], (H, D_C, R), jnp.float32) / np.sqrt(D_C).astype(np.float32), 'Wo': jax.random.normal(ks[7], (DIM_Q, H * K), jnp.float32) / np.sqrt(H * K).astype(np.float32)}
    _L3_xattn_all = _L3_xattn_setup()
    _L3_xattn_in = {k: v for k, v in _L3_xattn_all.items() if k in ('Wq', 'w_kc_q', 'w_kc_kv', 'W_qr', 'W_kr', 'Wo')}
    del _L3_xattn_all

    def _L3_ffn_setup():
        import jax, jax.numpy as jnp
        import numpy as np
        B, S, D = (2, 512, 256)
        E, DFF = (8, 1024)
        TOP_K = 2
        key = jax.random.key(seed)
        ks = jax.random.split(key, 4)
        scale_in = 1.0 / np.sqrt(D)
        scale_ff = 1.0 / np.sqrt(DFF)
        return {'hidden_states': jax.random.normal(ks[0], (B, S, D), dtype=jnp.float32), 'gate_w': jax.random.normal(ks[1], (E, D), dtype=jnp.float32) * scale_in, 'w1': jax.random.normal(ks[2], (E, D, DFF), dtype=jnp.float32) * scale_in, 'b1': jnp.zeros((E, DFF), dtype=jnp.float32), 'w2': jax.random.normal(ks[3], (E, DFF, D), dtype=jnp.float32) * scale_ff, 'b2': jnp.zeros((E, D), dtype=jnp.float32)}
    _L3_ffn_all = _L3_ffn_setup()
    _L3_ffn_in = {k: v for k, v in _L3_ffn_all.items() if k in ('gate_w', 'w1', 'b1', 'w2', 'b2')}
    del _L3_ffn_all
    return {'x': x, 'ctx_512': ctx_512, 'L0_xattn_Wq': _L0_xattn_in['Wq'], 'L0_xattn_w_kc_q': _L0_xattn_in['w_kc_q'], 'L0_xattn_w_kc_kv': _L0_xattn_in['w_kc_kv'], 'L0_xattn_W_qr': _L0_xattn_in['W_qr'], 'L0_xattn_W_kr': _L0_xattn_in['W_kr'], 'L0_xattn_Wo': _L0_xattn_in['Wo'], 'L0_ffn_router_w': _L0_ffn_in['router_w'], 'L0_ffn_router_bias': _L0_ffn_in['router_bias'], 'L0_ffn_wg': _L0_ffn_in['wg'], 'L0_ffn_wu': _L0_ffn_in['wu'], 'L0_ffn_wd': _L0_ffn_in['wd'], 'L0_ffn_swg': _L0_ffn_in['swg'], 'L0_ffn_swu': _L0_ffn_in['swu'], 'L0_ffn_swd': _L0_ffn_in['swd'], 'L1_xattn_Wq': _L1_xattn_in['Wq'], 'L1_xattn_w_kc_q': _L1_xattn_in['w_kc_q'], 'L1_xattn_w_kc_kv': _L1_xattn_in['w_kc_kv'], 'L1_xattn_W_qr': _L1_xattn_in['W_qr'], 'L1_xattn_W_kr': _L1_xattn_in['W_kr'], 'L1_xattn_Wo': _L1_xattn_in['Wo'], 'L1_ffn_weight': _L1_ffn_in['weight'], 'L1_ffn_bias': _L1_ffn_in['bias'], 'L2_xattn_Wq': _L2_xattn_in['Wq'], 'L2_xattn_Wkv_expand': _L2_xattn_in['Wkv_expand'], 'L2_xattn_Wout': _L2_xattn_in['Wout'], 'L2_ffn_Wr': _L2_ffn_in['Wr'], 'L2_ffn_br': _L2_ffn_in['br'], 'L2_ffn_W1': _L2_ffn_in['W1'], 'L2_ffn_W2': _L2_ffn_in['W2'], 'L3_xattn_Wq': _L3_xattn_in['Wq'], 'L3_xattn_w_kc_q': _L3_xattn_in['w_kc_q'], 'L3_xattn_w_kc_kv': _L3_xattn_in['w_kc_kv'], 'L3_xattn_W_qr': _L3_xattn_in['W_qr'], 'L3_xattn_W_kr': _L3_xattn_in['W_kr'], 'L3_xattn_Wo': _L3_xattn_in['Wo'], 'L3_ffn_gate_w': _L3_ffn_in['gate_w'], 'L3_ffn_w1': _L3_ffn_in['w1'], 'L3_ffn_b1': _L3_ffn_in['b1'], 'L3_ffn_w2': _L3_ffn_in['w2'], 'L3_ffn_b2': _L3_ffn_in['b2']}

def reference(x, ctx_512, L0_xattn_Wq, L0_xattn_w_kc_q, L0_xattn_w_kc_kv, L0_xattn_W_qr, L0_xattn_W_kr, L0_xattn_Wo, L0_ffn_router_w, L0_ffn_router_bias, L0_ffn_wg, L0_ffn_wu, L0_ffn_wd, L0_ffn_swg, L0_ffn_swu, L0_ffn_swd, L1_xattn_Wq, L1_xattn_w_kc_q, L1_xattn_w_kc_kv, L1_xattn_W_qr, L1_xattn_W_kr, L1_xattn_Wo, L1_ffn_weight, L1_ffn_bias, L2_xattn_Wq, L2_xattn_Wkv_expand, L2_xattn_Wout, L2_ffn_Wr, L2_ffn_br, L2_ffn_W1, L2_ffn_W2, L3_xattn_Wq, L3_xattn_w_kc_q, L3_xattn_w_kc_kv, L3_xattn_W_qr, L3_xattn_W_kr, L3_xattn_Wo, L3_ffn_gate_w, L3_ffn_w1, L3_ffn_b1, L3_ffn_w2, L3_ffn_b2):
    import jax
    import jax.numpy as jnp

    def _L0_xattn_ref(hidden_q, kv_c, Wq, w_kc_q, w_kc_kv, W_qr, W_kr, Wo):
        import jax, jax.numpy as jnp
        import numpy as np
        B, S, L = (2, 128, 128)
        DIM_Q, H, K, D_C, D_CQ, R = (256, 16, 128, 64, 192, 64)

        def _rope_tables(seq_len, dim, dtype):
            inv_freq = 1.0 / 10000.0 ** (jnp.arange(0, dim, 2, dtype=dtype) / dim)
            t = jnp.arange(seq_len, dtype=dtype)
            freqs = t[:, None] * inv_freq[None, :]
            sin = jnp.repeat(jnp.sin(freqs), 2, axis=-1)
            cos = jnp.repeat(jnp.cos(freqs), 2, axis=-1)
            return (sin, cos)

        def _rotate_half(x):
            h = x.shape[-1] // 2
            return jnp.concatenate([-x[..., h:], x[..., :h]], axis=-1)
        b, s, _ = hidden_q.shape
        l = kv_c.shape[1]
        q_hk = (hidden_q @ Wq.T).reshape(b, s, H, K)
        q_big = jnp.einsum('bshk,hkq->bshq', q_hk, w_kc_q)
        sin, cos = _rope_tables(l, D_C, kv_c.dtype)
        kv_rope = kv_c * cos[None] + _rotate_half(kv_c) * sin[None]
        q_r = jnp.einsum('bshq,hqr->bhsr', q_big, W_qr)
        k_r = jnp.einsum('bld,hdr->bhlr', kv_rope, W_kr)
        scores = jnp.einsum('bhsr,bhlr->bhsl', q_r, k_r)
        attn = jax.nn.softmax(scores, axis=-1)
        ctx_c = jnp.einsum('bhsl,bld->bhsd', attn, kv_rope)
        ctx_lat = jnp.einsum('bhsd,hkd->bshk', ctx_c, w_kc_kv)
        out = ctx_lat.reshape(b, s, H * K) @ Wo.T
        return out

    def _L0_ffn_ref(x, router_w, router_bias, wg, wu, wd, swg, swu, swd):
        import jax, jax.numpy as jnp
        import numpy as np
        B, T, D = (2, 128, 256)
        E, F, K = (64, 64, 4)
        S, HS = (2, 64 * 4)
        b, t, d = x.shape
        flat = x.reshape(b * t, d)
        n = flat.shape[0]
        logits = flat @ router_w
        scores = jax.nn.softmax(logits, axis=-1)
        _, topk_idx = jax.lax.top_k(logits + router_bias, K)
        topk_scores = jnp.take_along_axis(scores, topk_idx, axis=-1)
        topk_scores = topk_scores / topk_scores.sum(axis=-1, keepdims=True)
        comb = jnp.zeros((n, E), dtype=flat.dtype).at[jnp.arange(n)[:, None], topk_idx].set(topk_scores)
        g = jax.nn.silu(jnp.einsum('nd,edf->nef', flat, wg))
        u = jnp.einsum('nd,edf->nef', flat, wu)
        routed = jnp.einsum('ne,nef,efd->nd', comb, g * u, wd)
        sg = jax.nn.silu(jnp.einsum('nd,sdh->nsh', flat, swg))
        su = jnp.einsum('nd,sdh->nsh', flat, swu)
        shared = jnp.einsum('nsh,shd->nd', sg * su, swd)
        return (routed + shared).reshape(b, t, d)

    def _L1_xattn_ref(hidden_q, kv_c, Wq, w_kc_q, w_kc_kv, W_qr, W_kr, Wo):
        import jax, jax.numpy as jnp
        import numpy as np
        B, S, L = (2, 128, 128)
        DIM_Q, H, K, D_C, D_CQ, R = (256, 16, 128, 64, 192, 64)

        def _rope_tables(length, dim):
            inv = 1.0 / 10000.0 ** (jnp.arange(0, dim, 2, dtype=jnp.float32) / dim)
            f = jnp.arange(length, dtype=jnp.float32)[:, None] * inv[None, :]
            sin = jnp.repeat(jnp.sin(f), 2, axis=-1)
            cos = jnp.repeat(jnp.cos(f), 2, axis=-1)
            return (sin, cos)

        def _rotate_half(x):
            half = x.shape[-1] // 2
            return jnp.concatenate([-x[..., half:], x[..., :half]], axis=-1)

        def _apply_rope(x, sin, cos):
            return x * cos + _rotate_half(x) * sin
        Bv, Sv, _ = hidden_q.shape
        _, Lv, _ = kv_c.shape
        q_hk = (hidden_q @ Wq.T).reshape(Bv, Sv, H, K)
        q_big = jnp.einsum('bshk,hkq->bshq', q_hk, w_kc_q)
        sin_q, cos_q = _rope_tables(Sv, D_CQ)
        q_big = _apply_rope(q_big, sin_q[None, :, None, :], cos_q[None, :, None, :])
        sin_k, cos_k = _rope_tables(Lv, D_C)
        kv_r = _apply_rope(kv_c, sin_k[None], cos_k[None])
        q_r = jnp.einsum('bshq,hqr->bhsr', q_big, W_qr)
        k_r = jnp.einsum('bld,hdr->bhlr', kv_r, W_kr)
        scores = jnp.einsum('bhsr,bhlr->bhsl', q_r, k_r)
        attn = jax.nn.softmax(scores, axis=-1)
        ctx_c = jnp.einsum('bhsl,bld->bhsd', attn, kv_r)
        ctx_lat = jnp.einsum('bhsd,hkd->bhsk', ctx_c, w_kc_kv)
        ctx = ctx_lat.transpose(0, 2, 1, 3).reshape(Bv, Sv, H * K)
        return ctx @ Wo.T

    def _L1_ffn_ref(x, weight, bias):
        import jax, jax.numpy as jnp
        import numpy as np
        B, S, D_IN, D_OUT = (4, 256, 256, 256)
        EPS = 1e-10
        scale = jnp.mean(jnp.abs(weight))
        w_t = jnp.clip(jnp.round(weight / (scale + EPS)), -1.0, 1.0)
        w_ste = weight + jax.lax.stop_gradient(w_t * scale - weight)
        return jnp.einsum('bsi,oi->bso', x, w_ste) + bias

    def _L2_xattn_ref(q, latent_kv, Wq, Wkv_expand, Wout):
        import jax, jax.numpy as jnp
        import numpy as np
        B, S, H, NH, L = (2, 256, 256, 16, 64)
        HD = H // NH
        b, sq, _ = q.shape
        sk = latent_kv.shape[1]
        qp = q @ Wq.T
        kv = latent_kv @ Wkv_expand.T
        k, v = jnp.split(kv, 2, axis=-1)
        qh = qp.reshape(b, sq, NH, HD).transpose(0, 2, 1, 3)
        kh = k.reshape(b, sk, NH, HD).transpose(0, 2, 1, 3)
        vh = v.reshape(b, sk, NH, HD).transpose(0, 2, 1, 3)
        inv_sqrt_d = 1.0 / jnp.sqrt(jnp.float32(HD))
        scores = jnp.einsum('bhqd,bhkd->bhqk', qh, kh) * inv_sqrt_d
        causal = jnp.tril(jnp.ones((sq, sk), dtype=bool))
        scores = jnp.where(causal, scores, jnp.finfo(scores.dtype).min)
        attn = jax.nn.softmax(scores, axis=-1)
        out = jnp.einsum('bhqk,bhkd->bhqd', attn, vh)
        out = out.transpose(0, 2, 1, 3).reshape(b, sq, H)
        return out @ Wout.T

    def _L2_ffn_ref(x, Wr, br, W1, W2):
        import jax, jax.numpy as jnp
        import numpy as np
        N_BLOCKS = 16
        BLOCK_SIZE = 64
        TOP_K = N_BLOCKS // 4
        x_shape = x.shape
        in_f = x_shape[-1]
        xf = x.reshape(-1, in_f)
        n = xf.shape[0]
        prob = jax.nn.softmax(xf @ Wr.T + br, axis=-1)
        _, idx = jax.lax.top_k(prob, TOP_K)
        mask = jnp.zeros((n, N_BLOCKS), dtype=xf.dtype)
        mask = mask.at[jnp.arange(n)[:, None], idx].set(1.0)
        W1b = W1.reshape(N_BLOCKS, BLOCK_SIZE, in_f)
        h = jnp.einsum('nf,ibf->nib', xf, W1b)
        h = jax.nn.gelu(h, approximate=False) * mask[:, :, None]
        W2b = W2.reshape(in_f, N_BLOCKS, BLOCK_SIZE)
        y = jnp.einsum('nib,fib->nf', h, W2b)
        return y.reshape(x_shape)

    def _L3_xattn_ref(hidden_q, kv_c, Wq, w_kc_q, w_kc_kv, W_qr, W_kr, Wo):
        import jax, jax.numpy as jnp
        import numpy as np
        B, S, L = (2, 128, 128)
        DIM_Q, H, K, D_C, D_CQ, R = (256, 16, 128, 64, 192, 64)

        def _rope_tables(length, dim):
            inv = 1.0 / 10000.0 ** (jnp.arange(0, dim, 2, dtype=jnp.float32) / dim)
            f = jnp.arange(length, dtype=jnp.float32)[:, None] * inv[None, :]
            sin = jnp.repeat(jnp.sin(f), 2, axis=-1)
            cos = jnp.repeat(jnp.cos(f), 2, axis=-1)
            return (sin, cos)

        def _rotate_half(x):
            half = x.shape[-1] // 2
            return jnp.concatenate([-x[..., half:], x[..., :half]], axis=-1)

        def _apply_rope(x, sin, cos):
            return x * cos + _rotate_half(x) * sin
        Bv, Sv, _ = hidden_q.shape
        _, Lv, _ = kv_c.shape
        q_hk = (hidden_q @ Wq.T).reshape(Bv, Sv, H, K)
        q_big = jnp.einsum('bshk,hkq->bshq', q_hk, w_kc_q)
        sin_q, cos_q = _rope_tables(Sv, D_CQ)
        q_big = _apply_rope(q_big, sin_q[None, :, None, :], cos_q[None, :, None, :])
        sin_k, cos_k = _rope_tables(Lv, D_C)
        kv_r = _apply_rope(kv_c, sin_k[None], cos_k[None])
        q_r = jnp.einsum('bshq,hqr->bhsr', q_big, W_qr)
        k_r = jnp.einsum('bld,hdr->bhlr', kv_r, W_kr)
        scores = jnp.einsum('bhsr,bhlr->bhsl', q_r, k_r)
        attn = jax.nn.softmax(scores, axis=-1)
        ctx_c = jnp.einsum('bhsl,bld->bhsd', attn, kv_r)
        ctx_lat = jnp.einsum('bhsd,hkd->bhsk', ctx_c, w_kc_kv)
        ctx = ctx_lat.transpose(0, 2, 1, 3).reshape(Bv, Sv, H * K)
        return ctx @ Wo.T

    def _L3_ffn_ref(hidden_states, gate_w, w1, b1, w2, b2):
        import jax, jax.numpy as jnp
        import numpy as np
        B, S, D = (2, 512, 256)
        E, DFF = (8, 1024)
        TOP_K = 2
        b, s, d = hidden_states.shape
        x = hidden_states.reshape(-1, d)
        router_logits = x @ gate_w.T
        _, sel = jax.lax.top_k(router_logits.sum(axis=0), TOP_K)
        rw = jax.nn.softmax(router_logits[:, sel].astype(jnp.float32), axis=1)
        rw = rw.astype(x.dtype)
        w1s, b1s = (w1[sel], b1[sel])
        w2s, b2s = (w2[sel], b2[sel])
        h = jax.nn.gelu(jnp.einsum('nd,kdf->knf', x, w1s) + b1s[:, None, :])
        y = jnp.einsum('knf,kfd->knd', h, w2s) + b2s[:, None, :]
        out = jnp.einsum('nk,knd->nd', rw, y)
        return out.reshape(b, s, -1)
    x = x + _L0_xattn_ref(_layernorm(x, axis=-1), ctx_512, L0_xattn_Wq, L0_xattn_w_kc_q, L0_xattn_w_kc_kv, L0_xattn_W_qr, L0_xattn_W_kr, L0_xattn_Wo)
    x = x + _L0_ffn_ref(_layernorm(x, axis=-1), L0_ffn_router_w, L0_ffn_router_bias, L0_ffn_wg, L0_ffn_wu, L0_ffn_wd, L0_ffn_swg, L0_ffn_swu, L0_ffn_swd)
    x = x + _L1_xattn_ref(_layernorm(x, axis=-1), ctx_512, L1_xattn_Wq, L1_xattn_w_kc_q, L1_xattn_w_kc_kv, L1_xattn_W_qr, L1_xattn_W_kr, L1_xattn_Wo)
    x = x + _L1_ffn_ref(_layernorm(x, axis=-1), L1_ffn_weight, L1_ffn_bias)
    x = x + _L2_xattn_ref(_layernorm(x, axis=-1), ctx_512, L2_xattn_Wq, L2_xattn_Wkv_expand, L2_xattn_Wout)
    x = x + _L2_ffn_ref(_layernorm(x, axis=-1), L2_ffn_Wr, L2_ffn_br, L2_ffn_W1, L2_ffn_W2)
    x = x + _L3_xattn_ref(_layernorm(x, axis=-1), ctx_512, L3_xattn_Wq, L3_xattn_w_kc_q, L3_xattn_w_kc_kv, L3_xattn_W_qr, L3_xattn_W_kr, L3_xattn_Wo)
    x = x + _L3_ffn_ref(_layernorm(x, axis=-1), L3_ffn_gate_w, L3_ffn_w1, L3_ffn_b1, L3_ffn_w2, L3_ffn_b2)
    return x

_drawn_inputs = setup_inputs


def setup_inputs(seed=0):
    import zlib

    import numpy as np

    out = dict(_drawn_inputs(seed))
    spreads = {'L0_ffn_router_bias': (0.0, 0.56),
     'L2_ffn_br': (0.0, 0.1),
     'L3_ffn_b1': (0.0, 0.271),
     'L3_ffn_b2': (0.0, 0.1)}
    factors = {'L0_ffn_router_w': 4.27,
     'L0_ffn_wg': 4.373,
     'L0_ffn_wu': 4.646,
     'L0_ffn_wd': 5.547,
     'L2_xattn_Wq': 42.14}
    for name, (base, spread) in spreads.items():
        noise = np.random.default_rng([zlib.crc32(name.encode()), seed]).standard_normal(out[name].shape)
        drawn = base * np.exp(spread * noise) if base else spread * noise
        out[name] = jnp.asarray(drawn.astype(out[name].dtype))
    for name, factor in factors.items():
        out[name] = (out[name] * factor).astype(out[name].dtype)
    return out
```

```python
from contextlib import ExitStack

import concourse.bass as bass
import numpy as np
from concourse import mybir

F32 = mybir.dt.float32
F32R = mybir.dt.float32r
U32 = mybir.dt.uint32
ALU = mybir.AluOpType
ACT = mybir.ActivationFunctionType
AX = mybir.AxisListType

P = 128
B, S, D = 16, 56, 256
NT = B * S
TT = NT // P
KT = D // P
CH = NT // 2
BC = B // 2
L, DC = 1500, 64
H, HK, CQ, R = 16, 128, 192, 64
HP = H // 2
AQ = CQ // 2
NQ = H * S
KP = 125
NK = L // KP
MC = L // 3
EPS = 1e-5
E0, F0, TOP0, SH0 = 64, 64, 4, 512
E2, F2, TOP2 = 16, 64, 4
E3, F3, TOP3 = 8, 1024, 2
NEG = -1.0e30


class Net:
    pass


def phase_tools(net, ctx, tag):
    nc = net.nc

    def sb(name, shape, dt=F32):
        return ctx.enter_context(nc.sbuf_tensor(f"{tag}_{name}", shape, dt))

    def ps(name, shape, dt=F32):
        return ctx.enter_context(nc.psum_tensor(f"{tag}_{name}", shape, dt))

    def sem(name):
        return nc.alloc_semaphore(f"{tag}_{name}")

    return sb, ps, sem


def load_constants(net):
    nc = net.nc
    with nc.cleanup_on_exit(), ExitStack() as ctx:
        _, _, sem = phase_tools(net, ctx, "init")
        zeroed, ident_ready, x_loaded = sem("zeroed"), sem("ident_ready"), sem("x_loaded")
        block = ctx.enter_context(nc.Block())

        @block.sync
        def _(sp):
            sp.dma_start(net.x[:], net.inp["x"].rearrange("b s d -> (b s) d").rearrange("(t p) d -> p t d", p=P)).then_inc(x_loaded, 16)
            sp.wait_ge(x_loaded, 16)

        @block.gpsimd
        def _(pool):
            nc.gpsimd.memset(net.ident[:], 0.0).then_inc(zeroed, 1)
            nc.gpsimd.memset(net.ones[:], 1.0)
            nc.gpsimd.memset(net.eps[:], EPS)
            pool.wait_ge(zeroed, 1)
            nc.gpsimd.affine_select(out=net.ident[:], in_=net.ident[:], compare_op=ALU.not_equal, fill=1.0, base=0,
                                    pattern=[[-1, P]], channel_multiplier=1).then_inc(ident_ready, 1)

        @block.vector
        def _(dve):
            dve.wait_ge(ident_ready, 1)
            nc.vector.tensor_copy(net.ident_r[:], net.ident[:])



def rope_context(net):
    nc = net.nc
    with nc.cleanup_on_exit(), ExitStack() as ctx:
        sb, ps, sem = phase_tools(net, ctx, "rope")
        cos, sin = sb("cos", [KP, NK, DC]), sb("sin", [KP, NK, DC])
        raw = sb("raw", [KP, 2, NK, DC])
        prod = sb("prod", [KP, 2, NK, DC])
        turned = sb("turned", [KP, 2, NK, DC])
        rows = sb("rows", [KP, 2, NK, DC])
        high = [sb(f"high{i}", [DC, L], F32R) for i in range(2)]
        low = [sb(f"low{i}", [DC, L], F32R) for i in range(2)]
        turn_ps = ps("turn_ps", [P, 2, 3, 512])
        tables_in, ctx_in = sem("tables_in"), [sem("ctx_in0"), sem("ctx_in1")]
        cos_done = sem("cos_done")
        sin_done = sem("sin_done")
        rows_done = sem("rows_done")
        turns_done = sem("turns_done")
        high_done = sem("high_done")
        low_done = sem("low_done")
        waited = sem("waited")
        rows_out = [sem("rows_out0"), sem("rows_out1")]
        parts_out = [sem("parts_out0"), sem("parts_out1")]
        HD = DC // 2
        block = ctx.enter_context(nc.Block())

        @block.sync
        def _(sp):
            def load(b, par):
                sp.wait_ge(cos_done, b + 1)
                sp.wait_ge(sin_done, b + 1)
                sp.dma_start(raw[:, par], net.inp["ctx_512"][b].rearrange("(p t) d -> p t d", t=NK)).then_inc(ctx_in[par], 16)

            def store(b, par):
                sp.wait_ge(rows_done, b + 3)
                sp.dma_start(net.kv_rows[b], rows[:, par]).then_inc(rows_out[par], 16)
                sp.wait_ge(high_done, b + 3)
                sp.dma_start(net.kv_high[b], high[par][:].bitcast(F32)).then_inc(parts_out[par], 16)
                sp.wait_ge(low_done, b + 3)
                sp.dma_start(net.kv_low[b], low[par][:].bitcast(F32)).then_inc(parts_out[par], 16)

            sp.dma_start(cos[:], net.inp["kv_cos"].rearrange("(p t) d -> p t d", t=NK)).then_inc(tables_in, 16)
            sp.dma_start(sin[:], net.inp["kv_sin"].rearrange("(p t) d -> p t d", t=NK)).then_inc(tables_in, 16)
            load(0, 0)
            load(1, 1)
            with sp.Fori(0, B // 2 - 1) as i:
                for par in (0, 1):
                    store(2 * i + par, par)
                    load(2 * i + par + 2, par)
            store(B - 2, 0)
            store(B - 1, 1)
            for par in (0, 1):
                sp.wait_ge(rows_out[par], 16 * (B // 2 + 1))
                sp.wait_ge(parts_out[par], 32 * (B // 2 + 1))

        @block.gpsimd
        def _(pool):
            pool.sem_inc(sin_done, 2)
            for par in (0, 1):
                pool.sem_inc(rows_out[par], 16)
                pool.sem_inc(parts_out[par], 32)
            pool.wait_ge(tables_in, 32)
            with pool.Fori(0, B // 2) as i:
                for par in (0, 1):
                    pool.wait_ge(ctx_in[par], 16 * i + 16)
                    pool.wait_ge(rows_done, 2 * i + par + 1)
                    nc.gpsimd.tensor_tensor(turned[:, par, :, 0:HD], raw[:, par, :, HD:DC], sin[:, :, 0:HD], ALU.mult)
                    nc.gpsimd.tensor_tensor(turned[:, par, :, HD:DC], raw[:, par, :, 0:HD], sin[:, :, HD:DC],
                                            ALU.mult).then_inc(sin_done, 1)

        @block.vector
        def _(dve):
            def rotate(b, i, par):
                dve.wait_ge(ctx_in[par], 16 * i + 16)
                nc.vector.tensor_tensor(prod[:, par], raw[:, par], cos[:], ALU.mult).then_inc(cos_done, 1)
                dve.wait_ge(sin_done, b + 3)
                dve.wait_ge(cos_done, b + 3)
                dve.wait_ge(rows_out[par], 16 * i + 16)
                dve.wait_ge(turns_done, b + 1)
                nc.vector.tensor_tensor(rows[:, par], prod[:, par], turned[:, par], ALU.add).then_inc(rows_done, 1)

            def split(b, i, par):
                dve.wait_ge(high_done, b + 3)
                dve.wait_ge(parts_out[par], 32 * i + 32)
                nc.vector.tensor_tensor(low[par][:].rearrange("p (a k) -> p a k", a=3), turn_ps[0:DC, par, :, 0:MC],
                                        high[par][:].bitcast(F32).rearrange("p (a k) -> p a k", a=3),
                                        ALU.subtract).then_inc(low_done, 1)

            for s in (cos_done, rows_done, low_done):
                dve.sem_inc(s, 2)
            dve.wait_ge(tables_in, 32)
            rotate(0, 0, 0)
            with dve.Fori(0, B // 2 - 1) as i:
                rotate(2 * i + 1, i, 1)
                split(2 * i, i, 0)
                rotate(2 * i + 2, i + 1, 0)
                split(2 * i + 1, i, 1)
            rotate(B - 1, B // 2 - 1, 1)
            split(B - 2, B // 2 - 1, 0)
            split(B - 1, B // 2 - 1, 1)

        @block.tensor
        def _(pe):
            pe.sem_inc(turns_done, 2)
            with pe.Fori(0, B // 2) as i:
                for par in (0, 1):
                    pe.wait_ge(rows_done, 2 * i + par + 3)
                    pe.wait_ge(high_done, 2 * i + par + 1)
                    pe.wait_ge(low_done, 2 * i + par + 1)
                    pe.sem_inc(waited, 1)
                    for t in range(NK):
                        last = nc.tensor.transpose(turn_ps[0:DC, par, t // 4, (t % 4) * KP:(t % 4 + 1) * KP],
                                                   rows[:, par, t, :], net.ident[0:KP, 0:KP])
                    last.then_inc(turns_done, 1)

        @block.scalar
        def _(act):
            act.sem_inc(high_done, 2)
            with act.Fori(0, B // 2) as i:
                for par in (0, 1):
                    act.wait_ge(turns_done, 2 * i + par + 3)
                    act.wait_ge(parts_out[par], 32 * i + 32)
                    nc.scalar.activation(high[par][:].rearrange("p (a k) -> p a k", a=3), turn_ps[0:DC, par, :, 0:MC],
                                         ACT.Copy).then_inc(high_done, 1)


def layer_norm(net, tag):
    nc = net.nc
    with nc.cleanup_on_exit(), ExitStack() as ctx:
        sb, ps, sem = phase_tools(net, ctx, tag)
        stats, mv = sb("stats", [P, TT, 6]), sb("mv", [P, TT, 2])
        std, rstd = sb("std", [P, TT]), sb("rstd", [P, TT])
        normed = sb("normed", [P, TT, D])
        turn_ps = ps("turn_ps", [P, TT, 512])
        stats_done, mv_done, std_done, rstd_done = sem("stats_done"), sem("mv_done"), sem("std_done"), sem("rstd_done")
        norm_done, turns_done = sem("norm_done"), sem("turns_done")
        block = ctx.enter_context(nc.Block())

        @block.vector
        def _(dve):
            for t in range(TT):
                nc.vector.bn_stats(stats[:, t, :], net.x[:, t, :]).then_inc(stats_done, 1)
            for t in range(TT):
                dve.wait_ge(stats_done, t + 1)
                nc.vector.bn_aggr(mv[:, t, :], stats[:, t, :]).then_inc(mv_done, 1)
            dve.wait_ge(std_done, 1)
            nc.vector.reciprocal(rstd[:], std[:]).then_inc(rstd_done, 1)
            dve.wait_ge(rstd_done, 1)
            for t in range(TT):
                nc.vector.tensor_scalar(normed[:, t, :], net.x[:, t, :], mv[:, t, 0:1], rstd[:, t:t + 1],
                                        ALU.subtract, ALU.mult).then_inc(norm_done, 1)

        @block.scalar
        def _(act):
            act.wait_ge(mv_done, TT)
            nc.scalar.activation(std[:], mv[:, :, 1], ACT.Sqrt, bias=net.eps[:, 0:1]).then_inc(std_done, 1)
            for t in range(TT):
                act.wait_ge(turns_done, t + 1)
                nc.scalar.activation(net.hT[:, :, t * P:(t + 1) * P], turn_ps[:, t, 0:D].rearrange("p (k c) -> p k c", k=KT),
                                     ACT.Copy)

        @block.tensor
        def _(pe):
            for t in range(TT):
                pe.wait_ge(norm_done, t + 1)
                for k in range(KT):
                    last = nc.tensor.transpose(turn_ps[:, t, k * P:(k + 1) * P], normed[:, t, k * P:(k + 1) * P], net.ident[:])
                last.then_inc(turns_done, 1)


def project_queries(net, tag, rope):
    nc = net.nc
    w = {k: net.inp[f"{tag}_xattn_{k}"] for k in ("Wq", "w_kc_q", "w_kc_kv", "W_qr", "W_kr", "Wo")}
    src = {
        "wq": w["Wq"].rearrange("(a i k) d -> i k a d", a=2, i=HP),
        "wcq": w["w_kc_q"].rearrange("(a i) k q -> i k a q", a=2),
        "wckv": w["w_kc_kv"].rearrange("(a i) k c -> i k a c", a=2),
        "wkr": w["W_kr"].rearrange("(a i) c r -> i c a r", a=2),
    }
    src_wqr = [w["W_qr"].rearrange("(a i) (z p) r -> a i p z r", a=2, p=AQ)[a] for a in (0, 1)]
    src_wo = [w["Wo"].rearrange("(z o) (a i k) -> a i o z k", z=KT, a=2, i=HP)[a] for a in (0, 1)]
    UN = 4 if rope else 2
    NLOAD = 8
    with nc.cleanup_on_exit(), ExitStack() as ctx:
        sb, ps, sem = phase_tools(net, ctx, tag + "p")
        wq, wcq = sb("wq", [P, 2, 2, D]), sb("wcq", [P, 2, 2, CQ])
        wckv, wkr = sb("wckv", [P, 2, 2, DC]), sb("wkr", [DC, 2, 2, R])
        wqr, wo = sb("wqr", [AQ, 2, 2, 2, R]), sb("wo", [P, 2, 2, KT, HK])
        rT = sb("rT", [R, 512])
        woT = sb("woT", [P, 2, D])
        c_sb = sb("c_sb", [AQ, 2, 2, 2, DC])
        if rope:
            b_sb = sb("b_sb", [P, 2, 2, KT, CQ])
            tab = sb("tab", [AQ, 4, CH])
            prod = sb("prod", [AQ, 2, 4, CH])
            y = sb("y", [AQ, 2, 2, CH])
        else:
            bt_sb = sb("bt_sb", [AQ, 2, 2, D])
            a_sb = sb("a_sb", [P, 2, KT, P])
        ps_rT, ps_wo = ps("ps_rT", [P, 512]), ps("ps_wo", [P, 512])
        ps_b, ps_big, ps_q = ps("ps_b", [P, 2, 512]), ps("ps_big", [P, 2, 512]), ps("ps_q", [P, 2, 512])
        w_in = [sem("w_in0"), sem("w_in1")]
        tab_in = sem("tab_in")
        b_mm = sem("b_mm")
        rT_mm, wo_mm, c_mm, m_mm, a_mm = sem("rT_mm"), sem("wo_mm"), sem("c_mm"), sem("m_mm"), sem("a_mm")
        rT_out, wo_out = sem("rT_out"), sem("wo_out")
        c_out, m_out, b_out, a_out = sem("c_out"), sem("m_out"), sem("b_out"), sem("a_out")
        big_mm = sem("big_mm")
        rope_done = sem("rope_done")
        y_done = sem("y_done")
        q_mm = sem("q_mm")
        high_done = sem("high_done")
        low_done = sem("low_done")
        block = ctx.enter_context(nc.Block())

        @block.sync
        def _(sp):
            if rope:
                sp.dma_start(tab[:], net.inp["q_tab"]).then_inc(tab_in, 16)
            with sp.Fori(0, HP // 2) as it:
                for par in (0, 1):
                    i = 2 * it + par
                    sp.wait_ge(b_mm, i + 1)
                    for dst, name in ((wq, "wq"), (wcq, "wcq"), (wckv, "wckv"), (wkr, "wkr")):
                        sp.dma_start(dst[:, par], src[name][i]).then_inc(w_in[par], 16)
                    for a in (0, 1):
                        sp.dma_start(wqr[:, par, a], src_wqr[a][i]).then_inc(w_in[par], 16)
                        sp.dma_start(wo[:, par, a], src_wo[a][i]).then_inc(w_in[par], 16)

        @block.tensor
        def _(pe):
            def turn_weights(i, par, it):
                pe.wait_ge(w_in[par], 16 * NLOAD * it + 16 * NLOAD)
                pe.wait_ge(c_out if rope else a_out, i + 1)
                pe.wait_ge(m_out, i + 1)
                for a in (0, 1):
                    for z in range(KT):
                        last = nc.tensor.transpose(ps_wo[:, a * D + z * P:a * D + (z + 1) * P], wo[:, par, a, z, :], net.ident[:])
                last.then_inc(wo_mm, 1)
                for a in (0, 1):
                    for z in (0, 1):
                        nc.tensor.transpose(ps_rT[0:R, (2 * a + z) * AQ:(2 * a + z + 1) * AQ], wqr[:, par, a, z, :],
                                            net.ident[0:AQ, 0:AQ])
                for a in (0, 1):
                    last = nc.tensor.transpose(ps_rT[0:R, 4 * AQ + a * DC:4 * AQ + (a + 1) * DC], wkr[:, par, a, :],
                                               net.ident[0:DC, 0:DC])
                last.then_inc(rT_mm, 1)

            def fold_weights(i, par):
                pe.wait_ge(rT_out, i + 1)
                for a in (0, 1):
                    for z in (0, 1):
                        last = nc.tensor.matmul(ps_rT[0:AQ, (2 * a + z) * DC:(2 * a + z + 1) * DC],
                                                rT[:, (2 * a + z) * AQ:(2 * a + z + 1) * AQ],
                                                rT[:, 4 * AQ + a * DC:4 * AQ + (a + 1) * DC], start=True, stop=True)
                last.then_inc(c_mm, 1)
                pe.wait_ge(wo_out, i + 1)
                for a in (0, 1):
                    last = nc.tensor.matmul(ps_wo[a * DC:(a + 1) * DC, 0:D], wckv[:, par, a, :], woT[:, a, :],
                                            start=True, stop=True)
                last.then_inc(m_mm, 1)
                pe.wait_ge(b_out, i + 1)
                for a in (0, 1):
                    for z in (0, 1):
                        if rope:
                            last = nc.tensor.matmul(ps_b[:, a, z * CQ:(z + 1) * CQ], wq[:, par, a, z * P:(z + 1) * P],
                                                    wcq[:, par, a, :], start=True, stop=True)
                        else:
                            last = nc.tensor.matmul(ps_b[0:AQ, a, z * D:(z + 1) * D], wcq[:, par, a, z * AQ:(z + 1) * AQ],
                                                    wq[:, par, a, :], start=True, stop=True)
                last.then_inc(b_mm, 1)

            def fold_all(i, par):
                pe.wait_ge(c_out, i + 2)
                pe.wait_ge(b_out, i + 2)
                for z in range(KT):
                    for a in (0, 1):
                        for q in (0, 1):
                            last = nc.tensor.matmul(ps_rT[:, (2 * z + a) * DC:(2 * z + a + 1) * DC],
                                                    bt_sb[:, a, q, z * P:(z + 1) * P], c_sb[:, par, a, q, :],
                                                    start=(q == 0), stop=(q == 1))
                last.then_inc(a_mm, 1)

            def prep(i, par, n, it=0):
                if n == 0:
                    turn_weights(i, par, it)
                if n == 1:
                    fold_weights(i, par)
                if n == 2 and not rope:
                    fold_all(i, par)

            def big(i, par, u):
                a, c = u // 2, u % 2
                if u == 0:
                    pe.wait_ge(b_out, i + 2)
                    pe.wait_ge(c_out, i + 2)
                pe.wait_ge(rope_done, 4 * i + u + 1)
                for z in (0, 1):
                    for k in range(KT):
                        last = nc.tensor.matmul(ps_big[0:AQ, z, 0:CH], b_sb[:, par, a, k, z * AQ:(z + 1) * AQ],
                                                net.hT[:, k, c * CH:(c + 1) * CH], start=(k == 0), stop=(k == KT - 1))
                last.then_inc(big_mm, 1)

            def final(i, par, u):
                a, c = u // 2, u % 2
                pe.wait_ge(y_done, 4 * i + u + 3)
                pe.wait_ge(low_done, 4 * i + u + 1)
                for z in (0, 1):
                    last = nc.tensor.matmul(ps_q[a * DC:(a + 1) * DC, c, 0:CH], c_sb[:, par, a, z, :], y[:, u % 2, z, :],
                                            start=(z == 0), stop=(z == 1))
                last.then_inc(q_mm, 1)

            def direct(i, par, c):
                if c == 0:
                    pe.wait_ge(a_out, i + 2)
                pe.wait_ge(low_done, 2 * i + c + 1)
                for k in range(KT):
                    last = nc.tensor.matmul(ps_q[:, c, 0:CH], a_sb[:, par, k, :], net.hT[:, k, c * CH:(c + 1) * CH],
                                            start=(k == 0), stop=(k == KT - 1))
                last.then_inc(q_mm, 1)

            def project(i, par, step):
                if rope:
                    big(i, par, 0)
                    step(0)
                    big(i, par, 1)
                    final(i, par, 0)
                    step(1)
                    big(i, par, 2)
                    final(i, par, 1)
                    big(i, par, 3)
                    final(i, par, 2)
                    final(i, par, 3)
                else:
                    direct(i, par, 0)
                    step(0)
                    direct(i, par, 1)
                    step(1)
                    step(2)

            pe.sem_inc(b_mm, 2)
            pe.sem_inc(q_mm, 2)
            if rope:
                pe.wait_ge(tab_in, 16)
            prep(0, 0, 0)
            prep(0, 0, 1)
            prep(0, 0, 2)
            with pe.Fori(0, HP // 2 - 1) as it:
                project(2 * it, 0, lambda n: prep(2 * it + 1, 1, n, it))
                project(2 * it + 1, 1, lambda n: prep(2 * it + 2, 0, n, it + 1))
            project(HP - 2, 0, lambda n: prep(HP - 1, 1, n, HP // 2 - 1))
            project(HP - 1, 1, lambda n: None)

        def place(i, a, c, rows):
            return net.q[rows, c * BC:(c + 1) * BC, bass.ds((i + HP * a) * S, S)]

        @block.scalar
        def _(act):
            def prep(i, par, n):
                if n == 0:
                    act.wait_ge(wo_mm, i + 1)
                    nc.scalar.activation(woT[:].rearrange("p a d -> p (a d)"), ps_wo[:], ACT.Copy).then_inc(wo_out, 1)
                if n == 1:
                    act.wait_ge(c_mm, i + 1)
                    nc.scalar.activation(c_sb[:, par].rearrange("p a z c -> p (a z c)"), ps_rT[0:AQ, 0:4 * DC],
                                         ACT.Copy).then_inc(c_out, 1)
                    act.wait_ge(m_mm, i + 1)
                    nc.scalar.activation(net.m[:, i, :], ps_wo[:, 0:D], ACT.Copy).then_inc(m_out, 1)
                    act.wait_ge(b_mm, i + 3)
                    if rope:
                        nc.scalar.activation(b_sb[:, par].rearrange("p a k q -> p a (k q)"), ps_b[:, :, 0:KT * CQ],
                                             ACT.Copy).then_inc(b_out, 1)
                    else:
                        nc.scalar.activation(bt_sb[:].rearrange("p a z d -> p a (z d)"), ps_b[0:AQ], ACT.Copy).then_inc(b_out, 1)

            def high(i, u):
                act.wait_ge(q_mm, UN * i + u + 3)
                c = u % 2
                for a in ((u // 2,) if rope else (0, 1)):
                    last = nc.scalar.activation(place(i, a, c, slice(0, DC)),
                                                ps_q[a * DC:(a + 1) * DC, c, 0:CH].rearrange("p (b s) -> p b s", s=S), ACT.Copy)
                last.then_inc(high_done, 1)

            def project(i, par, step):
                if rope:
                    step(0)
                    high(i, 0)
                    step(1)
                    for u in (1, 2, 3):
                        high(i, u)
                else:
                    high(i, 0)
                    step(0)
                    high(i, 1)
                    step(1)

            for s in (c_out, m_out, b_out):
                act.sem_inc(s, 1)
            prep(0, 0, 0)
            prep(0, 0, 1)
            with act.Fori(0, HP // 2 - 1) as it:
                project(2 * it, 0, lambda n: prep(2 * it + 1, 1, n))
                project(2 * it + 1, 1, lambda n: prep(2 * it + 2, 0, n))
            project(HP - 2, 0, lambda n: prep(HP - 1, 1, n))
            project(HP - 1, 1, lambda n: None)

        @block.vector
        def _(dve):
            def prep(i, par, n):
                if n == 0:
                    dve.wait_ge(rT_mm, i + 1)
                    nc.vector.tensor_copy(rT[:], ps_rT[0:R, :]).then_inc(rT_out, 1)
                if n == 2 and not rope:
                    dve.wait_ge(a_mm, i + 1)
                    nc.vector.tensor_copy(a_sb[:, par].rearrange("p k c -> p (k c)"), ps_rT[:, 0:KT * P]).then_inc(a_out, 1)

            def rotate(i, u):
                dve.wait_ge(big_mm, 4 * i + u + 1)
                dve.wait_ge(y_done, 4 * i + u + 1)
                for n, (z, table) in enumerate(((0, 0), (1, 2), (1, 1), (0, 3))):
                    last = nc.vector.tensor_tensor(prod[:, u % 2, n, :], ps_big[0:AQ, z, 0:CH], tab[:, table, :], ALU.mult)
                last.then_inc(rope_done, 1)

            def low(i, u):
                dve.wait_ge(high_done, UN * i + u + 1)
                c = u % 2
                for a in ((u // 2,) if rope else (0, 1)):
                    last = nc.vector.tensor_tensor(place(i, a, c, slice(DC, P)),
                                                   ps_q[a * DC:(a + 1) * DC, c, 0:CH].rearrange("p (b s) -> p b s", s=S),
                                                   place(i, a, c, slice(0, DC)).bitcast(F32), ALU.subtract)
                last.then_inc(low_done, 1)

            def project(i, step):
                if rope:
                    rotate(i, 0)
                    step(0)
                    rotate(i, 1)
                    low(i, 0)
                    rotate(i, 2)
                    low(i, 1)
                    rotate(i, 3)
                    low(i, 2)
                    low(i, 3)
                else:
                    low(i, 0)
                    step(0)
                    low(i, 1)
                    step(2)

            dve.sem_inc(low_done, UN)
            dve.sem_inc(rope_done, 1)
            dve.sem_inc(a_out, 1)
            if rope:
                dve.wait_ge(tab_in, 16)
            prep(0, 0, 0)
            prep(0, 0, 2)
            with dve.Fori(0, HP // 2 - 1) as it:
                project(2 * it, lambda n: prep(2 * it + 1, 1, n))
                project(2 * it + 1, lambda n: prep(2 * it + 2, 0, n))
            project(HP - 2, lambda n: prep(HP - 1, 1, n))
            project(HP - 1, lambda n: None)

        @block.gpsimd
        def _(pool):
            if not rope:
                return
            pool.sem_inc(y_done, 2)
            with pool.Fori(0, HP) as i:
                for u in range(4):
                    pool.wait_ge(rope_done, 4 * i + u + 2)
                    pool.wait_ge(q_mm, 4 * i + u + 1)
                    nc.gpsimd.tensor_tensor(y[:, u % 2, 0, :], prod[:, u % 2, 0, :], prod[:, u % 2, 1, :], ALU.add)
                    nc.gpsimd.tensor_tensor(y[:, u % 2, 1, :], prod[:, u % 2, 2, :], prod[:, u % 2, 3, :],
                                            ALU.add).then_inc(y_done, 1)


def attend(net, tag):
    nc = net.nc
    with nc.cleanup_on_exit(), ExitStack() as ctx:
        sb, ps, sem = phase_tools(net, ctx, tag)
        k_all = [sb(f"k_all{i}", [P, L], F32R) for i in (0, 1)]
        k_low = [sb(f"k_low{i}", [DC + 1, L], F32R) for i in (0, 1)]
        kv = [sb(f"kv{i}", [KP, NK, DC]) for i in (0, 1)]
        q_all = [sb(f"q_all{i}", [P, NQ], F32R) for i in (0, 1)]
        q_max = [sb(f"q_max{i}", [DC + 1, NQ], F32R) for i in (0, 1)]
        part_max = sb("part_max", [P, TT, 3])
        neg_max = [sb(f"neg_max{i}", [P, TT], F32R) for i in (0, 1)]
        total = [sb(f"total{i}", [KP, NQ]) for i in (0, 1)]
        raw = [sb(f"raw{i}", [P, CH]) for i in (0, 1)]
        inv = sb("inv", [P, CH])
        prob = sb("prob", [KP, 4, NQ])
        ps_s = ps("ps_s", [P, 2, 2, 512])
        ps_max = ps("ps_max", [P, 3, 512])
        ps_v = ps("ps_v", [P, 512])
        max_in = [sem("max_in0"), sem("max_in1")]
        rest_in = [sem("rest_in0"), sem("rest_in1")]
        ones_set = sem("ones_set")
        score_mm = sem("score_mm")
        exp_done = sem("exp_done")
        pv_mm = sem("pv_mm")
        pool_added = sem("pool_added")
        dve_added = sem("dve_added")
        max_mm = sem("max_mm")
        max_done = sem("max_done")
        neg_done = sem("neg_done")
        row_mm = sem("row_mm")
        row_done = sem("row_done")
        total_mm = sem("total_mm")
        inv_done = sem("inv_done")
        raw_done = sem("raw_done")
        out_done = sem("out_done")
        block = ctx.enter_context(nc.Block())
        MAX_LOADS, REST_LOADS = 16 * 3, 16 * 3
        KD = 3
        KA = NK - KD

        @block.sync
        def _(sp):
            def load(b, par):
                sp.dma_start(k_all[par][0:DC].bitcast(F32), net.kv_high[b]).then_inc(max_in[par], 16)
                sp.dma_start(k_all[par][DC:P].bitcast(F32), net.kv_high[b]).then_inc(max_in[par], 16)
                sp.dma_start(q_all[par][:].bitcast(F32), net.q[:, b, :].bitcast(F32)).then_inc(max_in[par], 16)
                sp.dma_start(q_max[par][0:DC].bitcast(F32), net.q[0:DC, b, :].bitcast(F32)).then_inc(rest_in[par], 16)
                sp.dma_start(k_low[par][0:DC].bitcast(F32), net.kv_low[b]).then_inc(rest_in[par], 16)
                sp.dma_start(kv[par][:], net.kv_rows[b]).then_inc(rest_in[par], 16)

            load(0, 0)
            load(1, 1)
            with sp.Fori(0, B // 2 - 1) as it:
                for par in (0, 1):
                    b = 2 * it + 2 + par
                    sp.wait_ge(pv_mm, NK * (b - 1) + 4)
                    load(b, par)

        def over_batches(eng, batch):
            batch(0, 0, 1, True, first=True)
            with eng.Fori(0, B // 2 - 1) as it:
                batch(2 * it + 1, 1, it + 1, True)
                batch(2 * it + 2, 0, it + 2, True)
            batch(B - 1, 1, B // 2, False)

        @block.tensor
        def _(pe):
            def max_block(b, par, j):
                for c in range(3):
                    pe.wait_ge(max_done, 3 * (TT * b + j) + c + 1)
                    nc.tensor.matmul(ps_max[:, c, 0:MC], q_all[par][:, j * P:(j + 1) * P],
                                     k_all[par][:, c * MC:(c + 1) * MC], start=True, stop=True).then_inc(max_mm, 1)

            def max_row(b, par):
                pe.wait_ge(neg_done, b + 2)
                for j in range(TT):
                    last = nc.tensor.matmul(ps_max[0:1, j // 4, (j % 4) * P:(j % 4 + 1) * P], neg_max[par][:, j:j + 1],
                                            net.ident_r[:], start=True, stop=True)
                last.then_inc(row_mm, 1)

            def scores(b, par, t):
                pe.wait_ge(exp_done, NK * b + t + 1)
                for c in (0, 1):
                    nc.tensor.matmul(ps_s[0:KP, t % 2, c, 0:CH], k_all[par][:, t * KP:(t + 1) * KP],
                                     q_all[par][:, c * CH:(c + 1) * CH], start=True, stop=False)
                for c in (0, 1):
                    last = nc.tensor.matmul(ps_s[0:KP, t % 2, c, 0:CH], k_low[par][:, t * KP:(t + 1) * KP],
                                            q_max[par][:, c * CH:(c + 1) * CH], start=False, stop=True)
                last.then_inc(score_mm, 1)

            def values(b, par, t):
                pe.wait_ge(exp_done, NK * b + t + 3)
                if t == 0:
                    pe.wait_ge(raw_done, b + 1)
                for c in (0, 1):
                    last = nc.tensor.matmul(ps_v[c * DC:(c + 1) * DC, 0:CH], kv[par][:, t, :], prob[:, t % 4, c * CH:(c + 1) * CH],
                                            start=(t == 0), stop=(t == NK - 1))
                last.then_inc(pv_mm, 1)

            def totals(b, par):
                pe.wait_ge(dve_added, KD * b + KD + 3)
                for c in (0, 1):
                    last = nc.tensor.matmul(ps_max[c * DC:(c + 1) * DC, 2, 0:CH], net.ones[0:KP, 0:DC],
                                            total[par][:, c * CH:(c + 1) * CH], start=True, stop=True)
                last.then_inc(total_mm, 1)

            def batch(b, par, nth, more, first=False):
                pe.wait_ge(rest_in[par], REST_LOADS * nth)
                pe.wait_ge(row_done, b + 1)
                for t in range(NK):
                    scores(b, par, t)
                    if t >= 2:
                        values(b, par, t - 2)
                    if t == 1 and not first:
                        totals(b - 1, 1 - par)
                    if more and 4 <= t <= 10:
                        if t == 4:
                            pe.wait_ge(max_in[1 - par], MAX_LOADS * (nth + par))
                            pe.wait_ge(inv_done, b + 1)
                        max_block(b + 1, 1 - par, t - 4)
                values(b, par, NK - 2)
                if more:
                    max_row(b + 1, 1 - par)
                values(b, par, NK - 1)
                if not more:
                    totals(b, par)

            pe.sem_inc(pv_mm, 4)
            pe.sem_inc(total_mm, 2)
            pe.wait_ge(ones_set, 2)
            pe.wait_ge(max_in[0], MAX_LOADS)
            for j in range(TT):
                max_block(0, 0, j)
            max_row(0, 0)
            over_batches(pe, batch)

        @block.scalar
        def _(act):
            def row(b, par):
                act.wait_ge(row_mm, b + 1)
                nc.scalar.activation(q_max[par][DC:DC + 1, :], ps_max[0:1].rearrange("p a k -> p (a k)")[:, 0:NQ],
                                     ACT.Copy).then_inc(row_done, 1)

            def batch(b, par, nth, more, first=False):
                for t in range(NK):
                    act.wait_ge(score_mm, NK * b + t + 1)
                    act.wait_ge(pv_mm, NK * b + t + 1)
                    if 1 <= t <= KD:
                        act.wait_ge(dve_added, KD * b + t)
                    else:
                        act.wait_ge(pool_added, KA * b + max(t - 3, 0) + 1)
                    nc.scalar.activation(prob[:, t % 4, :].rearrange("p (c q) -> p c q", c=2), ps_s[0:KP, t % 2, :, 0:CH],
                                         ACT.Exp).then_inc(exp_done, 1)
                if more:
                    row(b + 1, 1 - par)
                act.wait_ge(pv_mm, NK * b + NK + 4)
                act.wait_ge(out_done, b + 1)
                nc.scalar.activation(raw[par][:], ps_v[:, 0:CH], ACT.Copy).then_inc(raw_done, 1)

            act.sem_inc(exp_done, 2)
            act.sem_inc(raw_done, 1)
            row(0, 0)
            over_batches(act, batch)

        @block.vector
        def _(dve):
            def maxima(b, par):
                for n in range(TT * 3):
                    dve.wait_ge(max_mm, 3 * TT * b + n + 1)
                    if n == 0:
                        dve.wait_ge(neg_done, b + 1)
                    nc.vector.tensor_reduce(part_max[:, n // 3, n % 3:n % 3 + 1], ps_max[:, n % 3, 0:MC], AX.X,
                                            ALU.max).then_inc(max_done, 1)
                dve.wait_ge(max_done, 3 * TT * (b + 1) + 3)
                nc.vector.tensor_reduce(neg_max[par][:], part_max[:], AX.X, ALU.max, negate=True).then_inc(neg_done, 1)

            def divide(b, par):
                dve.wait_ge(total_mm, b + 3)
                dve.wait_ge(out_done, b + 2)
                nc.vector.reciprocal(inv[:], ps_max[:, 2, 0:CH]).then_inc(inv_done, 1)
                dve.wait_ge(inv_done, b + 2)
                dve.wait_ge(raw_done, b + 2)
                nc.vector.tensor_tensor(net.cT[:, :, bass.ds(b * S, S)], raw[par][:].rearrange("p (h s) -> p h s", s=S),
                                        inv[:].rearrange("p (h s) -> p h s", s=S), ALU.mult).then_inc(out_done, 1)

            def batch(b, par, nth, more, first=False):
                if not first:
                    divide(b - 1, 1 - par)
                if more:
                    maxima(b + 1, 1 - par)
                for k in range(KD):
                    if k == 0:
                        dve.wait_ge(pool_added, KA * b + KA + 1)
                    else:
                        dve.wait_ge(dve_added, KD * b + k + 3)
                    dve.wait_ge(exp_done, NK * b + KA + k + 3)
                    nc.vector.tensor_tensor(total[par][:], total[par][:], prob[:, (KA + k) % 4, :], ALU.add).then_inc(dve_added, 1)
                if not more:
                    divide(b, par)

            dve.sem_inc(max_done, 3)
            dve.sem_inc(neg_done, 1)
            dve.sem_inc(dve_added, 3)
            dve.sem_inc(inv_done, 1)
            dve.sem_inc(out_done, 2)
            maxima(0, 0)
            over_batches(dve, batch)

        @block.gpsimd
        def _(pool):
            def batch(b, par, nth, more, first=False):
                pool.wait_ge(total_mm, b + 1)
                for t in range(1, KA):
                    pool.wait_ge(exp_done, NK * b + t + 3)
                    if t > 1:
                        pool.wait_ge(pool_added, KA * b + t + 1)
                    nc.gpsimd.tensor_tensor(total[par][:], prob[:, 0, :] if t == 1 else total[par][:], prob[:, t % 4, :],
                                            ALU.add).then_inc(pool_added, 2 if t == 1 else 1)

            nc.gpsimd.memset(k_low[0][DC:DC + 1, :].bitcast(F32), 1.0).then_inc(ones_set, 1)
            nc.gpsimd.memset(k_low[1][DC:DC + 1, :].bitcast(F32), 1.0).then_inc(ones_set, 1)
            pool.sem_inc(pool_added, 1)
            over_batches(pool, batch)


def add_attention(net, tag):
    nc = net.nc
    with nc.cleanup_on_exit(), ExitStack() as ctx:
        sb, ps, sem = phase_tools(net, ctx, tag + "o")
        ps_o = ps("ps_o", [P, TT, 512])
        o_mm = sem("o_mm")
        block = ctx.enter_context(nc.Block())

        @block.tensor
        def _(pe):
            for t in range(TT):
                for j in range(HP):
                    last = nc.tensor.matmul(ps_o[:, t, 0:D], net.cT[:, j, t * P:(t + 1) * P], net.m[:, j, :],
                                            start=(j == 0), stop=(j == HP - 1))
                last.then_inc(o_mm, 1)

        @block.vector
        def _(dve):
            for t in range(TT):
                dve.wait_ge(o_mm, t + 1)
                nc.vector.tensor_tensor(net.x[:, t, :], ps_o[:, t, 0:D], net.x[:, t, :], ALU.add)


def route(net, tag, n, top_k, w_name, bias_name, turn):
    nc = net.nc
    blocks = turn
    with nc.cleanup_on_exit(), ExitStack() as ctx:
        sb, ps, sem = phase_tools(net, ctx, tag + "r")
        w, bias, ids = sb("w", [P, KT, n]), sb("bias", [P, n]), sb("ids", [P, n])
        w_raw = sb("w_raw", [n, D])
        rank = sb("rank", [P, TT, n])
        top, idx, idx_f = sb("top", [P, TT, 8]), sb("idx", [P, TT, 8], U32), sb("idx_f", [P, TT, 8])
        hit, mask = sb("hit", [P, TT, top_k, n]), sb("mask", [P, TT, n])
        biased, peak, gap, e = sb("biased", [P, TT, n]), sb("peak", [P, TT]), sb("gap", [P, TT, n]), sb("e", [P, TT, n])
        chosen, total, inv, gate = sb("chosen", [P, TT, n]), sb("total", [P, TT]), sb("inv", [P, TT]), sb("gate", [P, TT, n])
        gate_t, one_rows = sb("gate_t", [n, NT]), sb("one_rows", [2, NT])
        ps_l, ps_t, ps_w = ps("ps_l", [P, 512]), ps("ps_t", [P, 2, 512]), ps("ps_w", [P, 512])
        w_in, turned, turn_out = sem("w_in"), sem("turned"), sem("turn_out")
        l_mm, gap_done, exp_done, gate_done = sem("l_mm"), sem("gap_done"), sem("exp_done"), sem("gate_done")
        t_mm, t_out, ones_set, stored = sem("t_mm"), sem("t_out"), sem("ones_set"), sem("stored")
        step = sem("step")
        logits = ps_l[:, 0:TT * n].rearrange("p (t e) -> p t e", e=n)
        block = ctx.enter_context(nc.Block())

        def wide(ap):
            return ap.unsqueeze(2).to_broadcast([P, TT, n])

        @block.sync
        def _(sp):
            if turn:
                sp.dma_start(w_raw[:], net.inp[w_name]).then_inc(w_in, 16)
            else:
                sp.dma_start(w[:], net.inp[w_name].rearrange("(k p) e -> p k e", p=P)).then_inc(w_in, 16)
            sp.dma_start(bias[:], net.inp[bias_name].partition_broadcast(P)).then_inc(w_in, 16)
            sp.dma_start(ids[:], net.inp["expert_ids"][0:n].partition_broadcast(P)).then_inc(w_in, 16)
            sp.wait_ge(t_out, 1)
            sp.dma_start(net.gates[0:n, :], gate_t[:]).then_inc(stored, 16)
            sp.wait_ge(ones_set, 1)
            sp.dma_start(net.gates[E0:E0 + 2, :], one_rows[:]).then_inc(stored, 16)
            sp.wait_ge(stored, 32)

        @block.gpsimd
        def _(pool):
            nc.gpsimd.memset(one_rows[:], 1.0).then_inc(ones_set, 1)

        @block.tensor
        def _(pe):
            pe.wait_ge(w_in, 48)
            if turn:
                for k in range(KT):
                    last = nc.tensor.transpose(ps_w[:, k * n:(k + 1) * n], w_raw[:, k * P:(k + 1) * P], net.ident[0:n, 0:n])
                last.then_inc(turned, 1)
                pe.wait_ge(turn_out, 1)
            for t in range(TT):
                for k in range(KT):
                    last = nc.tensor.matmul(ps_l[:, t * n:(t + 1) * n], net.hT[:, k, t * P:(t + 1) * P], w[:, k, :],
                                            start=(k == 0), stop=(k == KT - 1))
            last.then_inc(l_mm, 1)
            pe.wait_ge(gate_done, 1)
            for t in range(TT):
                last = nc.tensor.transpose(ps_t[0:n, t // 4, (t % 4) * P:(t % 4 + 1) * P], gate[:, t, :], net.ident[:])
            last.then_inc(t_mm, 1)

        @block.scalar
        def _(act):
            if turn:
                act.wait_ge(turned, 1)
                nc.scalar.activation(w[:].rearrange("p k e -> p (k e)"), ps_w[:, 0:KT * n], ACT.Copy).then_inc(turn_out, 1)
            act.wait_ge(gap_done, 1)
            nc.scalar.activation(e[:], gap[:], ACT.Exp).then_inc(exp_done, 1)
            act.wait_ge(t_mm, 1)
            nc.scalar.activation(gate_t[:], ps_t[0:n].rearrange("p a k -> p (a k)")[:, 0:NT], ACT.Copy).then_inc(t_out, 1)

        @block.vector
        def _(dve):
            count = [0]

            def done(ins):
                count[0] += 1
                ins.then_inc(step, 1)
                dve.wait_ge(step, count[0])

            def exponentials(values):
                done(nc.vector.tensor_reduce(peak[:], values, AX.X, ALU.max))
                nc.vector.tensor_tensor(gap[:], values, wide(peak[:]), ALU.subtract).then_inc(gap_done, 1)
                dve.wait_ge(exp_done, 1)

            def normalise(out, values):
                done(nc.vector.tensor_reduce(total[:], values, AX.X, ALU.add))
                done(nc.vector.reciprocal(inv[:], total[:]))
                return nc.vector.tensor_tensor(out, values, wide(inv[:]), ALU.mult)

            dve.wait_ge(l_mm, 1)
            by_bias = bias[:].unsqueeze(1).to_broadcast([P, TT, n])
            if blocks:
                done(nc.vector.tensor_tensor(biased[:], logits, by_bias, ALU.add))
                exponentials(biased[:])
                done(normalise(rank[:], e[:]))
            else:
                done(nc.vector.tensor_tensor(rank[:], logits, by_bias, ALU.add))
            for t in range(TT):
                done(nc.vector.max(top[:, t, :], rank[:, t, :]))
                done(nc.vector.max_index(idx[:, t, :], top[:, t, :], rank[:, t, :]))
            done(nc.vector.tensor_copy(idx_f[:], idx[:]))
            for t in range(TT):
                ins = nc.vector.tensor_tensor(hit[:, t], ids[:].unsqueeze(1).to_broadcast([P, top_k, n]),
                                              idx_f[:, t, 0:top_k].unsqueeze(2).to_broadcast([P, top_k, n]), ALU.is_equal)
            done(ins)
            if blocks:
                nc.vector.tensor_reduce(gate[:], hit[:].rearrange("p t k e -> p t e k"), AX.X, ALU.add).then_inc(gate_done, 1)
            else:
                done(nc.vector.tensor_reduce(mask[:], hit[:].rearrange("p t k e -> p t e k"), AX.X, ALU.add))
                exponentials(logits)
                done(nc.vector.tensor_tensor(chosen[:], e[:], mask[:], ALU.mult))
                normalise(gate[:], chosen[:]).then_inc(gate_done, 1)


def run_experts(net, tag, tiles, load, up, func, turn=False, bias1=False, before=None, first=None):
    nc = net.nc
    NU = 1 + up
    NW = 4
    with nc.cleanup_on_exit(), ExitStack() as ctx:
        sb, ps, sem = phase_tools(net, ctx, tag + "f")
        w1 = sb("w1", [P, NW, NU, KT, P])
        w2 = sb("w2", [P, NW, D])
        if turn:
            w1_raw, w2_raw = sb("w1_raw", [P, NW, KT, P]), sb("w2_raw", [P, NW, KT, P])
        gate = sb("gate", [P, NW, NT])
        b1 = sb("b1", [P, NW, 1])
        act_out = sb("act_out", [P, 2, CH])
        prod = sb("prod", [P, 2, CH])
        hid = sb("hid", [P, 2, NT])
        zero = sb("zero", [P, 512])
        ps_y = ps("ps_y", [P, 4, 512])
        ps_h = ps("ps_h", [P, 2 * NU, 512])
        if turn:
            ps_w = ps("ps_w", [P, 512])
        loaded = [sem(f"loaded{u}") for u in range(NW)]
        zero_set = sem("zero_set")
        turned, turn_out = sem("turned"), sem("turn_out")
        h_mm = sem("h_mm")
        act_done = sem("act_done")
        prod_done = sem("prod_done")
        hid_done = sem("hid_done")
        y_mm = sem("y_mm")
        block = ctx.enter_context(nc.Block())
        n_loads = []

        def y_at(t):
            return ps_y[:, t // 2, (t % 2) * D:(t % 2 + 1) * D]

        @block.sync
        def _(sp):
            bufs = {"w1": w1_raw if turn else w1, "w2": w2_raw if turn else w2, "gate": gate, "b1": b1}

            def start(part, m, in_part, u):
                sp.wait_ge(y_mm, m + 1)
                moves = load(part, in_part, u, bufs)
                for dst, src in moves:
                    sp.dma_start(dst, src).then_inc(loaded[u], 16)
                n_loads.append(len(moves))

            if before:
                before(sp)
            at = 0
            for part, n in enumerate(tiles):
                if n > NW:
                    with sp.Fori(0, n // NW) as it:
                        for u in range(NW):
                            start(part, at + NW * it + u, NW * it + u, u)
                else:
                    for u in range(NW):
                        start(part, at + u, u, u)
                at += n

        N = sum(tiles)
        assert len(set(n_loads)) == 1 and all(n % NW == 0 for n in tiles)
        LOADS = 16 * n_loads[0]

        def over_tiles(hidden, output):
            def run(eng):
                hidden(0, 0, 0)
                with eng.Fori(0, N // NW - 1) as it:
                    for u in range(NW):
                        hidden(NW * it + u + 1, (u + 1) % NW, it + (u + 1) // NW)
                        output(NW * it + u, u)
                for u in range(NW):
                    if u + 1 < NW:
                        hidden(N - NW + u + 1, u + 1, N // NW - 1)
                    output(N - NW + u, u)
            return run

        @block.tensor
        def _(pe):
            def hidden(m, u, it):
                pe.wait_ge(loaded[u], LOADS * it + LOADS)
                if turn:
                    pe.wait_ge(turn_out, m + 1)
                    for k in range(KT):
                        nc.tensor.transpose(ps_w[:, k * P:(k + 1) * P], w1_raw[:, u, k, :], net.ident[:])
                    for z in range(KT):
                        last = nc.tensor.transpose(ps_w[:, (KT + z) * P:(KT + z + 1) * P], w2_raw[:, u, z, :], net.ident[:])
                    last.then_inc(turned, 1)
                    pe.wait_ge(turn_out, m + 2)
                for c in (0, 1):
                    pe.wait_ge(act_done, 2 * m + c + 1)
                    if up:
                        pe.wait_ge(prod_done, 2 * m + c + 1)
                    for n in range(NU):
                        for k in range(KT):
                            last = nc.tensor.matmul(ps_h[:, NU * c + n, 0:CH], w1[:, u, n, k, :],
                                                    net.hT[:, k, c * CH:(c + 1) * CH], start=(k == 0), stop=(k == KT - 1))
                    last.then_inc(h_mm, 1)

            def output(m, u):
                pe.wait_ge(hid_done, 2 * m + 4)
                for t in range(TT):
                    last = nc.tensor.matmul(y_at(t), hid[:, u % 2, t * P:(t + 1) * P], w2[:, u, :],
                                            start=False, stop=False, skip_group_check=True)
                last.then_inc(y_mm, 1)

            pe.sem_inc(y_mm, NW)
            pe.wait_ge(zero_set, 1)
            for a in range(4):
                nc.tensor.matmul(ps_y[:, a, :], zero[:, 0:P], zero[:], start=True, stop=False, skip_group_check=True)
            if first:
                first(pe, y_at)
            over_tiles(hidden, output)(pe)

        @block.scalar
        def _(act):
            def hidden(m, u, it):
                if turn:
                    act.wait_ge(turned, m + 1)
                    nc.scalar.activation(w1[:, u].rearrange("p n k c -> p (n k c)"), ps_w[:, 0:KT * P], ACT.Copy)
                    nc.scalar.activation(w2[:, u], ps_w[:, KT * P:2 * KT * P], ACT.Copy).then_inc(turn_out, 1)
                for c in (0, 1):
                    act.wait_ge(h_mm, 2 * m + c + 1)
                    act.wait_ge(prod_done if up else hid_done, 2 * m + c + 1)
                    if bias1:
                        ins = nc.scalar.activation(act_out[:, c], ps_h[:, NU * c, 0:CH], func, bias=b1[:, u, :])
                    else:
                        ins = nc.scalar.activation(act_out[:, c], ps_h[:, NU * c, 0:CH], func)
                    ins.then_inc(act_done, 1)

            act.sem_inc(act_done, 2)
            if turn:
                act.sem_inc(turn_out, 1)
            with act.Fori(0, N // NW) as it:
                for u in range(NW):
                    hidden(NW * it + u, u, it)

        def gated(eng, m, u, c, src):
            eng.wait_ge(y_mm, m + NW - 1)
            eng.tensor_tensor(hid[:, u % 2, c * CH:(c + 1) * CH], src, gate[:, u, c * CH:(c + 1) * CH], ALU.mult).then_inc(hid_done, 1)

        @block.vector
        def _(dve):
            nc.vector.memset(zero[:], 0.0).then_inc(zero_set, 1)
            dve.sem_inc(prod_done, 2)
            if not up:
                dve.sem_inc(hid_done, 2)
            with dve.Fori(0, N // NW) as it:
                for u in range(NW):
                    m = NW * it + u
                    for c in (0, 1):
                        dve.wait_ge(act_done, 2 * m + c + 3)
                        if up:
                            dve.wait_ge(hid_done, 2 * m + c + 1)
                            nc.vector.tensor_tensor(prod[:, c], ps_h[:, NU * c + 1, 0:CH], act_out[:, c], ALU.mult).then_inc(prod_done, 1)
                        else:
                            if c == 0:
                                dve.wait_ge(loaded[u], LOADS * it + LOADS)
                            gated(dve, m, u, c, act_out[:, c])
            dve.wait_ge(y_mm, N + NW)
            for t in range(TT):
                nc.vector.tensor_tensor(net.x[:, t, :], y_at(t), net.x[:, t, :], ALU.add)

        @block.gpsimd
        def _(pool):
            if not up:
                return
            pool.sem_inc(hid_done, 2)
            with pool.Fori(0, N // NW) as it:
                for u in range(NW):
                    m = NW * it + u
                    pool.wait_ge(loaded[u], LOADS * it + LOADS)
                    for c in (0, 1):
                        pool.wait_ge(prod_done, 2 * m + c + 3)
                        gated(pool, m, u, c, prod[:, c])


def experts_0(net):
    def load(part, m, u, bufs):
        moves = []
        for n, name in enumerate(("wg", "wu")):
            for k in range(KT):
                if part == 0:
                    src = net.inp["L0_ffn_" + name].rearrange("(m e) (k p) f -> m k p e f", e=2, p=P)[m, k]
                else:
                    src = net.inp["L0_ffn_s" + name].rearrange("s (k p) (j f) -> s j k p f", p=P, f=P)[u // 2, u % 2, k]
                dst = bufs["w1"][:, u, n, k, :]
                moves.append((dst.rearrange("p (e f) -> p e f", e=2) if part == 0 else dst, src))
        if part == 0:
            moves.append((bufs["w2"][:, u], net.inp["L0_ffn_wd"].rearrange("(m e) f d -> m (e f) d", e=2)[m]))
            rows = net.gates[0:E0].rearrange("(m e) n -> m e n", e=2)[m]
        else:
            moves.append((bufs["w2"][:, u], net.inp["L0_ffn_swd"].rearrange("s (j f) d -> (s j) f d", f=P)[m]))
            rows = net.gates[E0:E0 + 2]
        for e in (0, 1):
            moves.append((bufs["gate"][e * F0:(e + 1) * F0, u, :], rows[e].partition_broadcast(F0)))
        return moves

    run_experts(net, "L0", (E0 * F0 // P, 4), load, True, ACT.Silu)


def ternary_layer(net):
    nc = net.nc
    with nc.cleanup_on_exit(), ExitStack() as ctx:
        sb, ps, sem = phase_tools(net, ctx, "L1f")
        w, bias = sb("w", [P, KT, D]), sb("bias", [P, D])
        part, scale, inv = sb("part", [P, 1]), sb("scale", [P, 2]), sb("inv", [P, 1])
        r, up_, down, tern, diff = sb("r", [P, KT, D]), sb("up", [P, KT, D]), sb("down", [P, KT, D]), sb("tern", [P, KT, D]), sb("diff", [P, KT, D])
        ste, wT = sb("ste", [P, KT, D]), sb("wT", [P, KT, D])
        xb = sb("xb", [P, TT, D])
        ps_s, ps_w, ps_y = ps("ps_s", [P, 512]), ps("ps_w", [P, 512]), ps("ps_y", [P, 4, 512])
        w_in, part_done, s_mm, ste_done, t_mm, t_out, y_mm = (
            sem("w_in"), sem("part_done"), sem("s_mm"), sem("ste_done"), sem("t_mm"), sem("t_out"), sem("y_mm"))
        step = sem("step")
        block = ctx.enter_context(nc.Block())

        @block.sync
        def _(sp):
            sp.dma_start(w[:], net.inp["L1_ffn_weight"].rearrange("(z p) d -> p z d", p=P)).then_inc(w_in, 16)
            sp.dma_start(bias[:], net.inp["L1_ffn_bias"].partition_broadcast(P)).then_inc(w_in, 16)

        @block.vector
        def _(dve):
            n = [0]

            def done(ins):
                n[0] += 1
                ins.then_inc(step, 1)
                dve.wait_ge(step, n[0])

            dve.wait_ge(w_in, 32)
            nc.vector.tensor_reduce(part[:], w[:], AX.XY, ALU.add, apply_absolute_value=True).then_inc(part_done, 1)
            dve.wait_ge(s_mm, 1)
            done(nc.vector.tensor_scalar(scale[:, 0:1], ps_s[:, 0:1], 1.0 / (D * D), None, ALU.mult))
            done(nc.vector.tensor_scalar(scale[:, 1:2], scale[:, 0:1], 1e-10, None, ALU.add))
            done(nc.vector.reciprocal(inv[:], scale[:, 1:2]))
            done(nc.vector.tensor_scalar(r[:], w[:], inv[:, 0:1], None, ALU.mult))
            done(nc.vector.tensor_scalar(up_[:], r[:], 0.5, None, ALU.is_gt))
            done(nc.vector.tensor_scalar(down[:], r[:], -0.5, None, ALU.is_lt))
            done(nc.vector.tensor_tensor(tern[:], up_[:], down[:], ALU.subtract))
            done(nc.vector.scalar_tensor_tensor(diff[:], tern[:], scale[:, 0:1], w[:], ALU.mult, ALU.subtract))
            nc.vector.tensor_tensor(ste[:], w[:], diff[:], ALU.add).then_inc(ste_done, 1)
            for t in range(TT):
                ins = nc.vector.tensor_tensor(xb[:, t, :], net.x[:, t, :], bias[:], ALU.add)
            done(ins)
            for t in range(TT):
                dve.wait_ge(y_mm, t // 2 + 1)
                nc.vector.tensor_tensor(net.x[:, t, :], ps_y[:, t // 2, (t % 2) * D:(t % 2 + 1) * D], xb[:, t, :], ALU.add)

        @block.tensor
        def _(pe):
            pe.wait_ge(part_done, 1)
            nc.tensor.matmul(ps_s[:, 0:1], net.ones[:], part[:], start=True, stop=True).then_inc(s_mm, 1)
            pe.wait_ge(ste_done, 1)
            for k in range(KT):
                for z in range(KT):
                    last = nc.tensor.transpose(ps_w[:, k * D + z * P:k * D + (z + 1) * P], ste[:, z, k * P:(k + 1) * P], net.ident[:])
            last.then_inc(t_mm, 1)
            pe.wait_ge(t_out, 1)
            for t in range(TT):
                for k in range(KT):
                    last = nc.tensor.matmul(ps_y[:, t // 2, (t % 2) * D:(t % 2 + 1) * D], net.hT[:, k, t * P:(t + 1) * P],
                                            wT[:, k, :], start=(k == 0), stop=(k == KT - 1))
                if t % 2 or t == TT - 1:
                    last.then_inc(y_mm, 1)

        @block.scalar
        def _(act):
            act.wait_ge(t_mm, 1)
            nc.scalar.activation(wT[:].rearrange("p k d -> p (k d)"), ps_w[:], ACT.Copy).then_inc(t_out, 1)


def experts_2(net):
    def load(part, m, u, bufs):
        moves = [(bufs["w1"][:, u].rearrange("p k c -> p (k c)"), net.inp["L2_ffn_W1"].rearrange("(m p) d -> m p d", p=P)[m])]
        moves.append((bufs["w2"][:, u], net.inp["L2_ffn_W2"].rearrange("(z p) (m f) -> m p z f", p=P, f=P)[m]))
        rows = net.gates[0:E2].rearrange("(m e) n -> m e n", e=2)[m]
        for e in (0, 1):
            moves.append((bufs["gate"][e * F2:(e + 1) * F2, u, :], rows[e].partition_broadcast(F2)))
        return moves

    run_experts(net, "L2", (E2 * F2 // P,), load, False, ACT.Gelu, turn=True)


def route_3(net):
    nc = net.nc
    with nc.cleanup_on_exit(), ExitStack() as ctx:
        sb, ps, sem = phase_tools(net, ctx, "L3r")
        w, w_raw, logits = sb("w", [P, KT, E3]), sb("w_raw", [E3, D]), sb("logits", [P, TT, E3])
        sums, top = sb("sums", [1, E3]), sb("top", [1, 8])
        own, peak = sb("own", [P, TOP3, TT]), sb("peak", [P, TT])
        gap, e = sb("gap", [P, TOP3, TT]), sb("e", [P, TOP3, TT])
        total, inv, rw = sb("total", [P, TT]), sb("inv", [P, TT]), sb("rw", [P, TOP3, TT])
        rw_t = sb("rw_t", [TOP3 * TT, P])
        ps_w, ps_l, ps_s, ps_t = ps("ps_w", [P, 512]), ps("ps_l", [P, 512]), ps("ps_s", [P, 512]), ps("ps_t", [P, 512])
        w_in, turned, turn_out, l_mm, l_out, s_mm = sem("w_in"), sem("turned"), sem("turn_out"), sem("l_mm"), sem("l_out"), sem("s_mm")
        picked, gap_done, exp_done, rw_done = sem("picked"), sem("gap_done"), sem("exp_done"), sem("rw_done")
        t_mm, t_out, stored, own_in = sem("t_mm"), sem("t_out"), sem("stored"), sem("own_in")
        step = sem("step")
        block = ctx.enter_context(nc.Block())

        @block.sync
        def _(sp):
            sp.dma_start(w_raw[:], net.inp["L3_ffn_gate_w"]).then_inc(w_in, 16)
            sp.wait_ge(picked, 1)
            for k in range(TOP3):
                sel = sp.value_load(net.sel[0:1, k:k + 1], min_val=0, max_val=E3 - 1)
                sp.dma_start(net.b2[k:k + 1, :], net.inp["L3_ffn_b2"][bass.ds(sel, 1), :]).then_inc(own_in, 16)
            sp.wait_ge(t_out, 1)
            sp.dma_start(net.gates[0:TOP3].rearrange("k (t p) -> (k t) p", p=P), rw_t[:]).then_inc(stored, 16)
            sp.wait_ge(stored, 16)
            sp.dma_start(net.rw[:], net.gates[0:TOP3]).then_inc(own_in, 16)
            sp.wait_ge(own_in, 16 * (TOP3 + 1))

        @block.tensor
        def _(pe):
            pe.wait_ge(w_in, 16)
            for k in range(KT):
                last = nc.tensor.transpose(ps_w[:, k * E3:(k + 1) * E3], w_raw[:, k * P:(k + 1) * P], net.ident[0:E3, 0:E3])
            last.then_inc(turned, 1)
            pe.wait_ge(turn_out, 1)
            for t in range(TT):
                for k in range(KT):
                    last = nc.tensor.matmul(ps_l[:, t * E3:(t + 1) * E3], net.hT[:, k, t * P:(t + 1) * P], w[:, k, :],
                                            start=(k == 0), stop=(k == KT - 1))
            last.then_inc(l_mm, 1)
            pe.wait_ge(l_out, 1)
            nc.tensor.matmul(ps_s[0:1, 0:TT * E3], net.ones[:, 0:1], logits[:].rearrange("p t e -> p (t e)"),
                             start=True, stop=True).then_inc(s_mm, 1)
            pe.wait_ge(rw_done, 1)
            nc.tensor.transpose(ps_t[0:TOP3 * TT, 0:P], rw[:].rearrange("p k t -> p (k t)"), net.ident[:]).then_inc(t_mm, 1)

        @block.scalar
        def _(act):
            act.wait_ge(turned, 1)
            nc.scalar.activation(w[:].rearrange("p k e -> p (k e)"), ps_w[:, 0:KT * E3], ACT.Copy).then_inc(turn_out, 1)
            act.wait_ge(gap_done, TOP3)
            nc.scalar.activation(e[:], gap[:], ACT.Exp).then_inc(exp_done, 1)
            act.wait_ge(t_mm, 1)
            nc.scalar.activation(rw_t[:], ps_t[0:TOP3 * TT, 0:P], ACT.Copy).then_inc(t_out, 1)

        @block.vector
        def _(dve):
            count = [0]

            def done(ins):
                count[0] += 1
                ins.then_inc(step, 1)
                dve.wait_ge(step, count[0])

            dve.wait_ge(l_mm, 1)
            nc.vector.tensor_copy(logits[:].rearrange("p t e -> p (t e)"), ps_l[:, 0:TT * E3]).then_inc(l_out, 1)
            dve.wait_ge(s_mm, 1)
            done(nc.vector.tensor_reduce(sums[:], ps_s[0:1, 0:TT * E3].rearrange("p (t e) -> p e t", e=E3), AX.X, ALU.add))
            done(nc.vector.max(top[:], sums[:]))
            nc.vector.max_index(net.sel[:], top[:], sums[:]).then_inc(picked, 1)
            dve.wait_ge(picked, 1)
            dve.wait_ge(l_out, 1)
            for k in range(TOP3):
                sel = dve.value_load(net.sel[0:1, k:k + 1], min_val=0, max_val=E3 - 1)
                done(nc.vector.tensor_copy(own[:, k, :], logits[:, :, bass.ds(sel, 1)].rearrange("p t e -> p (t e)")))
            done(nc.vector.tensor_tensor(peak[:], own[:, 0, :], own[:, 1, :], ALU.max))
            for k in range(TOP3):
                nc.vector.tensor_tensor(gap[:, k, :], own[:, k, :], peak[:], ALU.subtract).then_inc(gap_done, 1)
            dve.wait_ge(exp_done, 1)
            done(nc.vector.tensor_tensor(total[:], e[:, 0, :], e[:, 1, :], ALU.add))
            done(nc.vector.reciprocal(inv[:], total[:]))
            nc.vector.tensor_tensor(rw[:], e[:], inv[:].unsqueeze(1).to_broadcast([P, TOP3, TT]), ALU.mult).then_inc(rw_done, 1)


def experts_3(net):
    sel = []

    def before(sp):
        for k in range(TOP3):
            sel.append(sp.value_load(net.sel[0:1, k:k + 1], min_val=0, max_val=E3 - 1))

    def load(part, tile, u, bufs):
        w1 = net.inp["L3_ffn_w1"].rearrange("e (k p) (m f) -> e m p k f", p=P, f=P)[sel[part], tile]
        w2 = net.inp["L3_ffn_w2"].rearrange("e (m f) d -> e m f d", f=P)[sel[part], tile]
        b1 = net.inp["L3_ffn_b1"].rearrange("e (m f u) -> e m f u", f=P, u=1)[sel[part], tile]
        return [(bufs["w1"][:, u, 0], w1), (bufs["w2"][:, u], w2), (bufs["b1"][:, u], b1),
                (bufs["gate"][:, u, :], net.gates[part].partition_broadcast(P))]

    def first(pe, y_at):
        for t in range(TT):
            net.nc.tensor.matmul(y_at(t), net.rw[:, t * P:(t + 1) * P], net.b2[:], start=False, stop=False, skip_group_check=True)

    run_experts(net, "L3", (F3 // P, F3 // P), load, False, ACT.Gelu_apprx_tanh, bias1=True, before=before, first=first)


HD2, NB2 = D // 16, 8
QB2 = 2 * S


def project_small(net):
    nc = net.nc
    with nc.cleanup_on_exit(), ExitStack() as ctx:
        sb, ps, sem = phase_tools(net, ctx, "L2p")
        wq, wk, wv = sb("wq", [HD2, H, D]), sb("wk", [HD2, H, DC]), sb("wv", [HD2, H, DC])
        wo, woT = sb("wo", [P, KT, D]), sb("woT", [HD2, H, D])
        a_sb = sb("a_sb", [P, KT, HP, 2, DC])
        ps_a = ps("ps_a", [P, 4, 512])
        ps_t = ps("ps_t", [P, 4, 512])
        w_in, t_mm, t_out, a_mm, a_out, m_mm, m_out, q_mm, q_out = (
            sem("w_in"), sem("t_mm"), sem("t_out"), sem("a_mm"), sem("a_out"), sem("m_mm"), sem("m_out"), sem("q_mm"), sem("q_out"))
        kv = net.inp["L2_xattn_Wkv_expand"].rearrange("(v h j) c -> v j h c", v=2, j=HD2)
        block = ctx.enter_context(nc.Block())

        @block.sync
        def _(sp):
            sp.dma_start(wq[:], net.inp["L2_xattn_Wq"].rearrange("(h j) d -> j h d", j=HD2)).then_inc(w_in, 16)
            sp.dma_start(wk[:], kv[0]).then_inc(w_in, 16)
            sp.dma_start(wv[:], kv[1]).then_inc(w_in, 16)
            sp.dma_start(wo[:], net.inp["L2_xattn_Wout"].rearrange("(z p) d -> p z d", p=P)).then_inc(w_in, 16)

        @block.tensor
        def _(pe):
            pe.wait_ge(w_in, 64)
            for k in range(KT):
                for h in range(H):
                    last = nc.tensor.matmul(ps_a[:, 2 * k + h // HP, (h % HP) * DC:(h % HP + 1) * DC],
                                            wq[:, h, k * P:(k + 1) * P], wk[:, h, :], start=True, stop=True)
            last.then_inc(a_mm, 1)
            for r in (0, 1):
                pe.wait_ge(t_out, r) if r else None
                for h in range(HP):
                    for z in range(KT):
                        last = nc.tensor.transpose(ps_t[0:HD2, h // 2, (h % 2) * D + z * P:(h % 2) * D + (z + 1) * P],
                                                   wo[:, z, (HP * r + h) * HD2:(HP * r + h + 1) * HD2], net.ident[:])
                last.then_inc(t_mm, 1)
            pe.wait_ge(t_out, 2)
            for h in range(H):
                last = nc.tensor.matmul(ps_t[(h // HP) * DC:(h // HP + 1) * DC, (h % HP) // 2, (h % 2) * D:(h % 2 + 1) * D],
                                        wv[:, h, :], woT[:, h, :], start=True, stop=True)
            last.then_inc(m_mm, 1)
            pe.wait_ge(a_out, 1)
            for i in range(HP):
                for c in (0, 1):
                    n = 2 * i + c
                    if n >= 4:
                        pe.wait_ge(q_out, n - 3)
                    for k in range(KT):
                        last = nc.tensor.matmul(ps_a[:, n % 4, 0:CH], a_sb[:, k, i].rearrange("p a c -> p (a c)"),
                                                net.hT[:, k, c * CH:(c + 1) * CH], start=(k == 0), stop=(k == KT - 1))
                    last.then_inc(q_mm, 1)

        @block.scalar
        def _(act):
            act.wait_ge(a_mm, 1)
            for k in range(KT):
                for a in (0, 1):
                    last = nc.scalar.activation(a_sb[:, k, :, a, :], ps_a[:, 2 * k + a, :].rearrange("p (i c) -> p i c", c=DC),
                                                ACT.Copy, scale=0.25)
            last.then_inc(a_out, 1)
            act.wait_ge(m_mm, 1)
            nc.scalar.activation(net.m[:], ps_t[:].rearrange("p b (h d) -> p (b h) d", d=D), ACT.Copy).then_inc(m_out, 1)

        @block.vector
        def _(dve):
            for r in (0, 1):
                dve.wait_ge(t_mm, r + 1)
                nc.vector.tensor_copy(woT[:, HP * r:HP * r + HP, :], ps_t[0:HD2].rearrange("p b (h d) -> p (b h) d", d=D)).then_inc(t_out, 1)
            for i in range(HP):
                for c in (0, 1):
                    n = 2 * i + c
                    dve.wait_ge(q_mm, n + 1)
                    nc.vector.tensor_copy(net.q2[:, c * BC:(c + 1) * BC, i * S:(i + 1) * S],
                                          ps_a[:, n % 4, 0:CH].rearrange("p (b s) -> p b s", s=S)).then_inc(q_out, 1)


def attend_small(net):
    nc = net.nc
    with nc.cleanup_on_exit(), ExitStack() as ctx:
        sb, ps, sem = phase_tools(net, ctx, "L2a")
        q = sb("q", [P, 2, CH])
        lat = sb("lat", [S, 2, 2, DC])
        latT = sb("latT", [P, 2, S])
        mask = sb("mask", [QB2, S])
        masked, gap = sb("masked", [QB2, 2, NB2, S]), sb("gap", [QB2, 2, NB2, S])
        peak, e = sb("peak", [QB2, 2, NB2]), sb("e", [QB2, 2, NB2, S])
        total, inv, prob = sb("total", [QB2, 2, NB2]), sb("inv", [QB2, 2, NB2]), sb("prob", [QB2, 2, NB2, S])
        probT = sb("probT", [S, 2, NQ])
        ps_l, ps_s = ps("ps_l", [P, 512]), ps("ps_s", [P, 2, 2, 512])
        ps_t, ps_v = ps("ps_t", [P, 2, 512]), ps("ps_v", [P, 512])
        mask_in, loaded = sem("mask_in"), [sem("loaded0"), sem("loaded1")]
        waited, l_mm, l_out = sem("waited"), sem("l_mm"), sem("l_out")
        s_mm = sem("s_mm")
        masked_done = sem("masked_done")
        peak_done, total_done, inv_done = sem("peak_done"), sem("total_done"), sem("inv_done")
        gap_done = sem("gap_done")
        exp_done = sem("exp_done")
        prob_done = sem("prob_done")
        t_mm = sem("t_mm")
        t_out = sem("t_out")
        v_mm = sem("v_mm")
        v_out = sem("v_out")
        block = ctx.enter_context(nc.Block())

        def over_batches(eng, front, back):
            front(0, 0, 0)
            with eng.Fori(0, B // 2 - 1) as it:
                front(2 * it + 1, 1, it)
                back(2 * it, 0)
                front(2 * it + 2, 0, it + 1)
                back(2 * it + 1, 1)
            front(B - 1, 1, B // 2 - 1)
            back(B - 2, 0)
            back(B - 1, 1)

        @block.sync
        def _(sp):
            sp.dma_start(mask[:], net.inp["causal"]).then_inc(mask_in, 16)
            with sp.Fori(0, B // 2) as it:
                for par in (0, 1):
                    b = 2 * it + par
                    sp.wait_ge(v_mm, b + 1)
                    for a in (0, 1):
                        sp.dma_start(lat[:, par, a, :], net.inp["ctx_512"][b, 0:S, :]).then_inc(loaded[par], 16)
                    sp.dma_start(q[:, par, :], net.q2[:, b, :]).then_inc(loaded[par], 16)

        @block.tensor
        def _(pe):
            def front(b, par, it):
                pe.wait_ge(loaded[par], 48 * it + 48)
                pe.sem_inc(waited, 1)
                nc.tensor.transpose(ps_l[:, 0:S], lat[:, par].rearrange("p a c -> p (a c)"), net.ident[0:S, 0:S]).then_inc(l_mm, 1)
                pe.wait_ge(l_out, b + 1)
                pe.wait_ge(masked_done, b + 1)
                for a in (0, 1):
                    for n in range(NB2 // 2):
                        last = nc.tensor.matmul(ps_s[0:QB2, par, a, n * S:(n + 1) * S], q[a * DC:(a + 1) * DC, par, n * QB2:(n + 1) * QB2],
                                                latT[a * DC:(a + 1) * DC, par, :], start=True, stop=True)
                last.then_inc(s_mm, 1)

            def back(b, par):
                pe.wait_ge(prob_done, b + 1)
                pe.wait_ge(t_out, b + 1)
                pe.sem_inc(waited, 1)
                for n in range(NB2):
                    a, m = n // 4, n % 4
                    last = nc.tensor.transpose(ps_t[0:S, a, m * QB2:(m + 1) * QB2], prob[:, par, n, :], net.ident[0:QB2, 0:QB2])
                last.then_inc(t_mm, 1)
                pe.wait_ge(t_out, b + 2)
                pe.wait_ge(v_out, b + 1)
                pe.sem_inc(waited, 1)
                for a in (0, 1):
                    last = nc.tensor.matmul(ps_v[a * DC:(a + 1) * DC, 0:CH], lat[:, par, 0, :], probT[:, par, a * CH:(a + 1) * CH],
                                            start=True, stop=True)
                last.then_inc(v_mm, 1)

            pe.sem_inc(v_mm, 2)
            over_batches(pe, front, back)

        @block.vector
        def _(dve):
            def bc(ap):
                return ap.unsqueeze(2).to_broadcast([QB2, NB2, S])

            def front(b, par, it):
                dve.wait_ge(l_mm, b + 1)
                nc.vector.tensor_copy(latT[:, par, :], ps_l[:, 0:S]).then_inc(l_out, 1)
                dve.wait_ge(s_mm, b + 1)
                nc.vector.tensor_tensor(masked[:, par].rearrange("p (a n) s -> p a n s", a=2),
                                        ps_s[0:QB2, par, :, 0:NB2 // 2 * S].rearrange("p a (n s) -> p a n s", s=S),
                                        mask[:].unsqueeze(1).unsqueeze(1).to_broadcast([QB2, 2, NB2 // 2, S]),
                                        ALU.add).then_inc(masked_done, 1)
                dve.wait_ge(masked_done, b + 3)
                nc.vector.tensor_reduce(peak[:, par], masked[:, par], AX.X, ALU.max).then_inc(peak_done, 1)
                dve.wait_ge(peak_done, b + 1)
                nc.vector.tensor_tensor(gap[:, par], masked[:, par], bc(peak[:, par]), ALU.subtract).then_inc(gap_done, 1)

            def back(b, par):
                dve.wait_ge(exp_done, b + 1)
                nc.vector.tensor_reduce(total[:, par], e[:, par], AX.X, ALU.add).then_inc(total_done, 1)
                dve.wait_ge(total_done, b + 1)
                nc.vector.reciprocal(inv[:, par], total[:, par]).then_inc(inv_done, 1)
                dve.wait_ge(inv_done, b + 1)
                nc.vector.tensor_tensor(prob[:, par], e[:, par], bc(inv[:, par]), ALU.mult).then_inc(prob_done, 1)

            dve.sem_inc(masked_done, 2)
            dve.wait_ge(mask_in, 16)
            over_batches(dve, front, back)

        @block.scalar
        def _(act):
            def front(b, par, it):
                act.wait_ge(gap_done, b + 1)
                nc.scalar.activation(e[:, par], gap[:, par], ACT.Exp).then_inc(exp_done, 1)

            def back(b, par):
                act.wait_ge(t_mm, b + 1)
                nc.scalar.activation(probT[:, par].rearrange("p (a q) -> p a q", a=2), ps_t[0:S, :, 0:CH], ACT.Copy).then_inc(t_out, 1)
                act.wait_ge(v_mm, b + 3)
                nc.scalar.activation(net.cT[:, :, bass.ds(b * S, S)], ps_v[:, 0:CH].rearrange("p (h s) -> p h s", s=S),
                                     ACT.Copy).then_inc(v_out, 1)

            act.sem_inc(t_out, 1)
            act.sem_inc(v_out, 1)
            over_batches(act, front, back)


def store_result(net):
    nc = net.nc
    with nc.cleanup_on_exit(), ExitStack() as ctx:
        _, _, sem = phase_tools(net, ctx, "fin")
        stored = sem("stored")
        block = ctx.enter_context(nc.Block())

        @block.sync
        def _(sp):
            sp.dma_start(net.out.rearrange("b s d -> (b s) d").rearrange("(t p) d -> p t d", p=P), net.x[:]).then_inc(stored, 16)
            sp.wait_ge(stored, 16)


def network(nc, inp, out, upto=99, start_at=0):
    net = Net()
    net.nc, net.inp, net.out = nc, inp, out
    with ExitStack() as ctx:
        def sb(name, shape, dt=F32):
            return ctx.enter_context(nc.sbuf_tensor("net_" + name, shape, dt))

        net.x = sb("x", [P, TT, D])
        net.hT = sb("hT", [P, KT, NT])
        net.ident, net.ident_r = sb("ident", [P, P]), sb("ident_r", [P, P], F32R)
        net.ones, net.eps = sb("ones", [P, P]), sb("eps", [P, 1])
        net.kv_rows = nc.dram_tensor("kv_rows", (B, KP, NK, DC), F32).ap()
        net.kv_high = nc.dram_tensor("kv_high", (B, DC, L), F32).ap()
        net.kv_low = nc.dram_tensor("kv_low", (B, DC, L), F32).ap()
        net.gates = nc.dram_tensor("gates", (E0 + 2, NT), F32).ap()
        load_constants(net)
        rope_context(net)

        def latent_attention(tag, rope):
            with nc.cleanup_on_exit(), ExitStack() as own:
                net.q = own.enter_context(nc.sbuf_tensor(tag + "_q", [P, B, NQ], F32R))
                net.cT = own.enter_context(nc.sbuf_tensor(tag + "_cT", [P, HP, NT], F32))
                net.m = own.enter_context(nc.sbuf_tensor(tag + "_m", [P, HP, D], F32))
                layer_norm(net, tag + "n")
                project_queries(net, tag, rope)
                attend(net, tag)
                add_attention(net, tag)

        def layer_0_experts():
            layer_norm(net, "L0g")
            route(net, "L0", E0, TOP0, "L0_ffn_router_w", "L0_ffn_router_bias", False)
            experts_0(net)

        def layer_1_dense():
            layer_norm(net, "L1g")
            ternary_layer(net)

        def layer_2_attention():
            with nc.cleanup_on_exit(), ExitStack() as own:
                net.q2 = own.enter_context(nc.sbuf_tensor("L2_q2", [P, B, CH], F32))
                net.cT = own.enter_context(nc.sbuf_tensor("L2_cT", [P, HP, NT], F32))
                net.m = own.enter_context(nc.sbuf_tensor("L2_m", [P, HP, D], F32))
                layer_norm(net, "L2n")
                project_small(net)
                attend_small(net)
                add_attention(net, "L2")

        def layer_2_blocks():
            layer_norm(net, "L2g")
            route(net, "L2", E2, TOP2, "L2_ffn_Wr", "L2_ffn_br", True)
            experts_2(net)

        def layer_3_experts():
            with nc.cleanup_on_exit(), ExitStack() as own:
                net.sel = own.enter_context(nc.sbuf_tensor("L3_sel", [1, 8], U32))
                net.rw = own.enter_context(nc.sbuf_tensor("L3_rw", [TOP3, NT], F32))
                net.b2 = own.enter_context(nc.sbuf_tensor("L3_b2", [TOP3, D], F32))
                layer_norm(net, "L3g")
                route_3(net)
                experts_3(net)

        steps = [lambda: latent_attention("L0", False), layer_0_experts, lambda: latent_attention("L1", True), layer_1_dense,
                 layer_2_attention, layer_2_blocks, lambda: latent_attention("L3", True), layer_3_experts]
        for s in steps[start_at:upto]:
            s()
        store_result(net)


_SHAPES = None


def _tables():
    def angles(n, dim):
        inv = (np.float32(1.0) / np.float32(10000.0) ** (np.arange(0, dim, 2, dtype=np.float32) / np.float32(dim))).astype(np.float32)
        f = np.arange(n, dtype=np.float32)[:, None] * inv[None, :]
        return np.repeat(np.sin(f), 2, axis=-1).astype(np.float32), np.repeat(np.cos(f), 2, axis=-1).astype(np.float32)

    sin, cos = angles(L, DC)
    sin = np.concatenate([-sin[:, :DC // 2], sin[:, DC // 2:]], axis=1)
    qs, qc = angles(S, CQ)
    qs = np.concatenate([-qs[:, :AQ], qs[:, AQ:]], axis=1)
    tab = np.stack([np.tile(t.T, (1, BC)) for t in (qc[:, :AQ], qc[:, AQ:], qs[:, :AQ], qs[:, AQ:])], axis=1)
    return {"kv_cos": cos, "kv_sin": sin, "q_tab": np.ascontiguousarray(tab), "expert_ids": np.arange(E0, dtype=np.float32),
            "causal": np.where(np.arange(S)[None, :] <= np.arange(QB2)[:, None] % S, 0, NEG).astype(np.float32)}


def kernel(**inputs):
    import concourse.bacc as _bacc
    from concourse import mybir as _mybir
    from concourse.bass_utils import run_bass_kernel_spmd as _run

    nc = _bacc.Bacc("TRN2", target_bir_lowering=False, num_devices=1)
    arrays, inp = {}, {}
    for name, a in {**inputs, **_tables()}.items():
        a = np.ascontiguousarray(a)
        arrays[f"in_{name}"] = a
        inp[name] = nc.dram_tensor(f"in_{name}", a.shape, _mybir.dt.from_np(a.dtype), kind="ExternalInput").ap()
    out = nc.dram_tensor("out_x", (B, S, D), F32, kind="ExternalOutput").ap()
    network(nc, inp, out)
    r = _run(nc, [arrays], core_ids=[0])
    return r.results[0]["out_x"]
```

```python
from contextlib import ExitStack

import concourse.bass as bass
import numpy as np
from concourse import mybir

F32 = mybir.dt.float32
F32R = mybir.dt.float32r
U32 = mybir.dt.uint32
ALU = mybir.AluOpType
ACT = mybir.ActivationFunctionType
AX = mybir.AxisListType

P = 128
B, S, D = 16, 56, 256
NT = B * S
TT = NT // P
KT = D // P
CH = NT // 2
BC = B // 2
L, DC = 1500, 64
H, HK, CQ, R = 16, 128, 192, 64
HP = H // 2
AQ = CQ // 2
NQ = H * S
KP = 125
NK = L // KP
MC = L // 3
EPS = 1e-5
E0, F0, TOP0, SH0 = 64, 64, 4, 512
E2, F2, TOP2 = 16, 64, 4
E3, F3, TOP3 = 8, 1024, 2
NEG = -1.0e30


class Net:
    pass


def phase_tools(net, ctx, tag):
    nc = net.nc

    def sb(name, shape, dt=F32):
        return ctx.enter_context(nc.sbuf_tensor(f"{tag}_{name}", shape, dt))

    def ps(name, shape, dt=F32):
        return ctx.enter_context(nc.psum_tensor(f"{tag}_{name}", shape, dt))

    def sem(name):
        return nc.alloc_semaphore(f"{tag}_{name}")

    return sb, ps, sem


def load_constants(net):
    nc = net.nc
    with nc.cleanup_on_exit(), ExitStack() as ctx:
        _, _, sem = phase_tools(net, ctx, "init")
        zeroed, ident_ready, x_loaded = sem("zeroed"), sem("ident_ready"), sem("x_loaded")
        block = ctx.enter_context(nc.Block())

        @block.sync
        def _(sp):
            sp.dma_start(net.x[:], net.inp["x"].rearrange("b s d -> (b s) d").rearrange("(t p) d -> p t d", p=P)).then_inc(x_loaded, 16)
            sp.wait_ge(x_loaded, 16)

        @block.gpsimd
        def _(pool):
            nc.gpsimd.memset(net.ident[:], 0.0).then_inc(zeroed, 1)
            nc.gpsimd.memset(net.ones[:], 1.0)
            nc.gpsimd.memset(net.eps[:], EPS)
            pool.wait_ge(zeroed, 1)
            nc.gpsimd.affine_select(out=net.ident[:], in_=net.ident[:], compare_op=ALU.not_equal, fill=1.0, base=0,
                                    pattern=[[-1, P]], channel_multiplier=1).then_inc(ident_ready, 1)

        @block.vector
        def _(dve):
            dve.wait_ge(ident_ready, 1)
            nc.vector.tensor_copy(net.ident_r[:], net.ident[:])



class Rotation:

    GROUPS = 3
    HD = DC // 2

    def __init__(self, net, ctx):
        self.net, self.nc = net, net.nc
        sb, ps, sem = phase_tools(net, ctx, "rope")
        self.cos, self.sin = sb("cos", [KP, NK, DC]), sb("sin", [KP, NK, DC])
        self.raw = sb("raw", [KP, 2, NK, DC])
        flat = net.cT[:].rearrange("p k n -> p (k n)")
        self.prod, self.turned, self.rows = (
            flat[0:KP, TT * D + n * 2 * NK * DC:TT * D + (n + 1) * 2 * NK * DC].rearrange("p (a t d) -> p a t d", a=2, t=NK)
            for n in range(3))
        self.high = [sb(f"high{i}", [DC, L], F32R) for i in range(2)]
        self.low = [sb(f"low{i}", [DC, L], F32R) for i in range(2)]
        self.tables_in, self.ctx_in = sem("tables_in"), [sem("ctx_in0"), sem("ctx_in1")]
        self.cos_done, self.sin_done = sem("cos_done"), sem("sin_done")
        self.rows_done = sem("rows_done")
        self.turns_done = sem("turns_done")
        self.high_done = sem("high_done")
        self.low_done = sem("low_done")
        self.waited = sem("waited")
        self.rows_out = [sem("rows_out0"), sem("rows_out1")]
        self.parts_out = [sem("parts_out0"), sem("parts_out1")]

    def psum(self, ctx):
        _, ps, _ = phase_tools(self.net, ctx, "rope")
        self.turn_ps = ps("turn_ps", [P, 2, 512])


    def load(self, sp, b, par):
        sp.wait_ge(self.cos_done, b + 1)
        sp.wait_ge(self.sin_done, b + 1)
        sp.dma_start(self.raw[:, par], self.net.inp["ctx_512"][b].rearrange("(p t) d -> p t d", t=NK)).then_inc(self.ctx_in[par], 16)

    def early(self, sp):
        sp.dma_start(self.cos[:], self.net.inp["kv_cos"].rearrange("(p t) d -> p t d", t=NK)).then_inc(self.tables_in, 16)
        sp.dma_start(self.sin[:], self.net.inp["kv_sin"].rearrange("(p t) d -> p t d", t=NK)).then_inc(self.tables_in, 16)
        for b in (0, 1):
            sp.dma_start(self.raw[:, b], self.net.inp["ctx_512"][b].rearrange("(p t) d -> p t d", t=NK)).then_inc(self.ctx_in[b], 16)

    def store_rows(self, sp, b, par):
        sp.wait_ge(self.rows_done, b + 3)
        sp.dma_start(self.net.kv_rows[b], self.rows[:, par]).then_inc(self.rows_out[par], 16)

    def store_parts(self, sp, b, par):
        sp.wait_ge(self.low_done, self.GROUPS * b + self.GROUPS + 2)
        sp.dma_start(self.net.kv_high[b], self.high[par][:].bitcast(F32)).then_inc(self.parts_out[par], 16)
        sp.dma_start(self.net.kv_low[b], self.low[par][:].bitcast(F32)).then_inc(self.parts_out[par], 16)

    def wait_stores(self, sp):
        for par in (0, 1):
            sp.wait_ge(self.rows_out[par], 16 * (B // 2 + 1))
            sp.wait_ge(self.parts_out[par], 32 * (B // 2 + 1))


    def multiply_sin(self, pool):
        pool.sem_inc(self.sin_done, 2)
        for par in (0, 1):
            pool.sem_inc(self.rows_out[par], 16)
            pool.sem_inc(self.parts_out[par], 32)
        pool.wait_ge(self.tables_in, 32)
        with pool.Fori(0, B // 2) as i:
            for par in (0, 1):
                pool.wait_ge(self.ctx_in[par], 16 * i + 16)
                pool.wait_ge(self.rows_done, 2 * i + par + 1)
                HD = self.HD
                self.nc.gpsimd.tensor_tensor(self.turned[:, par, :, 0:HD], self.raw[:, par, :, HD:DC], self.sin[:, :, 0:HD], ALU.mult)
                self.nc.gpsimd.tensor_tensor(self.turned[:, par, :, HD:DC], self.raw[:, par, :, 0:HD], self.sin[:, :, HD:DC],
                                             ALU.mult).then_inc(self.sin_done, 1)

    def start_vector(self, dve):
        for s in (self.cos_done, self.rows_done, self.low_done):
            dve.sem_inc(s, 2)
        dve.wait_ge(self.tables_in, 32)

    def rotate(self, dve, i, par):
        b = 2 * i + par
        dve.wait_ge(self.ctx_in[par], 16 * i + 16)
        self.nc.vector.tensor_tensor(self.prod[:, par], self.raw[:, par], self.cos[:], ALU.mult).then_inc(self.cos_done, 1)
        dve.wait_ge(self.sin_done, b + 3)
        dve.wait_ge(self.cos_done, b + 3)
        dve.wait_ge(self.rows_out[par], 16 * i + 16)
        dve.wait_ge(self.turns_done, self.GROUPS * b + 3)
        self.nc.vector.tensor_tensor(self.rows[:, par], self.prod[:, par], self.turned[:, par], ALU.add).then_inc(self.rows_done, 1)


    def place(self, i, n):
        par, g = n // self.GROUPS, n % self.GROUPS
        return 2 * i + par, par, g, 6 * i + n, n % 2

    def transpose(self, pe, i, n):
        b, par, g, number, bank = self.place(i, n)
        pe.wait_ge(self.rows_done, b + 3)
        pe.wait_ge(self.low_done, number + 1)
        pe.sem_inc(self.waited, 1)
        for t in range(4):
            last = self.nc.tensor.transpose(self.turn_ps[0:DC, bank, t * KP:(t + 1) * KP], self.rows[:, par, 4 * g + t, :],
                                            self.net.ident[0:KP, 0:KP])
        last.then_inc(self.turns_done, 1)

    def take_high(self, act, i, n):
        b, par, g, number, bank = self.place(i, n)
        act.wait_ge(self.turns_done, number + 7)
        if g == 0:
            act.wait_ge(self.parts_out[par], 32 * i + 32)
        self.nc.scalar.activation(self.high[par][:, g * MC:(g + 1) * MC], self.turn_ps[0:DC, bank, 0:MC],
                                  ACT.Copy).then_inc(self.high_done, 1)

    def take_low(self, dve, i, n):
        b, par, g, number, bank = self.place(i, n)
        dve.wait_ge(self.high_done, number + 1)
        if g == 0:
            dve.wait_ge(self.parts_out[par], 32 * i + 32)
        self.nc.vector.tensor_tensor(self.low[par][:, g * MC:(g + 1) * MC], self.turn_ps[0:DC, bank, 0:MC],
                                     self.high[par][:, g * MC:(g + 1) * MC].bitcast(F32), ALU.subtract).then_inc(self.low_done, 1)


def layer_norm(net, tag, early):
    nc = net.nc
    with nc.cleanup_on_exit(), ExitStack() as ctx:
        sb, ps, sem = phase_tools(net, ctx, tag)
        stats, mv = sb("stats", [P, TT, 6]), sb("mv", [P, TT, 2])
        std, rstd = sb("std", [P, TT]), sb("rstd", [P, TT])
        normed = net.cT[:, 0:KT, :].rearrange("p k n -> p (k n)").rearrange("p (t d) -> p t d", d=D)
        turn_ps = ps("turn_ps", [P, TT, 512])
        stats_done, mv_done, std_done, rstd_done = sem("stats_done"), sem("mv_done"), sem("std_done"), sem("rstd_done")
        norm_done, turns_done, high_done = sem("norm_done"), sem("turns_done"), sem("high_done")
        block = ctx.enter_context(nc.Block())

        def tile(h, t):
            return h[:, :, t * P:(t + 1) * P]

        def turned(t):
            return turn_ps[:, t, 0:D].rearrange("p (k c) -> p k c", k=KT)

        @block.sync
        def _(sp):
            early(sp)

        @block.vector
        def _(dve):
            for t in range(TT):
                nc.vector.bn_stats(stats[:, t, :], net.x[:, t, :]).then_inc(stats_done, 1)
            for t in range(TT):
                dve.wait_ge(stats_done, t + 1)
                nc.vector.bn_aggr(mv[:, t, :], stats[:, t, :]).then_inc(mv_done, 1)
            dve.wait_ge(std_done, 1)
            nc.vector.reciprocal(rstd[:], std[:]).then_inc(rstd_done, 1)
            dve.wait_ge(rstd_done, 1)
            for t in range(TT):
                nc.vector.tensor_scalar(normed[:, t, :], net.x[:, t, :], mv[:, t, 0:1], rstd[:, t:t + 1],
                                        ALU.subtract, ALU.mult).then_inc(norm_done, 1)
            for t in range(TT):
                dve.wait_ge(high_done, t + 1)
                nc.vector.tensor_tensor(tile(net.h_low, t), turned(t), tile(net.h_high, t).bitcast(F32), ALU.subtract)

        @block.scalar
        def _(act):
            act.wait_ge(mv_done, TT)
            nc.scalar.activation(std[:], mv[:, :, 1], ACT.Sqrt, bias=net.eps[:, 0:1]).then_inc(std_done, 1)
            for t in range(TT):
                act.wait_ge(turns_done, t + 1)
                nc.scalar.activation(tile(net.h_high, t), turned(t), ACT.Copy).then_inc(high_done, 1)

        @block.tensor
        def _(pe):
            for t in range(TT):
                pe.wait_ge(norm_done, t + 1)
                for k in range(KT):
                    last = nc.tensor.transpose(turn_ps[:, t, k * P:(k + 1) * P], normed[:, t, k * P:(k + 1) * P], net.ident[:])
                last.then_inc(turns_done, 1)


def project_queries(net, tag, rope, rotate_context):
    nc = net.nc
    w = {k: net.inp[f"{tag}_xattn_{k}"] for k in ("Wq", "w_kc_q", "w_kc_kv", "W_qr", "W_kr", "Wo")}
    src = {
        "wq": w["Wq"].rearrange("(a i k) d -> i k a d", a=2, i=HP),
        "wcq": w["w_kc_q"].rearrange("(a i) k q -> i k a q", a=2),
        "wckv": w["w_kc_kv"].rearrange("(a i) k c -> i k a c", a=2),
        "wkr": w["W_kr"].rearrange("(a i) c r -> i c a r", a=2),
    }
    src_wqr = [w["W_qr"].rearrange("(a i) (z p) r -> a i p z r", a=2, p=AQ)[a] for a in (0, 1)]
    src_wo = [w["Wo"].rearrange("(z o) (a i k) -> a i o z k", z=KT, a=2, i=HP)[a] for a in (0, 1)]
    NLOAD = 8
    with nc.cleanup_on_exit(), ExitStack() as ctx:
        sb, ps, sem = phase_tools(net, ctx, tag + "p")
        wq, wcq = sb("wq", [P, 2, 2, D]), sb("wcq", [P, 2, 2, CQ])
        wckv, wkr = sb("wckv", [P, 2, 2, DC]), sb("wkr", [DC, 2, 2, R])
        wqr, wo = sb("wqr", [AQ, 2, 2, 2, R]), sb("wo", [P, 2, 2, KT, HK])
        rT = sb("rT", [R, 512])
        woT = sb("woT", [P, 2, D])
        c_sb = sb("c_sb", [AQ, 2, 2, 2, DC])
        if rope:
            b_high, b_low = sb("b_high", [P, 2, 2, KT, CQ], F32R), sb("b_low", [P, 2, 2, KT, CQ], F32R)
            tab = sb("tab", [AQ, 4, CH])
            prod = sb("prod", [AQ, 2, 4, CH])
            y = sb("y", [AQ, 4, 2, CH])
        else:
            bt_sb = sb("bt_sb", [AQ, 2, 2, D])
            a_high, a_low = sb("a_high", [P, 2, KT, P], F32R), sb("a_low", [P, 2, KT, P], F32R)
        w_in = [sem("w_in0"), sem("w_in1")]
        tab_in = sem("tab_in")
        b_mm = sem("b_mm")
        rT_mm, wo_mm, c_mm, m_mm, a_mm = sem("rT_mm"), sem("wo_mm"), sem("c_mm"), sem("m_mm"), sem("a_mm")
        rT_out, wo_out = sem("rT_out"), sem("wo_out")
        c_out, m_out, b_out, a_out = sem("c_out"), sem("m_out"), sem("b_out"), sem("a_out")
        part_done = sem("part_done")
        waited = sem("waited")
        rotation = Rotation(net, ctx) if rotate_context else None
        big_mm = sem("big_mm")
        rope_done = sem("rope_done")
        y_done = sem("y_done")
        q_mm = sem("q_mm")
        high_done = sem("high_done")
        low_done = sem("low_done")

        def load(sp, i, par):
            for dst, name in ((wq, "wq"), (wcq, "wcq"), (wckv, "wckv"), (wkr, "wkr")):
                sp.dma_start(dst[:, par], src[name][i]).then_inc(w_in[par], 16)
            for a in (0, 1):
                sp.dma_start(wqr[:, par, a], src_wqr[a][i]).then_inc(w_in[par], 16)
                sp.dma_start(wo[:, par, a], src_wo[a][i]).then_inc(w_in[par], 16)

        def early(sp):
            load(sp, 0, 0)
            if rotation:
                rotation.early(sp)
            if rope:
                sp.dma_start(tab[:], net.inp["q_tab"]).then_inc(tab_in, 16)
            load(sp, 1, 1)

        layer_norm(net, tag + "n", early)
        ps_rT, ps_wo = ps("ps_rT", [P, 512]), ps("ps_wo", [P, 512])
        ps_b, ps_q = ps("ps_b", [P, 2, 512]), ps("ps_q", [P, 2, 512])
        if rope:
            ps_big = ps("ps_big", [P, 2, 512])
        if rotation:
            rotation.psum(ctx)
        block = ctx.enter_context(nc.Block())

        def over_pairs(eng, project):
            project(0, 0, 1, first=True)
            with eng.Fori(0, HP // 2 - 1) as it:
                project(2 * it + 1, 1, it + 2)
                project(2 * it + 2, 0, it + 2)
            project(HP - 1, 1, None)

        @block.sync
        def _(sp):
            def step(i, par, weights=True, context=True):
                if rotation:
                    for q in (0, 1):
                        rotation.store_rows(sp, 2 * i + q, q)
                if weights:
                    sp.wait_ge(b_mm, i + 3)
                    load(sp, i + 2, par)
                if rotation:
                    for q in (0, 1):
                        rotation.store_parts(sp, 2 * i + q, q)
                        if context:
                            rotation.load(sp, 2 * i + 4 + q, q)

            if rotation:
                rotation.load(sp, 2, 0)
                rotation.load(sp, 3, 1)
            with sp.Fori(0, HP // 2 - 1) as it:
                for par in (0, 1):
                    step(2 * it + par, par)
            if rotation:
                step(HP - 2, 0, weights=False, context=False)
                step(HP - 1, 1, weights=False, context=False)
                rotation.wait_stores(sp)

        @block.tensor
        def _(pe):
            def turn_weights(i, par, nth):
                pe.wait_ge(w_in[par], 16 * NLOAD * nth)
                pe.wait_ge(m_out, i + 1)
                for a in (0, 1):
                    for z in range(KT):
                        last = nc.tensor.transpose(ps_wo[:, a * D + z * P:a * D + (z + 1) * P], wo[:, par, a, z, :], net.ident[:])
                last.then_inc(wo_mm, 1)
                pe.wait_ge(c_out if rope else a_out, i + 1)
                pe.sem_inc(waited, 1)
                for a in (0, 1):
                    for z in (0, 1):
                        nc.tensor.transpose(ps_rT[0:R, (2 * a + z) * AQ:(2 * a + z + 1) * AQ], wqr[:, par, a, z, :],
                                            net.ident[0:AQ, 0:AQ])
                for a in (0, 1):
                    last = nc.tensor.transpose(ps_rT[0:R, 4 * AQ + a * DC:4 * AQ + (a + 1) * DC], wkr[:, par, a, :],
                                               net.ident[0:DC, 0:DC])
                last.then_inc(rT_mm, 1)

            def fold_weights(i, par):
                pe.wait_ge(rT_out, i + 1)
                for a in (0, 1):
                    for z in (0, 1):
                        last = nc.tensor.matmul(ps_rT[0:AQ, (2 * a + z) * DC:(2 * a + z + 1) * DC],
                                                rT[:, (2 * a + z) * AQ:(2 * a + z + 1) * AQ],
                                                rT[:, 4 * AQ + a * DC:4 * AQ + (a + 1) * DC], start=True, stop=True)
                last.then_inc(c_mm, 1)
                pe.wait_ge(wo_out, i + 1)
                for a in (0, 1):
                    last = nc.tensor.matmul(ps_wo[a * DC:(a + 1) * DC, 0:D], wckv[:, par, a, :], woT[:, a, :],
                                            start=True, stop=True)
                last.then_inc(m_mm, 1)
                pe.wait_ge(b_out, i + 1)
                for a in (0, 1):
                    for z in (0, 1):
                        if rope:
                            last = nc.tensor.matmul(ps_b[:, a, z * CQ:(z + 1) * CQ], wq[:, par, a, z * P:(z + 1) * P],
                                                    wcq[:, par, a, :], start=True, stop=True)
                        else:
                            last = nc.tensor.matmul(ps_b[0:AQ, a, z * D:(z + 1) * D], wcq[:, par, a, z * AQ:(z + 1) * AQ],
                                                    wq[:, par, a, :], start=True, stop=True)
                last.then_inc(b_mm, 1)

            def fold_all(i, par):
                pe.wait_ge(c_out, i + 2)
                pe.wait_ge(b_out, i + 2)
                for z in range(KT):
                    for a in (0, 1):
                        for q in (0, 1):
                            last = nc.tensor.matmul(ps_rT[:, (2 * z + a) * DC:(2 * z + a + 1) * DC],
                                                    bt_sb[:, a, q, z * P:(z + 1) * P], c_sb[:, par, a, q, :],
                                                    start=(q == 0), stop=(q == 1))
                last.then_inc(a_mm, 1)

            def big(i, par, u):
                c, a = u // 2, u % 2
                if u == 0:
                    pe.wait_ge(b_out, i + 2)
                    pe.wait_ge(c_out, i + 2)
                for z in (0, 1):
                    pe.wait_ge(rope_done, 2 * (4 * i + u) + z + 1)
                    for k in range(KT):
                        for n, (w, h) in enumerate(((b_high, net.h_high), (b_high, net.h_low), (b_low, net.h_high))):
                            last = nc.tensor.matmul(ps_big[0:AQ, z, 0:CH], w[:, par, a, k, z * AQ:(z + 1) * AQ],
                                                    h[:, k, c * CH:(c + 1) * CH], start=(k == 0 and n == 0),
                                                    stop=(k == KT - 1 and n == 2))
                    last.then_inc(big_mm, 1)

            def final(i, par, c):
                pe.wait_ge(y_done, 4 * i + 2 * c + 4)
                pe.wait_ge(low_done, 2 * i + c + 1)
                for z in (0, 1):
                    for a in (0, 1):
                        last = nc.tensor.matmul(ps_q[a * DC:(a + 1) * DC, c, 0:CH], c_sb[:, par, a, z, :],
                                                y[:, 2 * c + a, z, :], start=(z == 0), stop=(z == 1))
                last.then_inc(q_mm, 1)

            def direct(i, par, c):
                if c == 0:
                    pe.wait_ge(a_out, i + 2)
                pe.wait_ge(low_done, 2 * i + c + 1)
                for k in range(KT):
                    for n, (w, h) in enumerate(((a_high, net.h_high), (a_high, net.h_low), (a_low, net.h_high))):
                        last = nc.tensor.matmul(ps_q[:, c, 0:CH], w[:, par, k, :], h[:, k, c * CH:(c + 1) * CH],
                                                start=(k == 0 and n == 0), stop=(k == KT - 1 and n == 2))
                last.then_inc(q_mm, 1)

            def project(i, par, nth, first=False):
                more = nth is not None
                if rope:
                    big(i, par, 0)
                    if more:
                        turn_weights(i + 1, 1 - par, nth)
                    if not first:
                        final(i - 1, 1 - par, 1)
                    big(i, par, 1)
                    if more:
                        fold_weights(i + 1, 1 - par)
                    big(i, par, 2)
                    final(i, par, 0)
                    big(i, par, 3)
                    if not more:
                        final(i, par, 1)
                else:
                    if more:
                        turn_weights(i + 1, 1 - par, nth)
                    rotation.transpose(pe, i, 0)
                    direct(i, par, 0)
                    rotation.transpose(pe, i, 1)
                    if more:
                        fold_weights(i + 1, 1 - par)
                    rotation.transpose(pe, i, 2)
                    direct(i, par, 1)
                    rotation.transpose(pe, i, 3)
                    if more:
                        fold_all(i + 1, 1 - par)
                    rotation.transpose(pe, i, 4)
                    rotation.transpose(pe, i, 5)

            pe.sem_inc(b_mm, 2)
            pe.sem_inc(q_mm, 2)
            if rope:
                pe.wait_ge(tab_in, 16)
            turn_weights(0, 0, 1)
            fold_weights(0, 0)
            if not rope:
                fold_all(0, 0)
            if rotation:
                pe.sem_inc(rotation.turns_done, 6)
            over_pairs(pe, project)

        def place(i, a, c, rows):
            return net.q[rows, c * BC:(c + 1) * BC, bass.ds((i + HP * a) * S, S)]

        @block.scalar
        def _(act):
            def prep(i, par, n):
                if n == 0:
                    act.wait_ge(wo_mm, i + 1)
                    nc.scalar.activation(woT[:].rearrange("p a d -> p (a d)"), ps_wo[:], ACT.Copy).then_inc(wo_out, 1)
                if n == 1:
                    act.wait_ge(c_mm, i + 1)
                    nc.scalar.activation(c_sb[:, par].rearrange("p a z c -> p (a z c)"), ps_rT[0:AQ, 0:4 * DC],
                                         ACT.Copy).then_inc(c_out, 1)
                    act.wait_ge(m_mm, i + 1)
                    nc.scalar.activation(net.m[:, i, :], ps_wo[:, 0:D], ACT.Copy).then_inc(m_out, 1)
                    act.wait_ge(b_mm, i + 3)
                    if rope:
                        nc.scalar.activation(b_high[:, par].rearrange("p a k q -> p a (k q)"), ps_b[:, :, 0:KT * CQ],
                                             ACT.Copy).then_inc(part_done, 1)
                    else:
                        nc.scalar.activation(bt_sb[:].rearrange("p a z d -> p a (z d)"), ps_b[0:AQ], ACT.Copy).then_inc(b_out, 1)

                if n == 2 and not rope:
                    act.wait_ge(a_mm, i + 1)
                    nc.scalar.activation(a_high[:, par].rearrange("p k c -> p (k c)"), ps_rT[:, 0:KT * P], ACT.Copy).then_inc(part_done, 1)

            def high(i, c):
                act.wait_ge(q_mm, 2 * i + c + 3)
                for a in (0, 1):
                    last = nc.scalar.activation(place(i, a, c, slice(0, DC)),
                                                ps_q[a * DC:(a + 1) * DC, c, 0:CH].rearrange("p (b s) -> p b s", s=S), ACT.Copy)
                last.then_inc(high_done, 1)

            def project(i, par, nth, first=False):
                more = nth is not None
                if rope:
                    if more:
                        prep(i + 1, 1 - par, 0)
                    if not first:
                        high(i - 1, 1)
                    if more:
                        prep(i + 1, 1 - par, 1)
                    high(i, 0)
                    if not more:
                        high(i, 1)
                else:
                    if more:
                        prep(i + 1, 1 - par, 0)
                    rotation.take_high(act, i, 0)
                    high(i, 0)
                    rotation.take_high(act, i, 1)
                    if more:
                        prep(i + 1, 1 - par, 1)
                    rotation.take_high(act, i, 2)
                    high(i, 1)
                    rotation.take_high(act, i, 3)
                    if more:
                        prep(i + 1, 1 - par, 2)
                    rotation.take_high(act, i, 4)
                    rotation.take_high(act, i, 5)

            for s in (c_out, m_out, b_out):
                act.sem_inc(s, 1)
            prep(0, 0, 0)
            prep(0, 0, 1)
            prep(0, 0, 2)
            over_pairs(act, project)

        @block.vector
        def _(dve):
            def prep(i, par, n):
                if n == 0:
                    dve.wait_ge(rT_mm, i + 1)
                    nc.vector.tensor_copy(rT[:], ps_rT[0:R, :]).then_inc(rT_out, 1)
                if n == 2 and rope:
                    dve.wait_ge(part_done, i + 1)
                    nc.vector.tensor_tensor(b_low[:, par].rearrange("p a k q -> p a (k q)"), ps_b[:, :, 0:KT * CQ],
                                            b_high[:, par].rearrange("p a k q -> p a (k q)").bitcast(F32), ALU.subtract).then_inc(b_out, 1)
                if n == 2 and not rope:
                    dve.wait_ge(part_done, i + 1)
                    nc.vector.tensor_tensor(a_low[:, par].rearrange("p k c -> p (k c)"), ps_rT[:, 0:KT * P],
                                            a_high[:, par].rearrange("p k c -> p (k c)").bitcast(F32), ALU.subtract).then_inc(a_out, 1)

            def rotate(i, u):
                dve.wait_ge(y_done, 4 * i + u + 1)
                for z, uses in ((0, ((0, 0), (3, 3))), (1, ((1, 2), (2, 1)))):
                    dve.wait_ge(big_mm, 2 * (4 * i + u) + z + 1)
                    for n, table in uses:
                        last = nc.vector.tensor_tensor(prod[:, u % 2, n, :], ps_big[0:AQ, z, 0:CH], tab[:, table, :], ALU.mult)
                    last.then_inc(rope_done, 1)

            def low(i, c):
                dve.wait_ge(high_done, 2 * i + c + 1)
                for a in (0, 1):
                    last = nc.vector.tensor_tensor(place(i, a, c, slice(DC, P)),
                                                   ps_q[a * DC:(a + 1) * DC, c, 0:CH].rearrange("p (b s) -> p b s", s=S),
                                                   place(i, a, c, slice(0, DC)).bitcast(F32), ALU.subtract)
                last.then_inc(low_done, 1)

            def project(i, par, nth, first=False):
                more = nth is not None
                if rope:
                    rotate(i, 0)
                    if more:
                        prep(i + 1, 1 - par, 0)
                    rotate(i, 1)
                    if not first:
                        low(i - 1, 1)
                    rotate(i, 2)
                    if more:
                        prep(i + 1, 1 - par, 2)
                    rotate(i, 3)
                    low(i, 0)
                    if not more:
                        low(i, 1)
                else:
                    if more:
                        prep(i + 1, 1 - par, 0)
                    rotation.take_low(dve, i, 0)
                    low(i, 0)
                    rotation.take_low(dve, i, 1)
                    rotation.take_low(dve, i, 2)
                    if more:
                        rotation.rotate(dve, i + 1, 0)
                    low(i, 1)
                    rotation.take_low(dve, i, 3)
                    if more:
                        prep(i + 1, 1 - par, 2)
                    rotation.take_low(dve, i, 4)
                    rotation.take_low(dve, i, 5)
                    if more:
                        rotation.rotate(dve, i + 1, 1)

            dve.sem_inc(low_done, 2)
            dve.sem_inc(rope_done, 2)
            dve.sem_inc(a_out, 1)
            if rope:
                dve.wait_ge(tab_in, 16)
            prep(0, 0, 0)
            prep(0, 0, 2)
            if rotation:
                rotation.start_vector(dve)
                rotation.rotate(dve, 0, 0)
                rotation.rotate(dve, 0, 1)
            over_pairs(dve, project)

        @block.gpsimd
        def _(pool):
            if rotation:
                rotation.multiply_sin(pool)
            if not rope:
                return
            pool.sem_inc(y_done, 2)
            with pool.Fori(0, HP) as i:
                for u in range(4):
                    pool.wait_ge(rope_done, 2 * (4 * i + u) + 4)
                    pool.wait_ge(q_mm, 2 * i + u // 2 + 1)
                    nc.gpsimd.tensor_tensor(y[:, u, 0, :], prod[:, u % 2, 0, :], prod[:, u % 2, 1, :], ALU.add)
                    nc.gpsimd.tensor_tensor(y[:, u, 1, :], prod[:, u % 2, 2, :], prod[:, u % 2, 3, :],
                                            ALU.add).then_inc(y_done, 1)


def attend(net, tag):
    nc = net.nc
    with nc.cleanup_on_exit(), ExitStack() as ctx:
        sb, ps, sem = phase_tools(net, ctx, tag)
        k_all = [sb(f"k_all{i}", [P, L], F32R) for i in (0, 1)]
        k_low = [sb(f"k_low{i}", [DC + 1, L], F32R) for i in (0, 1)]
        kv = [sb(f"kv{i}", [KP, NK, DC]) for i in (0, 1)]
        q_all = [sb(f"q_all{i}", [P, NQ], F32R) for i in (0, 1)]
        q_max = [sb(f"q_max{i}", [DC + 1, NQ], F32R) for i in (0, 1)]
        part_max = sb("part_max", [P, TT, 3])
        neg_max = [sb(f"neg_max{i}", [P, TT], F32R) for i in (0, 1)]
        total = [sb(f"total{i}", [KP, NQ]) for i in (0, 1)]
        raw = [sb(f"raw{i}", [P, CH]) for i in (0, 1)]
        inv = sb("inv", [P, CH])
        prob = sb("prob", [KP, 4, NQ])
        ps_s = ps("ps_s", [P, 2, 2, 512])
        ps_max = ps("ps_max", [P, 3, 512])
        ps_v = ps("ps_v", [P, 512])
        max_in = [sem("max_in0"), sem("max_in1")]
        rest_in = [sem("rest_in0"), sem("rest_in1")]
        ones_set = sem("ones_set")
        score_mm = sem("score_mm")
        exp_done = sem("exp_done")
        pv_mm = sem("pv_mm")
        pool_added = sem("pool_added")
        dve_added = sem("dve_added")
        max_mm = sem("max_mm")
        max_done = sem("max_done")
        neg_done = sem("neg_done")
        row_mm = sem("row_mm")
        row_done = sem("row_done")
        total_mm = sem("total_mm")
        inv_done = sem("inv_done")
        raw_done = sem("raw_done")
        out_done = sem("out_done")
        block = ctx.enter_context(nc.Block())
        MAX_LOADS, REST_LOADS = 16 * 3, 16 * 3
        KD = 3
        KA = NK - KD
        PARTS_AFTER_SCORES = {4: 1, 5: 2, 6: 1, 7: 2, 8: 1, 9: 2, 10: 1, 11: 2}
        PARTS_AFTER_VALUES = {5: 3, 7: 3, 9: 3}

        @block.sync
        def _(sp):
            def load(b, par):
                sp.dma_start(k_all[par][0:DC].bitcast(F32), net.kv_high[b]).then_inc(max_in[par], 16)
                sp.dma_start(k_all[par][DC:P].bitcast(F32), net.kv_high[b]).then_inc(max_in[par], 16)
                sp.dma_start(q_all[par][:].bitcast(F32), net.q[:, b, :].bitcast(F32)).then_inc(max_in[par], 16)
                sp.dma_start(q_max[par][0:DC].bitcast(F32), net.q[0:DC, b, :].bitcast(F32)).then_inc(rest_in[par], 16)
                sp.dma_start(k_low[par][0:DC].bitcast(F32), net.kv_low[b]).then_inc(rest_in[par], 16)
                sp.dma_start(kv[par][:], net.kv_rows[b]).then_inc(rest_in[par], 16)

            load(0, 0)
            load(1, 1)
            with sp.Fori(0, B // 2 - 1) as it:
                for par in (0, 1):
                    b = 2 * it + 2 + par
                    sp.wait_ge(pv_mm, NK * (b - 1) + 4)
                    load(b, par)

        def over_batches(eng, batch):
            batch(0, 0, 1, True, first=True)
            with eng.Fori(0, B // 2 - 1) as it:
                batch(2 * it + 1, 1, it + 1, True)
                batch(2 * it + 2, 0, it + 2, True)
            batch(B - 1, 1, B // 2, False)

        @block.tensor
        def _(pe):
            def max_part(b, par, n):
                j, c = n // 3, n % 3
                pe.wait_ge(max_done, 3 * TT * b + n + 1)
                nc.tensor.matmul(ps_max[:, c, 0:MC], q_all[par][:, j * P:(j + 1) * P],
                                 k_all[par][:, c * MC:(c + 1) * MC], start=True, stop=True).then_inc(max_mm, 1)

            def max_row(b, par):
                pe.wait_ge(neg_done, b + 2)
                for j in range(TT):
                    last = nc.tensor.matmul(ps_max[0:1, j // 4, (j % 4) * P:(j % 4 + 1) * P], neg_max[par][:, j:j + 1],
                                            net.ident_r[:], start=True, stop=True)
                last.then_inc(row_mm, 1)

            def scores(b, par, t):
                pe.wait_ge(exp_done, NK * b + t + 1)
                for c in (0, 1):
                    nc.tensor.matmul(ps_s[0:KP, t % 2, c, 0:CH], k_all[par][:, t * KP:(t + 1) * KP],
                                     q_all[par][:, c * CH:(c + 1) * CH], start=True, stop=False)
                for c in (0, 1):
                    last = nc.tensor.matmul(ps_s[0:KP, t % 2, c, 0:CH], k_low[par][:, t * KP:(t + 1) * KP],
                                            q_max[par][:, c * CH:(c + 1) * CH], start=False, stop=True)
                last.then_inc(score_mm, 1)

            def values(b, par, t):
                pe.wait_ge(exp_done, NK * b + t + 3)
                if t == 0:
                    pe.wait_ge(raw_done, b + 1)
                for c in (0, 1):
                    last = nc.tensor.matmul(ps_v[c * DC:(c + 1) * DC, 0:CH], kv[par][:, t, :], prob[:, t % 4, c * CH:(c + 1) * CH],
                                            start=(t == 0), stop=(t == NK - 1))
                last.then_inc(pv_mm, 1)

            def totals(b, par):
                pe.wait_ge(dve_added, KD * b + KD + 3)
                for c in (0, 1):
                    last = nc.tensor.matmul(ps_max[c * DC:(c + 1) * DC, 2, 0:CH], net.ones[0:KP, 0:DC],
                                            total[par][:, c * CH:(c + 1) * CH], start=True, stop=True)
                last.then_inc(total_mm, 1)

            def batch(b, par, nth, more, first=False):
                pe.wait_ge(rest_in[par], REST_LOADS * nth)
                pe.wait_ge(row_done, b + 1)
                done = 0
                for t in range(NK):
                    scores(b, par, t)
                    if t == 1 and not first:
                        totals(b - 1, 1 - par)
                    if more and t == 4:
                        pe.wait_ge(max_in[1 - par], MAX_LOADS * (nth + par))
                        pe.wait_ge(inv_done, b + 1)
                    for n in range(done, done + PARTS_AFTER_SCORES.get(t, 0) if more else 0):
                        max_part(b + 1, 1 - par, n)
                        done += 1
                    if t % 2 and 3 <= t < NK - 1:
                        values(b, par, t - 3)
                        values(b, par, t - 2)
                    for n in range(done, done + PARTS_AFTER_VALUES.get(t, 0) if more else 0):
                        max_part(b + 1, 1 - par, n)
                        done += 1
                assert done == (3 * TT if more else 0)
                values(b, par, NK - 4)
                values(b, par, NK - 3)
                if more:
                    max_row(b + 1, 1 - par)
                values(b, par, NK - 2)
                values(b, par, NK - 1)
                if not more:
                    totals(b, par)

            pe.sem_inc(pv_mm, 4)
            pe.sem_inc(total_mm, 2)
            pe.wait_ge(ones_set, 2)
            pe.wait_ge(max_in[0], MAX_LOADS)
            for n in range(3 * TT):
                max_part(0, 0, n)
            max_row(0, 0)
            over_batches(pe, batch)

        @block.scalar
        def _(act):
            def row(b, par):
                act.wait_ge(row_mm, b + 1)
                nc.scalar.activation(q_max[par][DC:DC + 1, :], ps_max[0:1].rearrange("p a k -> p (a k)")[:, 0:NQ],
                                     ACT.Copy).then_inc(row_done, 1)

            def batch(b, par, nth, more, first=False):
                for t in range(NK):
                    act.wait_ge(score_mm, NK * b + t + 1)
                    act.wait_ge(pv_mm, NK * b + t + 1)
                    if 1 <= t <= KD:
                        act.wait_ge(dve_added, KD * b + t)
                    else:
                        act.wait_ge(pool_added, KA * b + max(t - 3, 0) + 1)
                    nc.scalar.activation(prob[:, t % 4, :].rearrange("p (c q) -> p c q", c=2), ps_s[0:KP, t % 2, :, 0:CH],
                                         ACT.Exp).then_inc(exp_done, 1)
                if more:
                    row(b + 1, 1 - par)
                act.wait_ge(pv_mm, NK * b + NK + 4)
                act.wait_ge(out_done, b + 1)
                nc.scalar.activation(raw[par][:], ps_v[:, 0:CH], ACT.Copy).then_inc(raw_done, 1)

            act.sem_inc(exp_done, 2)
            act.sem_inc(raw_done, 1)
            row(0, 0)
            over_batches(act, batch)

        @block.vector
        def _(dve):
            def maxima(b, par):
                for n in range(TT * 3):
                    dve.wait_ge(max_mm, 3 * TT * b + n + 1)
                    if n == 0:
                        dve.wait_ge(neg_done, b + 1)
                    nc.vector.tensor_reduce(part_max[:, n // 3, n % 3:n % 3 + 1], ps_max[:, n % 3, 0:MC], AX.X,
                                            ALU.max).then_inc(max_done, 1)
                dve.wait_ge(max_done, 3 * TT * (b + 1) + 3)
                nc.vector.tensor_reduce(neg_max[par][:], part_max[:], AX.X, ALU.max, negate=True).then_inc(neg_done, 1)

            def divide(b, par):
                dve.wait_ge(total_mm, b + 3)
                dve.wait_ge(out_done, b + 2)
                nc.vector.reciprocal(inv[:], ps_max[:, 2, 0:CH]).then_inc(inv_done, 1)
                dve.wait_ge(inv_done, b + 2)
                dve.wait_ge(raw_done, b + 2)
                nc.vector.tensor_tensor(net.cT[:, :, bass.ds(b * S, S)], raw[par][:].rearrange("p (h s) -> p h s", s=S),
                                        inv[:].rearrange("p (h s) -> p h s", s=S), ALU.mult).then_inc(out_done, 1)

            def batch(b, par, nth, more, first=False):
                if not first:
                    divide(b - 1, 1 - par)
                if more:
                    maxima(b + 1, 1 - par)
                for k in range(KD):
                    if k == 0:
                        dve.wait_ge(pool_added, KA * b + KA + 1)
                    else:
                        dve.wait_ge(dve_added, KD * b + k + 3)
                    dve.wait_ge(exp_done, NK * b + KA + k + 3)
                    nc.vector.tensor_tensor(total[par][:], total[par][:], prob[:, (KA + k) % 4, :], ALU.add).then_inc(dve_added, 1)
                if not more:
                    divide(b, par)

            dve.sem_inc(max_done, 3)
            dve.sem_inc(neg_done, 1)
            dve.sem_inc(dve_added, 3)
            dve.sem_inc(inv_done, 1)
            dve.sem_inc(out_done, 2)
            maxima(0, 0)
            over_batches(dve, batch)

        @block.gpsimd
        def _(pool):
            def batch(b, par, nth, more, first=False):
                pool.wait_ge(total_mm, b + 1)
                for t in range(1, KA):
                    pool.wait_ge(exp_done, NK * b + t + 3)
                    if t > 1:
                        pool.wait_ge(pool_added, KA * b + t + 1)
                    nc.gpsimd.tensor_tensor(total[par][:], prob[:, 0, :] if t == 1 else total[par][:], prob[:, t % 4, :],
                                            ALU.add).then_inc(pool_added, 2 if t == 1 else 1)

            nc.gpsimd.memset(k_low[0][DC:DC + 1, :].bitcast(F32), 1.0).then_inc(ones_set, 1)
            nc.gpsimd.memset(k_low[1][DC:DC + 1, :].bitcast(F32), 1.0).then_inc(ones_set, 1)
            pool.sem_inc(pool_added, 1)
            over_batches(pool, batch)


def add_attention(net, tag, whole, split, early):
    nc = net.nc
    with nc.cleanup_on_exit(), ExitStack() as ctx:
        sb, ps, sem = phase_tools(net, ctx, tag + "o")
        stats, mv = sb("stats", [P, TT, 6]), sb("mv", [P, TT, 2])
        std, rstd = sb("std", [P, TT]), sb("rstd", [P, TT])
        normed = sb("normed", [P, TT, D])
        ps_o, turn_ps = ps("ps_o", [P, 4, 512]), ps("turn_ps", [P, 4, 512])
        o_mm, x_done, stats_done, mv_done = sem("o_mm"), sem("x_done"), sem("stats_done"), sem("mv_done")
        std_done, rstd_done, norm_done = sem("std_done"), sem("rstd_done"), sem("norm_done")
        turns_done, high_done = sem("turns_done"), sem("high_done")
        taken = sem("taken")
        block = ctx.enter_context(nc.Block())

        def tile(h, t):
            return h[:, :, t * P:(t + 1) * P]

        def turned(t):
            return turn_ps[:, t % 4, 0:D].rearrange("p (k c) -> p k c", k=KT)

        @block.sync
        def _(sp):
            early(sp)

        @block.tensor
        def _(pe):
            def transpose(t):
                pe.wait_ge(norm_done, t + 1)
                if t >= 4:
                    pe.wait_ge(taken, t - 3)
                for k in range(KT):
                    last = nc.tensor.transpose(turn_ps[:, t % 4, k * P:(k + 1) * P], normed[:, t, k * P:(k + 1) * P], net.ident[:])
                last.then_inc(turns_done, 1)

            for t in range(TT):
                if t >= 4:
                    pe.wait_ge(x_done, t - 3)
                for j in range(HP):
                    last = nc.tensor.matmul(ps_o[:, t % 4, 0:D], net.cT[:, j, t * P:(t + 1) * P], net.m[:, j, :],
                                            start=(j == 0), stop=(j == HP - 1))
                last.then_inc(o_mm, 1)
                if t:
                    transpose(t - 1)
            transpose(TT - 1)

        @block.vector
        def _(dve):
            def low(t):
                if split:
                    dve.wait_ge(high_done, t + 1)
                    nc.vector.tensor_tensor(tile(net.h_low, t), turned(t), tile(net.h_high, t).bitcast(F32),
                                            ALU.subtract).then_inc(taken, 1)

            for t in range(TT):
                dve.wait_ge(o_mm, t + 1)
                nc.vector.tensor_tensor(net.x[:, t, :], ps_o[:, t % 4, 0:D], net.x[:, t, :], ALU.add).then_inc(x_done, 1)
                dve.wait_ge(x_done, t + 1)
                nc.vector.bn_stats(stats[:, t, :], net.x[:, t, :]).then_inc(stats_done, 1)
                dve.wait_ge(stats_done, t + 1)
                nc.vector.bn_aggr(mv[:, t, :], stats[:, t, :]).then_inc(mv_done, 1)
                dve.wait_ge(std_done, t + 1)
                nc.vector.reciprocal(rstd[:, t:t + 1], std[:, t:t + 1]).then_inc(rstd_done, 1)
                dve.wait_ge(rstd_done, t + 1)
                nc.vector.tensor_scalar(normed[:, t, :], net.x[:, t, :], mv[:, t, 0:1], rstd[:, t:t + 1],
                                        ALU.subtract, ALU.mult).then_inc(norm_done, 1)
                if t:
                    low(t - 1)
            low(TT - 1)

        @block.scalar
        def _(act):
            def copy(t):
                act.wait_ge(turns_done, t + 1)
                if whole:
                    last = nc.scalar.activation(tile(net.hT, t), turned(t), ACT.Copy)
                if split:
                    nc.scalar.activation(tile(net.h_high, t), turned(t), ACT.Copy).then_inc(high_done, 1)
                else:
                    last.then_inc(taken, 1)

            for t in range(TT):
                act.wait_ge(mv_done, t + 1)
                nc.scalar.activation(std[:, t:t + 1], mv[:, t, 1:2], ACT.Sqrt, bias=net.eps[:, 0:1]).then_inc(std_done, 1)
                if t:
                    copy(t - 1)
            copy(TT - 1)


def route(net, tag, n, top_k, w_name, bias_name, turn, early, stored):
    nc = net.nc
    blocks = turn
    with nc.cleanup_on_exit(), ExitStack() as ctx:
        sb, ps, sem = phase_tools(net, ctx, tag + "r")
        w, bias, ids = sb("w", [P, KT, n]), sb("bias", [P, n]), sb("ids", [P, n])
        w_raw = sb("w_raw", [n, D])
        rank = sb("rank", [P, TT, n])
        top, idx, idx_f = sb("top", [P, TT, 8]), sb("idx", [P, TT, 8], U32), sb("idx_f", [P, TT, 8])
        hit, mask = sb("hit", [P, TT, top_k, n]), sb("mask", [P, TT, n])
        biased, peak, gap, e = sb("biased", [P, TT, n]), sb("peak", [P, TT]), sb("gap", [P, TT, n]), sb("e", [P, TT, n])
        chosen, total, inv, gate = sb("chosen", [P, TT, n]), sb("total", [P, TT]), sb("inv", [P, TT]), sb("gate", [P, TT, n])
        gate_t, one_rows = sb("gate_t", [n, NT]), sb("one_rows", [2, NT])
        w_in, turned, turn_out = sem("w_in"), sem("turned"), sem("turn_out")
        l_mm, gap_done, exp_done, gate_done = sem("l_mm"), sem("gap_done"), sem("exp_done"), sem("gate_done")
        t_mm, t_out, ones_set = sem("t_mm"), sem("t_out"), sem("ones_set")
        step = sem("step")

        def load(sp):
            if turn:
                sp.dma_start(w_raw[:], net.inp[w_name]).then_inc(w_in, 16)
            else:
                sp.dma_start(w[:], net.inp[w_name].rearrange("(k p) e -> p k e", p=P)).then_inc(w_in, 16)
            sp.dma_start(bias[:], net.inp[bias_name].partition_broadcast(P)).then_inc(w_in, 16)
            sp.dma_start(ids[:], net.inp["expert_ids"][0:n].partition_broadcast(P)).then_inc(w_in, 16)

        add_attention(net, tag, whole=True, split=True, early=load)
        ps_l, ps_t, ps_w = ps("ps_l", [P, 512]), ps("ps_t", [P, 2, 512]), ps("ps_w", [P, 512])
        logits = ps_l[:, 0:TT * n].rearrange("p (t e) -> p t e", e=n)
        block = ctx.enter_context(nc.Block())

        def wide(ap):
            return ap.unsqueeze(2).to_broadcast([P, TT, n])

        @block.sync
        def _(sp):
            early(sp)
            sp.wait_ge(t_out, 1)
            sp.dma_start(net.gates[0:n, :], gate_t[:]).then_inc(stored, 16)
            sp.wait_ge(ones_set, 1)
            sp.dma_start(net.gates[E0:E0 + 2, :], one_rows[:]).then_inc(stored, 16)

        @block.gpsimd
        def _(pool):
            nc.gpsimd.memset(one_rows[:], 1.0).then_inc(ones_set, 1)

        @block.tensor
        def _(pe):
            pe.wait_ge(w_in, 48)
            if turn:
                for k in range(KT):
                    last = nc.tensor.transpose(ps_w[:, k * n:(k + 1) * n], w_raw[:, k * P:(k + 1) * P], net.ident[0:n, 0:n])
                last.then_inc(turned, 1)
                pe.wait_ge(turn_out, 1)
            for t in range(TT):
                for k in range(KT):
                    last = nc.tensor.matmul(ps_l[:, t * n:(t + 1) * n], net.hT[:, k, t * P:(t + 1) * P], w[:, k, :],
                                            start=(k == 0), stop=(k == KT - 1))
            last.then_inc(l_mm, 1)
            pe.wait_ge(gate_done, 1)
            for t in range(TT):
                last = nc.tensor.transpose(ps_t[0:n, t // 4, (t % 4) * P:(t % 4 + 1) * P], gate[:, t, :], net.ident[:])
            last.then_inc(t_mm, 1)

        @block.scalar
        def _(act):
            if turn:
                act.wait_ge(turned, 1)
                nc.scalar.activation(w[:].rearrange("p k e -> p (k e)"), ps_w[:, 0:KT * n], ACT.Copy).then_inc(turn_out, 1)
            act.wait_ge(gap_done, 1)
            nc.scalar.activation(e[:], gap[:], ACT.Exp).then_inc(exp_done, 1)
            act.wait_ge(t_mm, 1)
            nc.scalar.activation(gate_t[:], ps_t[0:n].rearrange("p a k -> p (a k)")[:, 0:NT], ACT.Copy).then_inc(t_out, 1)

        @block.vector
        def _(dve):
            count = [0]

            def done(ins):
                count[0] += 1
                ins.then_inc(step, 1)
                dve.wait_ge(step, count[0])

            def exponentials(values):
                done(nc.vector.tensor_reduce(peak[:], values, AX.X, ALU.max))
                nc.vector.tensor_tensor(gap[:], values, wide(peak[:]), ALU.subtract).then_inc(gap_done, 1)
                dve.wait_ge(exp_done, 1)

            def normalise(out, values):
                done(nc.vector.tensor_reduce(total[:], values, AX.X, ALU.add))
                done(nc.vector.reciprocal(inv[:], total[:]))
                return nc.vector.tensor_tensor(out, values, wide(inv[:]), ALU.mult)

            dve.wait_ge(l_mm, 1)
            by_bias = bias[:].unsqueeze(1).to_broadcast([P, TT, n])
            if blocks:
                done(nc.vector.tensor_tensor(biased[:], logits, by_bias, ALU.add))
                exponentials(biased[:])
                done(normalise(rank[:], e[:]))
            else:
                done(nc.vector.tensor_tensor(rank[:], logits, by_bias, ALU.add))
            for t in range(TT):
                done(nc.vector.max(top[:, t, :], rank[:, t, :]))
                done(nc.vector.max_index(idx[:, t, :], top[:, t, :], rank[:, t, :]))
            done(nc.vector.tensor_copy(idx_f[:], idx[:]))
            for t in range(TT):
                ins = nc.vector.tensor_tensor(hit[:, t], ids[:].unsqueeze(1).to_broadcast([P, top_k, n]),
                                              idx_f[:, t, 0:top_k].unsqueeze(2).to_broadcast([P, top_k, n]), ALU.is_equal)
            done(ins)
            if blocks:
                nc.vector.tensor_reduce(gate[:], hit[:].rearrange("p t k e -> p t e k"), AX.X, ALU.add).then_inc(gate_done, 1)
            else:
                done(nc.vector.tensor_reduce(mask[:], hit[:].rearrange("p t k e -> p t e k"), AX.X, ALU.add))
                exponentials(logits)
                done(nc.vector.tensor_tensor(chosen[:], e[:], mask[:], ALU.mult))
                normalise(gate[:], chosen[:]).then_inc(gate_done, 1)


def run_experts(net, tag, tiles, load, up, func, router, stores, ahead, turn=False, bias1=False, before=None, first=None):
    nc = net.nc
    NU = 1 + up
    NW = 4
    W1 = NU * KT * P
    with nc.cleanup_on_exit(), ExitStack() as ctx:
        sb, ps, sem = phase_tools(net, ctx, tag + "f")
        raw = sb("raw", [P, NW, W1 + D])
        high, low = sb("high", [P, NW, W1 + D], F32R), sb("low", [P, NW, W1 + D], F32R)
        gate = sb("gate", [P, NW, NT])
        b1 = sb("b1", [P, NW, 1])
        act_out = sb("act_out", [P, 2, CH])
        prod = sb("prod", [P, 2, CH])
        hid = sb("hid", [P, 2, CH])
        hid_high, hid_low = sb("hid_high", [P, 2, NT], F32R), sb("hid_low", [P, 2, NT], F32R)
        zero = sb("zero", [P, 512], F32R)
        loaded = [sem(f"loaded{u}") for u in range(NW)]
        stored = sem("stored")
        zero_set = sem("zero_set")
        turned = sem("turned")
        w_high_done, w_low_done = sem("w_high_done"), sem("w_low_done")
        h_mm = sem("h_mm")
        act_done = sem("act_done")
        prod_done = sem("prod_done")
        hid_done = sem("hid_done")
        hid_high_done = sem("hid_high_done")
        hid_low_done = sem("hid_low_done")
        y_mm = sem("y_mm")

        def w1_of(t):
            return t[:, :, 0:W1].rearrange("p u (n k f) -> p u n k f", n=NU, k=KT)

        def w2_of(t):
            return t[:, :, W1:W1 + D]

        bufs = {"w1": raw[:, :, 0:W1].rearrange("p u (k f) -> p u k f", k=KT) if turn else w1_of(raw),
                "w2": w2_of(raw), "gate": gate, "b1": b1}
        counts = set()

        def start(sp, part, in_part, u, weights=True, gates=True):
            moves = load(part, in_part, u, bufs)
            counts.add(len(moves[0]) + len(moves[1]))
            for dst, src in (moves[0] if weights else []) + (moves[1] if gates else []):
                sp.dma_start(dst, src).then_inc(loaded[u], 16)

        def early(sp):
            if before:
                before(sp)
            for u in range(ahead):
                start(sp, 0, u, u, gates=False)

        router(early, stored)
        ps_y = ps("ps_y", [P, 4, 512])
        ps_h = ps("ps_h", [P, 2 * NU, 512])
        if turn:
            ps_w = ps("ps_w", [P, 512])
        block = ctx.enter_context(nc.Block())

        def y_at(t):
            return ps_y[:, t // 2, (t % 2) * D:(t % 2 + 1) * D]

        @block.sync
        def _(sp):
            if before:
                before(sp)
            sp.wait_ge(stored, stores)
            for u in range(NW):
                start(sp, 0, u, u, weights=(u >= ahead))
            at = 0
            for part, n in enumerate(tiles):
                if n > NW:
                    with sp.Fori(0, n // NW - (part == 0)) as it:
                        for u in range(NW):
                            in_part = NW * it + u + (NW if part == 0 else 0)
                            sp.wait_ge(y_mm, at + in_part + 1)
                            start(sp, part, in_part, u)
                else:
                    for u in range(NW):
                        sp.wait_ge(y_mm, at + u + 1)
                        start(sp, part, u, u)
                at += n

        N = sum(tiles)
        assert len(counts) == 1 and all(n % NW == 0 for n in tiles) and tiles[0] > NW
        LOADS = 16 * counts.pop()

        def over_tiles(eng, weights, work):
            weights(0, 0, 0)
            with eng.Fori(0, N // NW - 1) as it:
                for u in range(NW):
                    weights(NW * it + u + 1, (u + 1) % NW, it + (u + 1) // NW)
                    work(NW * it + u, u, it)
            for u in range(NW):
                if u + 1 < NW:
                    weights(N - NW + u + 1, u + 1, N // NW - 1)
                work(N - NW + u, u, N // NW - 1)

        @block.tensor
        def _(pe):
            def weights(m, u, it):
                if not turn:
                    return
                pe.wait_ge(loaded[u], LOADS * it + LOADS)
                if not isinstance(m, int) or m:
                    pe.wait_ge(w_low_done, m)
                for k in range(KT):
                    nc.tensor.transpose(ps_w[:, k * P:(k + 1) * P], raw[:, u, k * P:(k + 1) * P], net.ident[:])
                for z in range(KT):
                    last = nc.tensor.transpose(ps_w[:, (KT + z) * P:(KT + z + 1) * P], raw[:, u, W1 + z * P:W1 + (z + 1) * P],
                                               net.ident[:])
                last.then_inc(turned, 1)

            def hidden(m, u):
                pe.wait_ge(w_low_done, m + 1)
                for c in (0, 1):
                    pe.wait_ge(act_done, 2 * m + c + 1)
                    if up:
                        pe.wait_ge(prod_done, 2 * m + c + 1)
                    for n in range(NU):
                        for k in range(KT):
                            for j, (w, h) in enumerate(((high, net.h_high), (high, net.h_low), (low, net.h_high))):
                                last = nc.tensor.matmul(ps_h[:, NU * c + n, 0:CH], w1_of(w)[:, u, n, k, :],
                                                        h[:, k, c * CH:(c + 1) * CH], start=(k == 0 and j == 0),
                                                        stop=(k == KT - 1 and j == 2))
                    last.then_inc(h_mm, 1)

            def output(m, u):
                pe.wait_ge(hid_low_done, 2 * m + 4)
                for t in range(TT):
                    for w, h in ((high, hid_high), (high, hid_low), (low, hid_high)):
                        last = nc.tensor.matmul(y_at(t), h[:, u % 2, t * P:(t + 1) * P], w2_of(w)[:, u, :],
                                                start=False, stop=False, skip_group_check=True)
                last.then_inc(y_mm, 1)

            pe.sem_inc(y_mm, NW)
            pe.wait_ge(zero_set, 1)
            for a in range(4):
                nc.tensor.matmul(ps_y[:, a, :], zero[:, 0:P], zero[:], start=True, stop=False, skip_group_check=True)
            if first:
                first(pe, y_at)
            weights(0, 0, 0)
            weights(1, 1, 0)
            hidden(0, 0)
            with pe.Fori(0, N // NW - 1) as it:
                for u in range(NW):
                    weights(NW * it + u + 2, (u + 2) % NW, it + (u + 2) // NW)
                    hidden(NW * it + u + 1, (u + 1) % NW)
                    output(NW * it + u, u)
            for m in range(N - NW, N):
                if m + 2 < N:
                    weights(m + 2, (m + 2) % NW, (m + 2) // NW)
                if m + 1 < N:
                    hidden(m + 1, (m + 1) % NW)
                output(m, m % NW)

        @block.scalar
        def _(act):
            def weights(m, u, it):
                if turn:
                    act.wait_ge(turned, m + 1)
                    nc.scalar.activation(high[:, u], ps_w[:], ACT.Copy).then_inc(w_high_done, 1)
                else:
                    act.wait_ge(loaded[u], LOADS * it + LOADS)
                    nc.scalar.activation(high[:, u], raw[:, u], ACT.Copy).then_inc(w_high_done, 1)

            def work(m, u, it):
                for c in (0, 1):
                    act.wait_ge(h_mm, 2 * m + c + 1)
                    act.wait_ge(prod_done if up else hid_done, 2 * m + c + 1)
                    if bias1:
                        ins = nc.scalar.activation(act_out[:, c], ps_h[:, NU * c, 0:CH], func, bias=b1[:, u, :])
                    else:
                        ins = nc.scalar.activation(act_out[:, c], ps_h[:, NU * c, 0:CH], func)
                    ins.then_inc(act_done, 1)
                act.wait_ge(y_mm, m + NW - 1)
                for c in (0, 1):
                    act.wait_ge(hid_done, 2 * m + c + 3)
                    nc.scalar.activation(hid_high[:, u % 2, c * CH:(c + 1) * CH], hid[:, c], ACT.Copy).then_inc(hid_high_done, 1)

            act.sem_inc(act_done, 2)
            over_tiles(act, weights, work)

        @block.vector
        def _(dve):
            def weights(m, u, it):
                dve.wait_ge(w_high_done, m + 1)
                nc.vector.tensor_tensor(low[:, u], ps_w[:] if turn else raw[:, u], high[:, u].bitcast(F32),
                                        ALU.subtract).then_inc(w_low_done, 1)

            def work(m, u, it):
                for c in (0, 1):
                    if up:
                        dve.wait_ge(act_done, 2 * m + c + 3)
                        dve.wait_ge(hid_done, 2 * m + c + 1)
                        nc.vector.tensor_tensor(prod[:, c], ps_h[:, NU * c + 1, 0:CH], act_out[:, c], ALU.mult).then_inc(prod_done, 1)
                for c in (0, 1):
                    dve.wait_ge(hid_high_done, 2 * m + c + 1)
                    nc.vector.tensor_tensor(hid_low[:, u % 2, c * CH:(c + 1) * CH], hid[:, c],
                                            hid_high[:, u % 2, c * CH:(c + 1) * CH].bitcast(F32), ALU.subtract).then_inc(hid_low_done, 1)

            nc.vector.memset(zero[:].bitcast(F32), 0.0).then_inc(zero_set, 1)
            dve.sem_inc(prod_done, 2)
            dve.sem_inc(hid_low_done, 2)
            over_tiles(dve, weights, work)
            dve.wait_ge(y_mm, N + NW)
            for t in range(TT):
                nc.vector.tensor_tensor(net.x[:, t, :], y_at(t), net.x[:, t, :], ALU.add)

        @block.gpsimd
        def _(pool):
            pool.sem_inc(hid_done, 2)
            with pool.Fori(0, N // NW) as it:
                for u in range(NW):
                    m = NW * it + u
                    pool.wait_ge(loaded[u], LOADS * it + LOADS)
                    for c in (0, 1):
                        pool.wait_ge(prod_done if up else act_done, 2 * m + c + 3)
                        pool.wait_ge(hid_low_done, 2 * m + c + 1)
                        nc.gpsimd.tensor_tensor(hid[:, c], prod[:, c] if up else act_out[:, c],
                                                gate[:, u, c * CH:(c + 1) * CH], ALU.mult).then_inc(hid_done, 1)


def experts_0(net):
    def load(part, m, u, bufs):
        moves = []
        for n, name in enumerate(("wg", "wu")):
            for k in range(KT):
                if part == 0:
                    src = net.inp["L0_ffn_" + name].rearrange("(m e) (k p) f -> m k p e f", e=2, p=P)[m, k]
                else:
                    src = net.inp["L0_ffn_s" + name].rearrange("s (k p) (j f) -> s j k p f", p=P, f=P)[u // 2, u % 2, k]
                dst = bufs["w1"][:, u, n, k, :]
                moves.append((dst.rearrange("p (e f) -> p e f", e=2) if part == 0 else dst, src))
        if part == 0:
            moves.append((bufs["w2"][:, u], net.inp["L0_ffn_wd"].rearrange("(m e) f d -> m (e f) d", e=2)[m]))
            rows = net.gates[0:E0].rearrange("(m e) n -> m e n", e=2)[m]
        else:
            moves.append((bufs["w2"][:, u], net.inp["L0_ffn_swd"].rearrange("s (j f) d -> (s j) f d", f=P)[m]))
            rows = net.gates[E0:E0 + 2]
        return moves, [(bufs["gate"][e * F0:(e + 1) * F0, u, :], rows[e].partition_broadcast(F0)) for e in (0, 1)]

    def router(early, stored):
        route(net, "L0", E0, TOP0, "L0_ffn_router_w", "L0_ffn_router_bias", False, early, stored)

    run_experts(net, "L0", (E0 * F0 // P, 4), load, True, ACT.Silu, router, 32, 4)


def ternary_layer(net):
    nc = net.nc
    with nc.cleanup_on_exit(), ExitStack() as ctx:
        sb, ps, sem = phase_tools(net, ctx, "L1f")
        w, bias = sb("w", [P, KT, D]), sb("bias", [P, D])
        part, scale, inv = sb("part", [P, 1]), sb("scale", [P, 2]), sb("inv", [P, 1])
        r, up_, down, tern, diff = sb("r", [P, KT, D]), sb("up", [P, KT, D]), sb("down", [P, KT, D]), sb("tern", [P, KT, D]), sb("diff", [P, KT, D])
        ste, wT = sb("ste", [P, KT, D]), sb("wT", [P, KT, D])
        xb = sb("xb", [P, TT, D])
        w_in, part_done, s_mm, ste_done, t_mm, t_out, y_mm = (
            sem("w_in"), sem("part_done"), sem("s_mm"), sem("ste_done"), sem("t_mm"), sem("t_out"), sem("y_mm"))
        step = sem("step")

        def early(sp):
            sp.dma_start(w[:], net.inp["L1_ffn_weight"].rearrange("(z p) d -> p z d", p=P)).then_inc(w_in, 16)
            sp.dma_start(bias[:], net.inp["L1_ffn_bias"].partition_broadcast(P)).then_inc(w_in, 16)

        add_attention(net, "L1", whole=True, split=False, early=early)
        ps_s, ps_w, ps_y = ps("ps_s", [P, 512]), ps("ps_w", [P, 512]), ps("ps_y", [P, 4, 512])
        block = ctx.enter_context(nc.Block())

        @block.vector
        def _(dve):
            n = [0]

            def done(ins):
                n[0] += 1
                ins.then_inc(step, 1)
                dve.wait_ge(step, n[0])

            dve.wait_ge(w_in, 32)
            nc.vector.tensor_reduce(part[:], w[:], AX.XY, ALU.add, apply_absolute_value=True).then_inc(part_done, 1)
            dve.wait_ge(s_mm, 1)
            done(nc.vector.tensor_scalar(scale[:, 0:1], ps_s[:, 0:1], 1.0 / (D * D), None, ALU.mult))
            done(nc.vector.tensor_scalar(scale[:, 1:2], scale[:, 0:1], 1e-10, None, ALU.add))
            done(nc.vector.reciprocal(inv[:], scale[:, 1:2]))
            done(nc.vector.tensor_scalar(r[:], w[:], inv[:, 0:1], None, ALU.mult))
            done(nc.vector.tensor_scalar(up_[:], r[:], 0.5, None, ALU.is_gt))
            done(nc.vector.tensor_scalar(down[:], r[:], -0.5, None, ALU.is_lt))
            done(nc.vector.tensor_tensor(tern[:], up_[:], down[:], ALU.subtract))
            done(nc.vector.scalar_tensor_tensor(diff[:], tern[:], scale[:, 0:1], w[:], ALU.mult, ALU.subtract))
            nc.vector.tensor_tensor(ste[:], w[:], diff[:], ALU.add).then_inc(ste_done, 1)
            for t in range(TT):
                ins = nc.vector.tensor_tensor(xb[:, t, :], net.x[:, t, :], bias[:], ALU.add)
            done(ins)
            for t in range(TT):
                dve.wait_ge(y_mm, t // 2 + 1)
                nc.vector.tensor_tensor(net.x[:, t, :], ps_y[:, t // 2, (t % 2) * D:(t % 2 + 1) * D], xb[:, t, :], ALU.add)

        @block.tensor
        def _(pe):
            pe.wait_ge(part_done, 1)
            nc.tensor.matmul(ps_s[:, 0:1], net.ones[:], part[:], start=True, stop=True).then_inc(s_mm, 1)
            pe.wait_ge(ste_done, 1)
            for k in range(KT):
                for z in range(KT):
                    last = nc.tensor.transpose(ps_w[:, k * D + z * P:k * D + (z + 1) * P], ste[:, z, k * P:(k + 1) * P], net.ident[:])
            last.then_inc(t_mm, 1)
            pe.wait_ge(t_out, 1)
            for t in range(TT):
                for k in range(KT):
                    last = nc.tensor.matmul(ps_y[:, t // 2, (t % 2) * D:(t % 2 + 1) * D], net.hT[:, k, t * P:(t + 1) * P],
                                            wT[:, k, :], start=(k == 0), stop=(k == KT - 1))
                if t % 2 or t == TT - 1:
                    last.then_inc(y_mm, 1)

        @block.scalar
        def _(act):
            act.wait_ge(t_mm, 1)
            nc.scalar.activation(wT[:].rearrange("p k d -> p (k d)"), ps_w[:], ACT.Copy).then_inc(t_out, 1)


def experts_2(net):
    def load(part, m, u, bufs):
        moves = [(bufs["w1"][:, u].rearrange("p k c -> p (k c)"), net.inp["L2_ffn_W1"].rearrange("(m p) d -> m p d", p=P)[m])]
        moves.append((bufs["w2"][:, u], net.inp["L2_ffn_W2"].rearrange("(z p) (m f) -> m p z f", p=P, f=P)[m]))
        rows = net.gates[0:E2].rearrange("(m e) n -> m e n", e=2)[m]
        return moves, [(bufs["gate"][e * F2:(e + 1) * F2, u, :], rows[e].partition_broadcast(F2)) for e in (0, 1)]

    def router(early, stored):
        route(net, "L2", E2, TOP2, "L2_ffn_Wr", "L2_ffn_br", True, early, stored)

    run_experts(net, "L2", (E2 * F2 // P,), load, False, ACT.Gelu, router, 32, 4, turn=True)


def route_3(net, early, stored):
    nc = net.nc
    with nc.cleanup_on_exit(), ExitStack() as ctx:
        sb, ps, sem = phase_tools(net, ctx, "L3r")
        w, w_raw, logits = sb("w", [P, KT, E3]), sb("w_raw", [E3, D]), sb("logits", [P, TT, E3])
        sums, top = sb("sums", [1, E3]), sb("top", [1, 8])
        own, peak = sb("own", [P, TOP3, TT]), sb("peak", [P, TT])
        gap, e = sb("gap", [P, TOP3, TT]), sb("e", [P, TOP3, TT])
        total, inv, rw = sb("total", [P, TT]), sb("inv", [P, TT]), sb("rw", [P, TOP3, TT])
        w_in, turned, turn_out, l_mm, l_out, s_mm = sem("w_in"), sem("turned"), sem("turn_out"), sem("l_mm"), sem("l_out"), sem("s_mm")
        picked, gap_done, exp_done, rw_done = sem("picked"), sem("gap_done"), sem("exp_done"), sem("rw_done")
        t_mm, t_out, own_in = sem("t_mm"), sem("t_out"), sem("own_in")
        step = sem("step")

        def load(sp):
            sp.dma_start(w_raw[:], net.inp["L3_ffn_gate_w"]).then_inc(w_in, 16)

        add_attention(net, "L3", whole=True, split=True, early=load)
        ps_w, ps_l, ps_s, ps_t = ps("ps_w", [P, 512]), ps("ps_l", [P, 512]), ps("ps_s", [P, 512]), ps("ps_t", [P, 2, 512])
        block = ctx.enter_context(nc.Block())

        @block.sync
        def _(sp):
            sp.wait_ge(picked, 1)
            for k in range(TOP3):
                sel = sp.value_load(net.sel[0:1, k:k + 1], min_val=0, max_val=E3 - 1)
                sp.dma_start(net.b2[k:k + 1, :], net.inp["L3_ffn_b2"][bass.ds(sel, 1), :]).then_inc(own_in, 16)
            early(sp)
            sp.wait_ge(t_out, 1)
            sp.dma_start(net.gates[0:TOP3], net.rw[:]).then_inc(stored, 16)
            sp.wait_ge(own_in, 16 * TOP3)

        @block.tensor
        def _(pe):
            pe.wait_ge(w_in, 16)
            for k in range(KT):
                last = nc.tensor.transpose(ps_w[:, k * E3:(k + 1) * E3], w_raw[:, k * P:(k + 1) * P], net.ident[0:E3, 0:E3])
            last.then_inc(turned, 1)
            pe.wait_ge(turn_out, 1)
            for t in range(TT):
                for k in range(KT):
                    last = nc.tensor.matmul(ps_l[:, t * E3:(t + 1) * E3], net.hT[:, k, t * P:(t + 1) * P], w[:, k, :],
                                            start=(k == 0), stop=(k == KT - 1))
            last.then_inc(l_mm, 1)
            pe.wait_ge(l_out, 1)
            nc.tensor.matmul(ps_s[0:1, 0:TT * E3], net.ones[:, 0:1], logits[:].rearrange("p t e -> p (t e)"),
                             start=True, stop=True).then_inc(s_mm, 1)
            pe.wait_ge(rw_done, 1)
            for t in range(TT):
                last = nc.tensor.transpose(ps_t[0:TOP3, t // 4, (t % 4) * P:(t % 4 + 1) * P], rw[:, :, t], net.ident[:])
            last.then_inc(t_mm, 1)

        @block.scalar
        def _(act):
            act.wait_ge(turned, 1)
            nc.scalar.activation(w[:].rearrange("p k e -> p (k e)"), ps_w[:, 0:KT * E3], ACT.Copy).then_inc(turn_out, 1)
            act.wait_ge(gap_done, TOP3)
            nc.scalar.activation(e[:], gap[:], ACT.Exp).then_inc(exp_done, 1)
            act.wait_ge(t_mm, 1)
            nc.scalar.activation(net.rw[:], ps_t[0:TOP3].rearrange("p a k -> p (a k)")[:, 0:NT], ACT.Copy).then_inc(t_out, 1)

        @block.vector
        def _(dve):
            count = [0]

            def done(ins):
                count[0] += 1
                ins.then_inc(step, 1)
                dve.wait_ge(step, count[0])

            dve.wait_ge(l_mm, 1)
            nc.vector.tensor_copy(logits[:].rearrange("p t e -> p (t e)"), ps_l[:, 0:TT * E3]).then_inc(l_out, 1)
            dve.wait_ge(s_mm, 1)
            done(nc.vector.tensor_reduce(sums[:], ps_s[0:1, 0:TT * E3].rearrange("p (t e) -> p e t", e=E3), AX.X, ALU.add))
            done(nc.vector.max(top[:], sums[:]))
            nc.vector.max_index(net.sel[:], top[:], sums[:]).then_inc(picked, 1)
            dve.wait_ge(picked, 1)
            dve.wait_ge(l_out, 1)
            for k in range(TOP3):
                sel = dve.value_load(net.sel[0:1, k:k + 1], min_val=0, max_val=E3 - 1)
                done(nc.vector.tensor_copy(own[:, k, :], logits[:, :, bass.ds(sel, 1)].rearrange("p t e -> p (t e)")))
            done(nc.vector.tensor_tensor(peak[:], own[:, 0, :], own[:, 1, :], ALU.max))
            for k in range(TOP3):
                nc.vector.tensor_tensor(gap[:, k, :], own[:, k, :], peak[:], ALU.subtract).then_inc(gap_done, 1)
            dve.wait_ge(exp_done, 1)
            done(nc.vector.tensor_tensor(total[:], e[:, 0, :], e[:, 1, :], ALU.add))
            done(nc.vector.reciprocal(inv[:], total[:]))
            nc.vector.tensor_tensor(rw[:], e[:], inv[:].unsqueeze(1).to_broadcast([P, TOP3, TT]), ALU.mult).then_inc(rw_done, 1)


def experts_3(net):
    sel = {}

    def before(sp):
        for k in range(TOP3):
            sel[k] = sp.value_load(net.sel[0:1, k:k + 1], min_val=0, max_val=E3 - 1)

    def load(part, tile, u, bufs):
        w1 = net.inp["L3_ffn_w1"].rearrange("e (k p) (m f) -> e m p k f", p=P, f=P)[sel[part], tile]
        w2 = net.inp["L3_ffn_w2"].rearrange("e (m f) d -> e m f d", f=P)[sel[part], tile]
        b1 = net.inp["L3_ffn_b1"].rearrange("e (m f u) -> e m f u", f=P, u=1)[sel[part], tile]
        return ([(bufs["w1"][:, u, 0], w1), (bufs["w2"][:, u], w2), (bufs["b1"][:, u], b1)],
                [(bufs["gate"][:, u, :], net.gates[part].partition_broadcast(P))])

    def first(pe, y_at):
        for t in range(TT):
            net.nc.tensor.matmul(y_at(t), net.rw[:, t * P:(t + 1) * P], net.b2[:], start=False, stop=False, skip_group_check=True)

    def router(early, stored):
        route_3(net, early, stored)

    run_experts(net, "L3", (F3 // P, F3 // P), load, False, ACT.Gelu_apprx_tanh, router, 16, 2, bias1=True, before=before,
                first=first)


HD2, NB2 = D // 16, 8
QB2 = 2 * S


def project_small(net):
    nc = net.nc
    with nc.cleanup_on_exit(), ExitStack() as ctx:
        sb, ps, sem = phase_tools(net, ctx, "L2p")
        wq, wk, wv = sb("wq", [HD2, H, D]), sb("wk", [HD2, H, DC]), sb("wv", [HD2, H, DC])
        wo, woT = sb("wo", [P, KT, D]), sb("woT", [HD2, H, D])
        a_high, a_low = sb("a_high", [P, KT, HP, 2, DC], F32R), sb("a_low", [P, KT, HP, 2, DC], F32R)
        w_in, t_mm, t_out, a_mm, a_out, m_mm, m_out, q_mm, q_out = (
            sem("w_in"), sem("t_mm"), sem("t_out"), sem("a_mm"), sem("a_out"), sem("m_mm"), sem("m_out"), sem("q_mm"), sem("q_out"))
        a_part = sem("a_part")
        kv = net.inp["L2_xattn_Wkv_expand"].rearrange("(v h j) c -> v j h c", v=2, j=HD2)

        def early(sp):
            sp.dma_start(wq[:], net.inp["L2_xattn_Wq"].rearrange("(h j) d -> j h d", j=HD2)).then_inc(w_in, 16)
            sp.dma_start(wk[:], kv[0]).then_inc(w_in, 16)
            sp.dma_start(wv[:], kv[1]).then_inc(w_in, 16)
            sp.dma_start(wo[:], net.inp["L2_xattn_Wout"].rearrange("(z p) d -> p z d", p=P)).then_inc(w_in, 16)

        layer_norm(net, "L2n", early)
        ps_a = ps("ps_a", [P, 4, 512])
        ps_t = ps("ps_t", [P, 4, 512])
        block = ctx.enter_context(nc.Block())

        @block.tensor
        def _(pe):
            pe.wait_ge(w_in, 64)
            for r in range(KT):
                if r:
                    pe.wait_ge(t_out, r)
                for h in range(HP):
                    for z in range(KT):
                        last = nc.tensor.transpose(ps_t[0:HD2, h // 2, (h % 2) * D + z * P:(h % 2) * D + (z + 1) * P],
                                                   wo[:, z, (HP * r + h) * HD2:(HP * r + h + 1) * HD2], net.ident[:])
                last.then_inc(t_mm, 1)
                for h in range(H):
                    last = nc.tensor.matmul(ps_a[:, 2 * r + h // HP, (h % HP) * DC:(h % HP + 1) * DC],
                                            wq[:, h, r * P:(r + 1) * P], wk[:, h, :], start=True, stop=True)
                last.then_inc(a_mm, 1)
            pe.wait_ge(t_out, 2)
            for i in range(HP):
                for h in (i, i + HP):
                    last = nc.tensor.matmul(ps_t[(h // HP) * DC:(h // HP + 1) * DC, i // 2, (i % 2) * D:(i % 2 + 1) * D],
                                            wv[:, h, :], woT[:, h, :], start=True, stop=True)
            last.then_inc(m_mm, 1)
            pe.wait_ge(a_out, 1)
            for i in range(HP):
                for c in (0, 1):
                    n = 2 * i + c
                    if n >= 4:
                        pe.wait_ge(q_out, n - 3)
                    for k in range(KT):
                        for j, (w, h) in enumerate(((a_high, net.h_high), (a_high, net.h_low), (a_low, net.h_high))):
                            last = nc.tensor.matmul(ps_a[:, n % 4, 0:CH], w[:, k, i].rearrange("p a c -> p (a c)"),
                                                    h[:, k, c * CH:(c + 1) * CH], start=(k == 0 and j == 0),
                                                    stop=(k == KT - 1 and j == 2))
                    last.then_inc(q_mm, 1)

        @block.scalar
        def _(act):
            for k in range(KT):
                act.wait_ge(a_mm, k + 1)
                for a in (0, 1):
                    nc.scalar.activation(a_high[:, k, :, a, :], ps_a[:, 2 * k + a, :].rearrange("p (i c) -> p i c", c=DC),
                                         ACT.Copy, scale=0.25).then_inc(a_part, 1)
            act.wait_ge(m_mm, 1)
            nc.scalar.activation(net.m[:], ps_t[:].rearrange("p b (h d) -> p (b h) d", d=D), ACT.Copy).then_inc(m_out, 1)

        @block.vector
        def _(dve):
            for k in range(KT):
                dve.wait_ge(t_mm, k + 1)
                nc.vector.tensor_copy(woT[:, HP * k:HP * k + HP, :], ps_t[0:HD2].rearrange("p b (h d) -> p (b h) d", d=D)).then_inc(t_out, 1)
                for a in (0, 1):
                    dve.wait_ge(a_part, 2 * k + a + 1)
                    last = nc.vector.scalar_tensor_tensor(
                        out=a_low[:, k, :, a, :], in0=ps_a[:, 2 * k + a, :].rearrange("p (i c) -> p i c", c=DC), scalar=0.25,
                        in1=a_high[:, k, :, a, :].bitcast(F32), op0=ALU.mult, op1=ALU.subtract)
            last.then_inc(a_out, 1)
            for i in range(HP):
                for c in (0, 1):
                    n = 2 * i + c
                    dve.wait_ge(q_mm, n + 1)
                    nc.vector.tensor_copy(net.q2[:, c * BC:(c + 1) * BC, i * S:(i + 1) * S],
                                          ps_a[:, n % 4, 0:CH].rearrange("p (b s) -> p b s", s=S)).then_inc(q_out, 1)


def attend_small(net):
    nc = net.nc
    with nc.cleanup_on_exit(), ExitStack() as ctx:
        sb, ps, sem = phase_tools(net, ctx, "L2a")
        NB = 4
        q = sb("q", [P, NB, CH])
        lat = sb("lat", [S, NB, 2, DC])
        latT = sb("latT", [P, 2, S])
        mask = sb("mask", [QB2, S])
        masked, gap = sb("masked", [QB2, 2, NB2, S]), sb("gap", [QB2, 2, NB2, S])
        peak, e = sb("peak", [QB2, 2, NB2]), sb("e", [QB2, 2, NB2, S])
        total, inv, prob = sb("total", [QB2, 2, NB2]), sb("inv", [QB2, 2, NB2]), sb("prob", [QB2, 2, NB2, S])
        probT = sb("probT", [S, 2, NQ])
        ps_l, ps_s = ps("ps_l", [P, 512]), ps("ps_s", [P, 2, 2, 512])
        ps_t, ps_v = ps("ps_t", [P, 2, 512]), ps("ps_v", [P, 512])
        mask_in, loaded = sem("mask_in"), [sem(f"loaded{u}") for u in range(NB)]
        waited, l_mm, l_out = sem("waited"), sem("l_mm"), sem("l_out")
        s_mm = sem("s_mm")
        masked_done = sem("masked_done")
        peak_done, total_done, inv_done = sem("peak_done"), sem("total_done"), sem("inv_done")
        gap_done = sem("gap_done")
        exp_done = sem("exp_done")
        prob_done = sem("prob_done")
        t_mm = sem("t_mm")
        t_out = sem("t_out")
        v_mm = sem("v_mm")
        v_out = sem("v_out")
        block = ctx.enter_context(nc.Block())

        def over_batches(eng, step):
            step(0, 0, 0, True, False)
            step(1, 1, 0, True, False)
            with eng.Fori(0, (B - NB) // NB) as it:
                for u in range(NB):
                    step(NB * it + u + 2, (u + 2) % NB, it + (u + 2) // NB, True, True)
            for b in range(B - NB + 2, B + 2):
                step(b, b % NB, b // NB, b < B, True)

        @block.sync
        def _(sp):
            sp.dma_start(mask[:], net.inp["causal"]).then_inc(mask_in, 16)
            with sp.Fori(0, B // NB) as it:
                for u in range(NB):
                    b = NB * it + u
                    sp.wait_ge(v_mm, b + 1)
                    for a in (0, 1):
                        sp.dma_start(lat[:, u, a, :], net.inp["ctx_512"][b, 0:S, :]).then_inc(loaded[u], 16)
                    sp.dma_start(q[:, u, :], net.q2[:, b, :]).then_inc(loaded[u], 16)

        @block.tensor
        def _(pe):
            def turn_context(b, u, it):
                pe.wait_ge(loaded[u], 48 * it + 48)
                pe.sem_inc(waited, 1)
                nc.tensor.transpose(ps_l[:, 0:S], lat[:, u].rearrange("p a c -> p (a c)"), net.ident[0:S, 0:S]).then_inc(l_mm, 1)

            def step(b, u, it, scores, values):
                v, w = b - 2, (u - 2) % NB
                if values:
                    pe.wait_ge(prob_done, v + 1)
                    pe.wait_ge(t_out, v + 1)
                    pe.sem_inc(waited, 1)
                    for n in range(NB2):
                        a, m = n // 4, n % 4
                        last = nc.tensor.transpose(ps_t[0:S, a, m * QB2:(m + 1) * QB2], prob[:, w % 2, n, :], net.ident[0:QB2, 0:QB2])
                    last.then_inc(t_mm, 1)
                if scores:
                    pe.wait_ge(l_out, b + 1)
                    pe.wait_ge(masked_done, b + 1)
                    for a in (0, 1):
                        for n in range(NB2 // 2):
                            last = nc.tensor.matmul(ps_s[0:QB2, u % 2, a, n * S:(n + 1) * S], q[a * DC:(a + 1) * DC, u, n * QB2:(n + 1) * QB2],
                                                    latT[a * DC:(a + 1) * DC, u % 2, :], start=True, stop=True)
                    last.then_inc(s_mm, 1)
                if values:
                    pe.wait_ge(t_out, v + 2)
                    pe.wait_ge(v_out, v + 1)
                    pe.sem_inc(waited, 1)
                    for a in (0, 1):
                        last = nc.tensor.matmul(ps_v[a * DC:(a + 1) * DC, 0:CH], lat[:, w, 0, :], probT[:, w % 2, a * CH:(a + 1) * CH],
                                                start=True, stop=True)
                    last.then_inc(v_mm, 1)
                if not isinstance(b, int) or b + 1 < B:
                    turn_context(b + 1, (u + 1) % NB, it + (u + 1) // NB)

            pe.sem_inc(v_mm, NB)
            turn_context(0, 0, 0)
            over_batches(pe, step)

        @block.vector
        def _(dve):
            def bc(ap):
                return ap.unsqueeze(2).to_broadcast([QB2, NB2, S])

            def step(b, front, back):
                par = 1 - back if front is None else front
                if back is not None:
                    dve.wait_ge(exp_done, b)
                    nc.vector.tensor_reduce(total[:, back], e[:, back], AX.X, ALU.add).then_inc(total_done, 1)
                if front is not None:
                    dve.wait_ge(s_mm, b + 1)
                    nc.vector.tensor_tensor(masked[:, par].rearrange("p (a n) s -> p a n s", a=2),
                                            ps_s[0:QB2, par, :, 0:NB2 // 2 * S].rearrange("p a (n s) -> p a n s", s=S),
                                            mask[:].unsqueeze(1).unsqueeze(1).to_broadcast([QB2, 2, NB2 // 2, S]),
                                            ALU.add).then_inc(masked_done, 1)
                if back is not None:
                    dve.wait_ge(total_done, b)
                    nc.vector.reciprocal(inv[:, back], total[:, back]).then_inc(inv_done, 1)
                if front is not None:
                    dve.wait_ge(masked_done, b + 3)
                    nc.vector.tensor_reduce(peak[:, par], masked[:, par], AX.X, ALU.max).then_inc(peak_done, 1)
                if back is not None:
                    dve.wait_ge(inv_done, b)
                    nc.vector.tensor_tensor(prob[:, back], e[:, back], bc(inv[:, back]), ALU.mult).then_inc(prob_done, 1)
                if front is not None:
                    dve.wait_ge(peak_done, b + 1)
                    nc.vector.tensor_tensor(gap[:, par], masked[:, par], bc(peak[:, par]), ALU.subtract).then_inc(gap_done, 1)

            dve.sem_inc(masked_done, 2)
            dve.wait_ge(mask_in, 16)
            step(0, 0, None)
            with dve.Fori(0, (B - 2) // 2) as it:
                step(2 * it + 1, 1, 0)
                step(2 * it + 2, 0, 1)
            step(B - 1, 1, 0)
            step(B, None, 1)

        @block.scalar
        def _(act):
            def turn_context(b, u):
                act.wait_ge(l_mm, b + 1)
                if not isinstance(b, int) or b >= 2:
                    act.wait_ge(s_mm, b - 1)
                nc.scalar.activation(latT[:, u % 2, :], ps_l[:, 0:S], ACT.Copy).then_inc(l_out, 1)

            def step(b, u, it, scores, values):
                v, w = b - 2, (u - 2) % NB
                if values:
                    act.wait_ge(t_mm, v + 1)
                    nc.scalar.activation(probT[:, w % 2].rearrange("p (a q) -> p a q", a=2), ps_t[0:S, :, 0:CH],
                                         ACT.Copy).then_inc(t_out, 1)
                if not isinstance(b, int) or 1 <= b <= B:
                    act.wait_ge(gap_done, b)
                    nc.scalar.activation(e[:, (u - 1) % 2], gap[:, (u - 1) % 2], ACT.Exp).then_inc(exp_done, 1)
                if values:
                    act.wait_ge(v_mm, v + NB + 1)
                    nc.scalar.activation(net.cT[:, :, bass.ds(v * S, S)], ps_v[:, 0:CH].rearrange("p (h s) -> p h s", s=S),
                                         ACT.Copy).then_inc(v_out, 1)
                if not isinstance(b, int) or b + 1 < B:
                    turn_context(b + 1, u + 1)

            act.sem_inc(t_out, 1)
            act.sem_inc(v_out, 1)
            turn_context(0, 0)
            over_batches(act, step)


def store_result(net):
    nc = net.nc
    with nc.cleanup_on_exit(), ExitStack() as ctx:
        _, _, sem = phase_tools(net, ctx, "fin")
        stored = sem("stored")
        block = ctx.enter_context(nc.Block())

        @block.sync
        def _(sp):
            sp.dma_start(net.out.rearrange("b s d -> (b s) d").rearrange("(t p) d -> p t d", p=P), net.x[:]).then_inc(stored, 16)
            sp.wait_ge(stored, 16)


def network(nc, inp, out):
    net = Net()
    net.nc, net.inp, net.out = nc, inp, out
    with ExitStack() as ctx:
        def sb(name, shape, dt=F32):
            return ctx.enter_context(nc.sbuf_tensor("net_" + name, shape, dt))

        net.x = sb("x", [P, TT, D])
        net.hT = sb("hT", [P, KT, NT])
        net.h_high, net.h_low = sb("h_high", [P, KT, NT], F32R), sb("h_low", [P, KT, NT], F32R)
        net.ident, net.ident_r = sb("ident", [P, P]), sb("ident_r", [P, P], F32R)
        net.ones, net.eps = sb("ones", [P, P]), sb("eps", [P, 1])
        net.cT = sb("cT", [P, HP, NT])
        net.m = sb("m", [P, HP, D])
        net.kv_rows = nc.dram_tensor("kv_rows", (B, KP, NK, DC), F32).ap()
        net.kv_high = nc.dram_tensor("kv_high", (B, DC, L), F32).ap()
        net.kv_low = nc.dram_tensor("kv_low", (B, DC, L), F32).ap()
        net.gates = nc.dram_tensor("gates", (E0 + 2, NT), F32).ap()
        load_constants(net)

        def latent_attention(tag, rope):
            with ExitStack() as own:
                net.q = own.enter_context(nc.sbuf_tensor(tag + "_q", [P, B, NQ], F32R))
                project_queries(net, tag, rope, rotate_context=not rope)
                attend(net, tag)

        def small_attention():
            with ExitStack() as own:
                net.q2 = own.enter_context(nc.sbuf_tensor("L2_q2", [P, B, CH], F32))
                project_small(net)
                attend_small(net)

        def chosen_experts():
            with ExitStack() as own:
                net.sel = own.enter_context(nc.sbuf_tensor("L3_sel", [1, 8], U32))
                net.rw = own.enter_context(nc.sbuf_tensor("L3_rw", [TOP3, NT], F32))
                net.b2 = own.enter_context(nc.sbuf_tensor("L3_b2", [TOP3, D], F32))
                experts_3(net)

        latent_attention("L0", False)
        experts_0(net)
        latent_attention("L1", True)
        ternary_layer(net)
        small_attention()
        experts_2(net)
        latent_attention("L3", True)
        chosen_experts()
        store_result(net)


def _tables():
    def angles(n, dim):
        inv = (np.float32(1.0) / np.float32(10000.0) ** (np.arange(0, dim, 2, dtype=np.float32) / np.float32(dim))).astype(np.float32)
        f = np.arange(n, dtype=np.float32)[:, None] * inv[None, :]
        return np.repeat(np.sin(f), 2, axis=-1).astype(np.float32), np.repeat(np.cos(f), 2, axis=-1).astype(np.float32)

    sin, cos = angles(L, DC)
    sin = np.concatenate([-sin[:, :DC // 2], sin[:, DC // 2:]], axis=1)
    qs, qc = angles(S, CQ)
    qs = np.concatenate([-qs[:, :AQ], qs[:, AQ:]], axis=1)
    tab = np.stack([np.tile(t.T, (1, BC)) for t in (qc[:, :AQ], qc[:, AQ:], qs[:, :AQ], qs[:, AQ:])], axis=1)
    return {"kv_cos": cos, "kv_sin": sin, "q_tab": np.ascontiguousarray(tab), "expert_ids": np.arange(E0, dtype=np.float32),
            "causal": np.where(np.arange(S)[None, :] <= np.arange(QB2)[:, None] % S, 0, NEG).astype(np.float32)}


def kernel(**inputs):
    import concourse.bacc as _bacc
    from concourse import mybir as _mybir
    from concourse.bass_utils import run_bass_kernel_spmd as _run

    nc = _bacc.Bacc("TRN2", target_bir_lowering=False, num_devices=1)
    arrays, inp = {}, {}
    for name, a in {**inputs, **_tables()}.items():
        a = np.ascontiguousarray(a)
        arrays[f"in_{name}"] = a
        inp[name] = nc.dram_tensor(f"in_{name}", a.shape, _mybir.dt.from_np(a.dtype), kind="ExternalInput").ap()
    out = nc.dram_tensor("out_x", (B, S, D), F32, kind="ExternalOutput").ap()
    network(nc, inp, out)
    r = _run(nc, [arrays], core_ids=[0])
    return r.results[0]["out_x"]
```
